# Optimizing a Trainium2 kernel written in Bass

```python
import numpy as np
import jax
import jax.numpy as jnp

def _softmax(x, axis=-1):
    return jax.nn.softmax(x, axis=axis)

def _gelu(x):
    return jax.nn.gelu(x, approximate=True)

def _silu(x):
    return jax.nn.silu(x)

def _sigmoid(x):
    return jax.nn.sigmoid(x)

def _layernorm(x, axis=-1, eps=1e-05):
    m = jnp.mean(x, axis=axis, keepdims=True)
    v = jnp.var(x, axis=axis, keepdims=True)
    return (x - m) / jnp.sqrt(v + eps)

def _scatter_add(tgt, idx, src, axis=0):
    return tgt.at[idx].add(src)

def _segment_sum(src, seg, n):
    return jax.ops.segment_sum(src, seg, n)
kernel_name = 'mk_lm_tower_d1_tok_ids256_r4_60bb63'

def setup_inputs(seed: int=0):
    np.random.seed(seed)
    _w = jnp.asarray

    def _rec_inputs():
        import jax
        import jax.numpy as jnp
        _rk = jax.random.key(seed)
        x = jax.random.randint(jax.random.fold_in(_rk, 1), (128, 128), 0, 16, jnp.int32)
        pos_S = jnp.broadcast_to(jnp.arange(128, dtype=jnp.int32), (128,))
        return (x, pos_S)
    x, pos_S = _rec_inputs()

    def _L0_tok_setup():
        import jax, jax.numpy as jnp
        import numpy as np
        import math
        EMB_DIM = 64
        HEADS = 8
        HEAD_DIM = EMB_DIM // HEADS
        N_LAYERS = 6
        GRID_H = 32
        GRID_W = 32
        SEQ = GRID_H * GRID_W
        LN_EPS = 1e-05

        def _layernorm(x, w, b):
            mu = jnp.mean(x, axis=-1, keepdims=True)
            var = jnp.mean(jnp.square(x - mu), axis=-1, keepdims=True)
            return (x - mu) * jax.lax.rsqrt(var + LN_EPS) * w + b

        def _sinusoidal_table(num_pos, dim):
            inv_freq = 1.0 / 10000.0 ** (jnp.arange(0, dim, 2, dtype=jnp.float32) / dim)
            t = jnp.arange(num_pos, dtype=jnp.float32)
            sinusoid = t[:, None] * inv_freq[None, :]
            return jnp.concatenate([jnp.sin(sinusoid), jnp.cos(sinusoid)], axis=-1)

        def _alibi_bias(num_heads, seq_len):
            xs, ys = jnp.meshgrid(jnp.arange(GRID_H), jnp.arange(GRID_W), indexing='ij')
            xf = xs.reshape(-1).astype(jnp.float32)
            yf = ys.reshape(-1).astype(jnp.float32)
            dist = jnp.abs(xf[:, None] - xf[None, :]) + jnp.abs(yf[:, None] - yf[None, :])
            dist = jnp.abs(dist[:seq_len, :seq_len])
            i = jnp.arange(num_heads, dtype=jnp.float32)
            slopes_l = -2.0 ** (-(1.0 + i))
            slopes_r = -2.0 ** (-(0.5 + i))
            alibi_l = slopes_l[:, None, None] * dist[None]
            alibi_r = slopes_r[:, None, None] * dist[None]
            return jnp.triu(alibi_r) + jnp.tril(alibi_l)
        key = jax.random.key(seed)
        ks = jax.random.split(key, 8)
        B, S, D, L = (16, SEQ, EMB_DIM, N_LAYERS)
        H2 = 2 * 128
        return {'tokens': jax.random.randint(ks[0], (B, S), 0, 16), 'pos_ids': jnp.arange(S), 'emb_table': jax.random.normal(ks[1], (16, D), dtype=jnp.float32), 'input_weight': jnp.ones((1,), jnp.float32), 'position_weight': jnp.ones((1,), jnp.float32), 'ln1_w': jnp.ones((L, D), jnp.float32), 'ln1_b': jnp.zeros((L, D), jnp.float32), 'ln2_w': jnp.ones((L, D), jnp.float32), 'ln2_b': jnp.zeros((L, D), jnp.float32), 'w1': jax.random.normal(ks[2], (L, D, H2), dtype=jnp.float32) * (1.0 / np.sqrt(D)), 'b1': jnp.zeros((L, H2), jnp.float32), 'w2': jax.random.normal(ks[3], (L, H2, D), dtype=jnp.float32) * (1.0 / np.sqrt(H2)), 'b2': jnp.zeros((L, D), jnp.float32), 'lnf_w': jnp.ones((D,), jnp.float32), 'lnf_b': jnp.zeros((D,), jnp.float32)}
    _L0_tok_all = _L0_tok_setup()
    _L0_tok_in = {k: v for k, v in _L0_tok_all.items() if k in ('emb_table', 'input_weight', 'position_weight', 'ln1_w', 'ln1_b', 'ln2_w', 'ln2_b', 'w1', 'b1', 'w2', 'b2', 'lnf_w', 'lnf_b')}
    del _L0_tok_all

    def _L0_attn_setup():
        import jax, jax.numpy as jnp
        import numpy as np
        B, T, DIM, H = (2, 512, 64, 4)
        HD = DIM // H
        SCALE = HD ** (-0.5)
        SINKHORN_ITERS = 5

        def _sinkhorn(log_scores, tau):
            la = log_scores / tau
            for _ in range(SINKHORN_ITERS):
                la = la - jax.nn.logsumexp(la, axis=-1, keepdims=True)
                la = la - jax.nn.logsumexp(la, axis=-2, keepdims=True)
            la = la - 0.5 * (jax.nn.logsumexp(la, axis=-1, keepdims=True) + jax.nn.logsumexp(la, axis=-2, keepdims=True))
            return jnp.exp(la)
        key = jax.random.key(seed)
        ks = jax.random.split(key, 8)
        x = jax.random.normal(ks[0], (B, T, DIM), dtype=jnp.float32)
        W_qkv = jax.random.normal(ks[1], (DIM, 3 * DIM), dtype=jnp.float32) * DIM ** (-0.5)
        W_proj = jax.random.normal(ks[2], (DIM, DIM), dtype=jnp.float32) * DIM ** (-0.5)
        b_proj = jnp.zeros((DIM,), dtype=jnp.float32)
        phase = jax.random.normal(ks[3], (H,), dtype=jnp.float32) * 0.1
        ent = jnp.full((H,), 0.3, dtype=jnp.float32)
        gate = jnp.full((H,), 0.5, dtype=jnp.float32)
        tau = jnp.array(1.0, dtype=jnp.float32)
        return {'x': x, 'W_qkv': W_qkv, 'W_proj': W_proj, 'b_proj': b_proj, 'phase': phase, 'ent': ent, 'gate': gate, 'tau': tau}
    _L0_attn_all = _L0_attn_setup()
    _L0_attn_in = {k: v for k, v in _L0_attn_all.items() if k in ('W_qkv', 'W_proj', 'b_proj', 'phase', 'ent', 'gate', 'tau')}
    del _L0_attn_all

    def _L0_ffn_setup():
        import jax, jax.numpy as jnp
        import numpy as np
        TOP_K = 2
        LN_EPS = 1e-05
        key = jax.random.key(seed)
        ks = jax.random.split(key, 8)
        B, S, D, E, H = (16, 256, 64, 8, 256)
        x = jax.random.normal(ks[0], (B, S, D), dtype=jnp.float32)
        Wr = jax.random.normal(ks[1], (D, E), dtype=jnp.float32) * 0.1
        br = jnp.zeros((E,), dtype=jnp.float32)
        ln_g = jnp.ones((E, D), dtype=jnp.float32)
        ln_b = jnp.zeros((E, D), dtype=jnp.float32)
        W1 = jax.random.normal(ks[2], (E, D, H), dtype=jnp.float32) * (1.0 / np.sqrt(D))
        b1 = jnp.zeros((E, H), dtype=jnp.float32)
        W2 = jax.random.normal(ks[3], (E, H, D), dtype=jnp.float32) * (1.0 / np.sqrt(H))
        b2 = jnp.zeros((E, D), dtype=jnp.float32)
        return {'x': x, 'Wr': Wr, 'br': br, 'ln_g': ln_g, 'ln_b': ln_b, 'W1': W1, 'b1': b1, 'W2': W2, 'b2': b2}
    _L0_ffn_all = _L0_ffn_setup()
    _L0_ffn_in = {k: v for k, v in _L0_ffn_all.items() if k in ('Wr', 'br', 'ln_g', 'ln_b', 'W1', 'b1', 'W2', 'b2')}
    del _L0_ffn_all
    return {'x': x, 'pos_S': pos_S, 'L0_tok_emb_table': _L0_tok_in['emb_table'], 'L0_tok_input_weight': _L0_tok_in['input_weight'], 'L0_tok_position_weight': _L0_tok_in['position_weight'], 'L0_tok_ln1_w': _L0_tok_in['ln1_w'], 'L0_tok_ln1_b': _L0_tok_in['ln1_b'], 'L0_tok_ln2_w': _L0_tok_in['ln2_w'], 'L0_tok_ln2_b': _L0_tok_in['ln2_b'], 'L0_tok_w1': _L0_tok_in['w1'], 'L0_tok_b1': _L0_tok_in['b1'], 'L0_tok_w2': _L0_tok_in['w2'], 'L0_tok_b2': _L0_tok_in['b2'], 'L0_tok_lnf_w': _L0_tok_in['lnf_w'], 'L0_tok_lnf_b': _L0_tok_in['lnf_b'], 'L0_attn_W_qkv': _L0_attn_in['W_qkv'], 'L0_attn_W_proj': _L0_attn_in['W_proj'], 'L0_attn_b_proj': _L0_attn_in['b_proj'], 'L0_attn_phase': _L0_attn_in['phase'], 'L0_attn_ent': _L0_attn_in['ent'], 'L0_attn_gate': _L0_attn_in['gate'], 'L0_attn_tau': _L0_attn_in['tau'], 'L0_ffn_Wr': _L0_ffn_in['Wr'], 'L0_ffn_br': _L0_ffn_in['br'], 'L0_ffn_ln_g': _L0_ffn_in['ln_g'], 'L0_ffn_ln_b': _L0_ffn_in['ln_b'], 'L0_ffn_W1': _L0_ffn_in['W1'], 'L0_ffn_b1': _L0_ffn_in['b1'], 'L0_ffn_W2': _L0_ffn_in['W2'], 'L0_ffn_b2': _L0_ffn_in['b2']}

def reference(x, pos_S, L0_tok_emb_table, L0_tok_input_weight, L0_tok_position_weight, L0_tok_ln1_w, L0_tok_ln1_b, L0_tok_ln2_w, L0_tok_ln2_b, L0_tok_w1, L0_tok_b1, L0_tok_w2, L0_tok_b2, L0_tok_lnf_w, L0_tok_lnf_b, L0_attn_W_qkv, L0_attn_W_proj, L0_attn_b_proj, L0_attn_phase, L0_attn_ent, L0_attn_gate, L0_attn_tau, L0_ffn_Wr, L0_ffn_br, L0_ffn_ln_g, L0_ffn_ln_b, L0_ffn_W1, L0_ffn_b1, L0_ffn_W2, L0_ffn_b2):
    import jax
    import jax.numpy as jnp

    def _L0_tok_ref(tokens, pos_ids, emb_table, input_weight, position_weight, ln1_w, ln1_b, ln2_w, ln2_b, w1, b1, w2, b2, lnf_w, lnf_b):
        import jax, jax.numpy as jnp
        import numpy as np
        import math
        EMB_DIM = 64
        HEADS = 8
        HEAD_DIM = EMB_DIM // HEADS
        N_LAYERS = 6
        GRID_H = 32
        GRID_W = 32
        SEQ = GRID_H * GRID_W
        LN_EPS = 1e-05

        def _layernorm(x, w, b):
            mu = jnp.mean(x, axis=-1, keepdims=True)
            var = jnp.mean(jnp.square(x - mu), axis=-1, keepdims=True)
            return (x - mu) * jax.lax.rsqrt(var + LN_EPS) * w + b

        def _sinusoidal_table(num_pos, dim):
            inv_freq = 1.0 / 10000.0 ** (jnp.arange(0, dim, 2, dtype=jnp.float32) / dim)
            t = jnp.arange(num_pos, dtype=jnp.float32)
            sinusoid = t[:, None] * inv_freq[None, :]
            return jnp.concatenate([jnp.sin(sinusoid), jnp.cos(sinusoid)], axis=-1)

        def _alibi_bias(num_heads, seq_len):
            xs, ys = jnp.meshgrid(jnp.arange(GRID_H), jnp.arange(GRID_W), indexing='ij')
            xf = xs.reshape(-1).astype(jnp.float32)
            yf = ys.reshape(-1).astype(jnp.float32)
            dist = jnp.abs(xf[:, None] - xf[None, :]) + jnp.abs(yf[:, None] - yf[None, :])
            dist = jnp.abs(dist[:seq_len, :seq_len])
            i = jnp.arange(num_heads, dtype=jnp.float32)
            slopes_l = -2.0 ** (-(1.0 + i))
            slopes_r = -2.0 ** (-(0.5 + i))
            alibi_l = slopes_l[:, None, None] * dist[None]
            alibi_r = slopes_r[:, None, None] * dist[None]
            return jnp.triu(alibi_r) + jnp.tril(alibi_l)
        B, S = tokens.shape
        x_emb = emb_table[tokens]
        pos_emb = _sinusoidal_table(SEQ, EMB_DIM)[pos_ids][None]
        x = input_weight * x_emb + position_weight * pos_emb
        bias = _alibi_bias(HEADS, S)[None]
        scale = 1.0 / math.sqrt(HEAD_DIM)
        for l in range(N_LAYERS):
            xn = _layernorm(x, ln1_w[l], ln1_b[l])
            qkv = xn.reshape(B, S, HEADS, HEAD_DIM).transpose(0, 2, 1, 3)
            scores = jnp.einsum('bhsd,bhtd->bhst', qkv, qkv) * scale + bias
            attn = jax.nn.softmax(scores, axis=-1)
            out = jnp.einsum('bhst,bhtd->bhsd', attn, qkv)
            out = out.transpose(0, 2, 1, 3).reshape(B, S, EMB_DIM)
            x = x + out
            xn = _layernorm(x, ln2_w[l], ln2_b[l])
            h = jax.nn.gelu(xn @ w1[l] + b1[l], approximate=False)
            x = x + (h @ w2[l] + b2[l])
        return _layernorm(x, lnf_w, lnf_b)

    def _L0_attn_ref(x, W_qkv, W_proj, b_proj, phase, ent, gate, tau):
        import jax, jax.numpy as jnp
        import numpy as np
        B, T, DIM, H = (2, 512, 64, 4)
        HD = DIM // H
        SCALE = HD ** (-0.5)
        SINKHORN_ITERS = 5

        def _sinkhorn(log_scores, tau):
            la = log_scores / tau
            for _ in range(SINKHORN_ITERS):
                la = la - jax.nn.logsumexp(la, axis=-1, keepdims=True)
                la = la - jax.nn.logsumexp(la, axis=-2, keepdims=True)
            la = la - 0.5 * (jax.nn.logsumexp(la, axis=-1, keepdims=True) + jax.nn.logsumexp(la, axis=-2, keepdims=True))
            return jnp.exp(la)
        Bc, Tc, Dc = x.shape
        qkv = (x @ W_qkv).reshape(Bc, Tc, 3, H, HD)
        q = jnp.transpose(qkv[:, :, 0], (0, 2, 1, 3))
        k = jnp.transpose(qkv[:, :, 1], (0, 2, 1, 3))
        v = jnp.transpose(qkv[:, :, 2], (0, 2, 1, 3))
        scores = jnp.einsum('bhid,bhjd->bhij', q, k) * SCALE
        cos = jnp.cos(phase)[None, :, None, None]
        sin = jnp.sin(phase)[None, :, None, None]
        sT = jnp.swapaxes(scores, -2, -1)
        rotated = 0.5 * ((cos + sin) * scores + (cos - sin) * sT)
        entangled = jnp.einsum('bhid,bhjd->bhij', q, q) * ent[None, :, None, None]
        quantum = rotated + 0.1 * entangled
        g = jax.nn.sigmoid(gate)[None, :, None, None]
        mixed = (1.0 - g) * scores + g * quantum
        attn = _sinkhorn(mixed, tau)
        out = jnp.einsum('bhij,bhjd->bhid', attn, v)
        out = jnp.transpose(out, (0, 2, 1, 3)).reshape(Bc, Tc, Dc)
        return out @ W_proj + b_proj

    def _L0_ffn_ref(x, Wr, br, ln_g, ln_b, W1, b1, W2, b2):
        import jax, jax.numpy as jnp
        import numpy as np
        TOP_K = 2
        LN_EPS = 1e-05
        B, S, D = x.shape
        N = B * S
        xt = x.reshape(N, D)
        logits = xt @ Wr + br
        probs = jax.nn.softmax(logits, axis=-1)
        top_p, top_idx = jax.lax.top_k(probs, TOP_K)
        weights = top_p / top_p.sum(axis=-1, keepdims=True)
        mu = xt.mean(axis=-1, keepdims=True)
        var = ((xt - mu) ** 2).mean(axis=-1, keepdims=True)
        xn = (xt - mu) * jax.lax.rsqrt(var + LN_EPS)
        xe = xn[None, :, :] * ln_g[:, None, :] + ln_b[:, None, :]
        h = jax.nn.gelu(jnp.einsum('end,edh->enh', xe, W1) + b1[:, None, :], approximate=False)
        y = jnp.einsum('enh,ehd->end', h, W2) + b2[:, None, :]
        y_tok = jnp.transpose(y, (1, 0, 2))
        sel = jnp.take_along_axis(y_tok, top_idx[:, :, None], axis=1)
        out = (weights[:, :, None] * sel).sum(axis=1)
        return out.reshape(B, S, D)
    h = _L0_tok_ref(x, pos_S, L0_tok_emb_table, L0_tok_input_weight, L0_tok_position_weight, L0_tok_ln1_w, L0_tok_ln1_b, L0_tok_ln2_w, L0_tok_ln2_b, L0_tok_w1, L0_tok_b1, L0_tok_w2, L0_tok_b2, L0_tok_lnf_w, L0_tok_lnf_b)
    h = h + _L0_attn_ref(_layernorm(h, axis=-1), L0_attn_W_qkv, L0_attn_W_proj, L0_attn_b_proj, L0_attn_phase, L0_attn_ent, L0_attn_gate, L0_attn_tau)
    h = h + _L0_ffn_ref(_layernorm(h, axis=-1), L0_ffn_Wr, L0_ffn_br, L0_ffn_ln_g, L0_ffn_ln_b, L0_ffn_W1, L0_ffn_b1, L0_ffn_W2, L0_ffn_b2)
    return h

_drawn_inputs = setup_inputs


def setup_inputs(seed=0):
    import zlib

    import numpy as np

    out = dict(_drawn_inputs(seed))
    spreads = {'L0_tok_ln1_w': (1.0, 0.2),
     'L0_tok_ln1_b': (0.0, 0.1),
     'L0_tok_ln2_w': (1.0, 0.2),
     'L0_tok_ln2_b': (0.0, 0.1),
     'L0_tok_b1': (0.0, 0.1),
     'L0_tok_b2': (0.0, 0.1),
     'L0_tok_lnf_w': (1.0, 0.2),
     'L0_tok_lnf_b': (0.0, 0.1),
     'L0_attn_b_proj': (0.0, 0.1),
     'L0_attn_ent': (0.30000001192092896, 0.6),
     'L0_attn_gate': (0.5, 0.6),
     'L0_ffn_br': (0.0, 0.1),
     'L0_ffn_ln_g': (1.0, 0.2),
     'L0_ffn_ln_b': (0.0, 0.1),
     'L0_ffn_b1': (0.0, 0.1),
     'L0_ffn_b2': (0.0, 0.1)}
    factors = {'L0_attn_phase': 7.33}
    for name, (base, spread) in spreads.items():
        noise = np.random.default_rng([zlib.crc32(name.encode()), seed]).standard_normal(out[name].shape)
        drawn = base * np.exp(spread * noise) if base else spread * noise
        out[name] = jnp.asarray(drawn.astype(out[name].dtype))
    for name, factor in factors.items():
        out[name] = (out[name] * factor).astype(out[name].dtype)
    return out
```

```python
from contextlib import ExitStack

import numpy as np

import concourse.bass as bass
from concourse import mybir
from concourse.alu_op_type import AluOpType as ALU

ACT = mybir.ActivationFunctionType
AX = mybir.AxisListType
F32 = mybir.dt.float32
F16 = mybir.dt.float16
BF16 = mybir.dt.bfloat16
I32 = mybir.dt.int32
ds = bass.ds

P = 128
B, S, D = 128, 128, 64
LAYERS, H = 6, 8
HD = D // H
HID = 256
HALVES = HID // P
VOCAB = 16
POSITIONS = 1024
POS_CHUNKS = POSITIONS // P
GRID_W = 32
GB = 4
NG = B // GB
GC = GB * D
PAIRS = GB * H
NPAIR2 = GB // 2
EB = 8
BANK = 512
SBANKS = 4
QROWS = 32
EPS = 1e-5
SCALE = 1.0 / float(np.sqrt(HD))


def group(t, g):
    return t[:, ds(g * GC, GC)].rearrange("p (b d) -> p b d", d=D)


def bcast(t, n):
    return t.unsqueeze(2).broadcast_to([t.shape[0], t.shape[1], n])


def mid(t, n):
    return t.unsqueeze(1).broadcast_to([t.shape[0], n, t.shape[1]])


def own_wait(e, c):
    e.sem_inc(c.waited, 1)


def embed(nc, c, a):
    with ExitStack() as ctx:
        sb = lambda n, s, d=F32: ctx.enter_context(nc.sbuf_tensor(n, s, d))
        ps = lambda n, s, d=F32: ctx.enter_context(nc.psum_tensor(n, s, d))
        sem = lambda n: ctx.enter_context(nc.semaphore(n))
        steps = B // EB
        tok_i, tok_f = sb("tok_i", [P, S], I32), sb("tok_f", [P, S])
        tok_t = sb("tok_t", [P, B])
        pos_i, pos_f = sb("pos_i", [P, S], I32), sb("pos_f", [P, S])
        iota_v = sb("iota_v", [P, VOCAB])
        iota_p = sb("iota_p", [P, 1])
        onehot = sb("onehot", [P, B * VOCAB])
        pos_hot = sb("pos_hot", [P, POS_CHUNKS, S])
        pos_tab = sb("pos_tab", [P, POS_CHUNKS, D])
        emb = sb("emb", [P, EB * D])
        weights = sb("weights", [P, 2])
        pos_emb = sb("pos_emb", [P, D])
        hot_t = sb("hot_t", [P, 2, S])
        tokt_ps, hot_ps = ps("tokt_ps", [P, B]), ps("hot_ps", [P, 2, BANK])
        pos_ps, x_ps = ps("pos_ps", [P, D]), ps("x_ps", [P, 2, BANK])
        loaded, emb_zero, emb_loaded = sem("e_loaded"), sem("e_emb_zero"), sem("e_emb_loaded")
        cast, tok_turned, tok_copied = sem("e_cast"), sem("e_tok_turned"), sem("e_tok_copied")
        hot, pos_made, pos_done, x_made = sem("e_hot"), sem("e_pos_made"), sem("e_pos_done"), sem("e_x_made")
        turned, copied = sem("e_turned"), sem("e_copied")

        with nc.Block() as block:
            @block.sync
            def _(e):
                for dst, src in (
                    (c.ident, a["c_ident"]), (c.sel_f, a["c_sel"]), (tok_i, a["x"]),
                    (iota_v, a["c_iota_v"]), (iota_p, a["c_iota_p"]), (pos_tab, a["c_pos"]),
                    (c.bias, a["c_bias"]),
                    (pos_i, a["pos_S"].partition_broadcast(P)),
                    (weights[:, 0:1], a["L0_tok_input_weight"].partition_broadcast(P)),
                    (weights[:, 1:2], a["L0_tok_position_weight"].partition_broadcast(P)),
                    (c.ln1_w, a["L0_tok_ln1_w"].rearrange("l d -> (l d)").partition_broadcast(P)),
                    (c.ln1_b, a["L0_tok_ln1_b"].rearrange("l d -> (l d)").partition_broadcast(P)),
                    (c.ln2, a["ln2"]), (c.priority, a["c_priority"]), (c.diag_ones, a["c_diag"]),
                    (c.wr, a["wr"]), (c.br, a["L0_ffn_br"].partition_broadcast(P)),
                    (c.lnf_w, a["L0_tok_lnf_w"].partition_broadcast(P)),
                    (c.lnf_b, a["L0_tok_lnf_b"].partition_broadcast(P)),
                ):
                    e.dma_start(dst[:] if not isinstance(dst, bass.AP) else dst, src).then_inc(loaded, 16)
                e.wait_ge(emb_zero, 1)
                for b in range(EB):
                    e.dma_start(emb[b * VOCAB:(b + 1) * VOCAB, b * D:(b + 1) * D],
                                a["L0_tok_emb_table"]).then_inc(emb_loaded, 16)

            @block.gpsimd
            def _(e):
                e.memset(emb[:], 0.0).then_inc(emb_zero, 1)
                e.memset(c.minus_half[:], -0.5)
                for par in range(2):
                    e.memset(c.v[:, par, :, HD:HD + 1], 1.0)
                    e.memset(c.v[:, par, :, HD + 1:QROWS], 0.0)

            @block.vector
            def _(e):
                e.wait_ge(loaded, 16 * 19)
                e.tensor_copy(tok_f[:], tok_i[:]).then_inc(cast, 1)
                e.tensor_copy(pos_f[:], pos_i[:]).then_inc(cast, 1)
                e.tensor_copy(c.ident16[:], c.ident[:])
                e.tensor_copy(c.sel[:], c.sel_f[:])
                e.tensor_scalar(c.neg_ident[:], c.ident[:], -1.0, None, ALU.mult)
                e.wait_ge(cast, 2)
                for k in range(POS_CHUNKS):
                    e.tensor_scalar(pos_hot[:, k, :], pos_f[:], float(-k * P), iota_p[:, 0:1],
                                    ALU.add, ALU.is_equal).then_inc(hot, 1)
                e.wait_ge(tok_turned, 1)
                e.tensor_copy(tok_t[:], tokt_ps[:]).then_inc(tok_copied, 1)
                e.wait_ge(tok_copied, 1)
                e.tensor_tensor(onehot[:].rearrange("p (b v) -> p b v", v=VOCAB), bcast(tok_t[:], VOCAB),
                                mid(iota_v[:], B), ALU.is_equal).then_inc(hot, 1)
                e.wait_ge(emb_loaded, 16 * EB)
                e.tensor_scalar(emb[:], emb[:], weights[:, 0:1], None, ALU.mult).then_inc(cast, 1)
                e.wait_ge(pos_made, 1)
                e.tensor_scalar(pos_emb[:], pos_ps[:], weights[:, 1:2], None, ALU.mult).then_inc(pos_done, 1)
                e.wait_ge(pos_done, 1)
                for i in range(steps):
                    e.wait_ge(x_made, i + 1)
                    for k in range(EB // GB):
                        e.tensor_tensor(group(c.x, i * EB // GB + k),
                                        x_ps[:, i % 2, k * GC:(k + 1) * GC].rearrange("p (b d) -> p b d", d=D),
                                        mid(pos_emb[:], GB), ALU.add).then_inc(c.x_ready, 1)

            @block.tensor
            def _(e):
                e.wait_ge(loaded, 16 * 19)
                e.wait_ge(cast, 1)
                e.transpose(tokt_ps[:], tok_f[:], c.ident[:]).then_inc(tok_turned, 1)
                e.wait_ge(hot, POS_CHUNKS)
                for k in range(POS_CHUNKS):
                    mm = e.matmul(pos_ps[:], pos_hot[:, k, :], pos_tab[:, k, :],
                                  start=k == 0, stop=k == POS_CHUNKS - 1)
                mm.then_inc(pos_made, 1)
                e.wait_ge(hot, POS_CHUNKS + 1)
                e.wait_ge(cast, 3)
                for i in range(steps + 1):
                    if i < steps:
                        if i >= 2:
                            e.wait_ge(copied, i - 1)
                        e.transpose(hot_ps[:, i % 2, 0:S], onehot[:, i * EB * VOCAB:(i + 1) * EB * VOCAB],
                                    c.ident[:]).then_inc(turned, 1)
                    if i >= 1:
                        e.wait_ge(copied, i)
                        if i >= 3:
                            e.wait_ge(c.x_ready, (i - 2) * EB // GB)
                        e.matmul(x_ps[:, (i - 1) % 2, :], hot_t[:, (i - 1) % 2, :], emb[:],
                                 start=True, stop=True).then_inc(x_made, 1)

            @block.scalar
            def _(e):
                for i in range(steps):
                    e.wait_ge(turned, i + 1)
                    if i >= 2:
                        e.wait_ge(x_made, i - 1)
                    e.activation(hot_t[:, i % 2, :], hot_ps[:, i % 2, 0:S], ACT.Copy).then_inc(copied, 1)


def tower(nc, c, a):
    with ExitStack() as ctx:
        sb = lambda n, s, d=F32: ctx.enter_context(nc.sbuf_tensor(n, s, d))
        ps = lambda n, s, d=F32: ctx.enter_context(nc.psum_tensor(n, s, d))
        sem = lambda n: ctx.enter_context(nc.semaphore(n))

        sum1, mean1, var1, rstd1 = (sb(n, [P, GB]) for n in ("sum1", "mean1", "var1", "rstd1"))
        xc1, sq1, z1, zw1 = (sb(n, [P, GC]) for n in ("xc1", "sq1", "z1", "zw1"))
        q16 = sb("q16", [P, GB, 2, D], F16)
        qt16 = sb("qt16", [P, GB * S], F16)
        left = sb("left", [P, 2, 2, GB * S], F16)
        right = sb("right", [P, 2, 2, GB * S], F16)
        mx = sb("mx", [P, SBANKS, GB], BF16)
        biased = sb("biased", [P, 4, BANK])
        prob = sb("prob", [P, H, BANK])
        out_t = sb("out_t", [P, 2, BANK])
        rden = sb("rden", [P, 2, GB, 4])
        att = sb("att", [P, GC])
        sum2, mean2, var2, rstd2 = (sb(n, [P, GB]) for n in ("sum2", "mean2", "var2", "rstd2"))
        xc2, sq2, z2 = (sb(n, [P, GC]) for n in ("xc2", "sq2", "z2"))
        zt = c.zt
        wcur = sb("wcur", [P, 2 * HID + HALVES * D + HALVES + 1])
        W1 = lambda par, half: wcur[:, par * HID + half * P:par * HID + (half + 1) * P]
        W2 = lambda half: wcur[:, 2 * HID + half * D:2 * HID + (half + 1) * D]
        B1 = lambda half: wcur[:, 2 * HID + HALVES * D + half:2 * HID + HALVES * D + half + 1]
        B2 = wcur[:, 2 * HID + HALVES * D + HALVES:]
        hid = sb("hid", [P, 2, HALVES, BANK])
        y_t = sb("y_t", [P, 2, NPAIR2 * S])

        pool = [ps(f"bank{i}", [P, BANK]) for i in range(8)]
        score_ps = pool[0:SBANKS]
        turn_ps, stack_ps, out_ps, back_ps = pool[SBANKS:]
        q_turn_ps = turn_ps[:, 0:GB * S // 2].bitcast(F16)
        h_ps = lambda par, half: pool[2 * par + half]
        y_ps = lambda par: pool[4 + par]
        yb_ps = lambda par: pool[6 + par]

        names = ("sqsum1", "sqsum2", "sum1", "mean1", "xc1", "sq1", "var1", "rstd1", "z1", "zw1", "q", "hi", "lo", "q_turned",
                 "q_copied", "stacked", "stack_copied", "scored", "maxed", "shifted", "biased", "exped",
                 "weighed", "out_copied", "back", "recip", "divided", "x_att", "sum2", "mean2", "xc2", "sq2",
                 "var2", "rstd2", "z2", "z2_turned", "zt_copied", "w_loaded", "h_made", "gelued", "y_made",
                 "y_copied", "y_back")
        s = type("Sems", (), {n: sem("t_" + n) for n in names})

        def over_groups(e, step):
            step(-1, 1, "p")
            step(0, 0, "pa")
            with e.Fori(0, (NG - 2) // 2) as j:
                step(j * 2 + 1, 1, "paf")
                step(j * 2 + 2, 0, "paf")
            step(NG - 1, 1, "af")
            step(NG, 0, "f")

        def over_mlp_groups(e, step):
            step(0, 0, "a")
            step(1, 1, "ab")
            with e.Fori(0, (NG - 2) // 2) as j:
                step(j * 2 + 2, 0, "abc")
                step(j * 2 + 3, 1, "abc")
            step(NG, 0, "bc")
            step(NG + 1, 1, "c")

        with nc.Block() as block:
            @block.sync
            def _(e):
                with e.Fori(0, LAYERS) as l:
                    e.wait_ge(s.y_copied, l * NG)
                    e.dma_start(wcur[:], a["mlp"][ds(l, 1)].rearrange("l p n -> (l p) n")).then_inc(s.w_loaded, 16)

            @block.vector
            def _(e):
                with e.Fori(0, LAYERS) as l:
                    def step(i, par, what):
                        n, k, m = l * NG + i, l * NG + i + 1, l * NG + i - 1

                        def scores(h0, h1):
                            for h in range(h0, h1):
                                e.wait_ge(s.scored, n * H + h + 1)
                                e.tensor_reduce(mx[:, h % SBANKS, :],
                                                score_ps[h % SBANKS][:].rearrange("p (b t) -> p b t", t=S),
                                                AX.X, ALU.max).then_inc(s.maxed, 1)
                                if h > h0:
                                    add(h - 1)
                            add(h1 - 1)

                        def add(h):
                            e.wait_ge(s.shifted, n * H + h + 1)
                            e.wait_ge(s.exped, n * H + h - 3) if not isinstance(i, int) or i > 0 or h > 3 else \
                                (e.wait_ge(s.exped, l * (NG * H) + h - 3) if h >= 3 else
                                 e.wait_ge(s.exped, l * (NG * H)))
                            e.tensor_tensor(biased[:, h % 4, :].rearrange("p (b t) -> p b t", t=S),
                                            score_ps[h % SBANKS][:].rearrange("p (b t) -> p b t", t=S),
                                            mid(c.bias[:, h, :], GB), ALU.add).then_inc(s.biased, 1)

                        if "p" in what:
                            e.wait_ge(c.x_ready, k + 1)
                            e.wait_ge(s.var1, k)
                            e.tensor_reduce(sum1[:], group(c.x, i + 1), AX.X, ALU.add).then_inc(s.sum1, 1)
                            e.wait_ge(s.sum1, k + 1)
                            e.tensor_scalar(mean1[:], sum1[:], -1.0 / D, None, ALU.mult).then_inc(s.mean1, 1)
                        if "a" in what:
                            scores(0, 2)
                        if "f" in what:
                            for g in range(2):
                                e.wait_ge(s.back, m * 2 + g + 1)
                                back = back_ps[:].rearrange("p (b j r) -> p b j r", b=GB, j=4)
                                e.reciprocal(rden[:, g], back[:, :, :, HD]).then_inc(s.recip, 1)
                                e.wait_ge(s.recip, m * 2 + g + 1)
                                if g == 0:
                                    e.wait_ge(s.x_att, m) if not isinstance(i, int) or i > 1 else \
                                        e.wait_ge(s.x_att, l * NG)
                                e.tensor_tensor(
                                    att[:].rearrange("p (b g j d) -> p b g j d", b=GB, g=2, j=4)[:, :, g],
                                    back[:, :, :, 0:HD],
                                    rden[:, g].unsqueeze(3).broadcast_to([P, GB, 4, HD]),
                                    ALU.mult).then_inc(s.divided, 1)
                                if "a" in what and g == 0:
                                    scores(2, 3)
                            if "a" in what:
                                scores(3, 4)
                            e.wait_ge(s.x_att, m + 1)
                            e.wait_ge(s.var2, m if not isinstance(i, int) or i > 1 else l * NG)
                            e.tensor_reduce(sum2[:], group(c.x, i - 1), AX.X, ALU.add).then_inc(s.sum2, 1)
                            e.wait_ge(s.sum2, m + 1)
                            e.tensor_scalar(mean2[:], sum2[:], -1.0 / D, None, ALU.mult).then_inc(s.mean2, 1)
                        elif "a" in what:
                            scores(2, 4)
                        if "p" in what:
                            e.wait_ge(s.sq1, k + 1)
                            e.tensor_reduce(sum1[:], sq1[:].rearrange("p (b d) -> p b d", d=D), AX.X,
                                            ALU.add).then_inc(s.sqsum1, 1)
                            e.wait_ge(s.sqsum1, k + 1)
                            e.tensor_scalar(var1[:], sum1[:], EPS, None, ALU.add).then_inc(s.var1, 1)
                        if "a" in what:
                            scores(4, 6)
                        if "f" in what:
                            e.wait_ge(s.sq2, m + 1)
                            e.tensor_reduce(sum2[:], sq2[:].rearrange("p (b d) -> p b d", d=D), AX.X,
                                            ALU.add).then_inc(s.sqsum2, 1)
                            e.wait_ge(s.sqsum2, m + 1)
                            e.tensor_scalar(var2[:], sum2[:], EPS, None, ALU.add).then_inc(s.var2, 1)
                        if "a" in what:
                            scores(6, 8)

                    over_groups(e, step)

                    def mlp(i, par, what):
                        if "c" in what:
                            e.wait_ge(s.y_back, l * NG + i - 1)
                            e.tensor_tensor(group(c.x, i - 2), group(c.x, i - 2),
                                            yb_ps(par)[:, 0:GC].rearrange("p (b d) -> p b d", d=D),
                                            ALU.add).then_inc(c.x_ready, 1)

                    over_mlp_groups(e, mlp)

            @block.gpsimd
            def _(e):
                with e.Fori(0, LAYERS) as l:
                    def step(i, par, what):
                        k, m = l * NG + i + 1, l * NG + i - 1
                        if "f" in what:
                            e.wait_ge(s.divided, m * 2 + 2)
                            own_wait(e, c)
                            e.tensor_tensor(group(c.x, i - 1), group(c.x, i - 1),
                                            att[:].rearrange("p (b d) -> p b d", d=D), ALU.add).then_inc(s.x_att, 1)
                        if "p" in what:
                            e.wait_ge(s.mean1, k + 1)
                            own_wait(e, c)
                            e.tensor_tensor(xc1[:].rearrange("p (b d) -> p b d", d=D), group(c.x, i + 1),
                                            bcast(mean1[:], D), ALU.add).then_inc(s.xc1, 1)
                        if "f" in what:
                            e.wait_ge(s.mean2, m + 1)
                            own_wait(e, c)
                            e.tensor_tensor(xc2[:].rearrange("p (b d) -> p b d", d=D), group(c.x, i - 1),
                                            bcast(mean2[:], D), ALU.add).then_inc(s.xc2, 1)
                        if "p" in what:
                            e.wait_ge(s.var1, k + 1)
                            e.tensor_tensor(rstd1[:], var1[:], c.minus_half[:, 0:GB], ALU.pow).then_inc(s.rstd1, 1)
                            e.wait_ge(s.rstd1, k + 1)
                            e.tensor_tensor(z1[:].rearrange("p (b d) -> p b d", d=D),
                                            xc1[:].rearrange("p (b d) -> p b d", d=D),
                                            bcast(rstd1[:], D), ALU.mult).then_inc(s.z1, 1)
                            e.wait_ge(s.z1, k + 1)
                            own_wait(e, c)
                            e.tensor_tensor(zw1[:].rearrange("p (b d) -> p b d", d=D),
                                            z1[:].rearrange("p (b d) -> p b d", d=D),
                                            mid(c.ln1_w[:, ds(l * D, D)], GB), ALU.mult).then_inc(s.zw1, 1)
                            e.wait_ge(s.zw1, k + 1)
                            if isinstance(i, int) and i <= 0:
                                e.wait_ge(s.weighed, l * (NG * 2))
                            else:
                                e.wait_ge(s.weighed, k * 2 - 2)
                            q = c.v[:, 1 - par, :, 0:HD]
                            own_wait(e, c)
                            for b in range(GB):
                                ins = e.tensor_tensor(
                                    q[:, b * H:(b + 1) * H, :],
                                    zw1[:, b * D:(b + 1) * D].rearrange("p (h d) -> p h d", d=HD),
                                    c.ln1_b[:, ds(l * D, D)].rearrange("p (h d) -> p h d", d=HD), ALU.add)
                            ins.then_inc(s.q, 1)
                            e.wait_ge(s.hi, k + 1)
                            for b in range(GB):
                                ins = e.tensor_tensor(
                                    q16[:, b, 1, :].rearrange("p (h d) -> p h d", d=HD), q[:, b * H:(b + 1) * H, :],
                                    q16[:, b, 0, :].rearrange("p (h d) -> p h d", d=HD), ALU.subtract)
                            ins.then_inc(s.lo, 1)
                        if "f" in what:
                            e.wait_ge(s.var2, m + 1)
                            e.tensor_tensor(rstd2[:], var2[:], c.minus_half[:, 0:GB], ALU.pow).then_inc(s.rstd2, 1)
                            e.wait_ge(s.rstd2, m + 1)
                            e.wait_ge(s.z2_turned, l * NG if isinstance(i, int) and i <= 1 else m)
                            e.tensor_tensor(z2[:].rearrange("p (b d) -> p b d", d=D),
                                            xc2[:].rearrange("p (b d) -> p b d", d=D),
                                            bcast(rstd2[:], D), ALU.mult).then_inc(s.z2, 1)

                    over_groups(e, step)

            @block.scalar
            def _(e):
                with e.Fori(0, LAYERS) as l:
                    def step(i, par, what):
                        n, k, m = l * NG + i, l * NG + i + 1, l * NG + i - 1

                        def exps(h0, h1):
                            for h in range(h0, h1):
                                e.wait_ge(s.biased, n * H + h + 1)
                                e.wait_ge(s.weighed, l * (2 * NG) if isinstance(i, int) and i == 0 else
                                          n * 2 - 1 + h // 4)
                                e.activation(prob[:, h, :], biased[:, h % 4, :], ACT.Exp,
                                             scale=SCALE).then_inc(s.exped, 1)

                        def copy_out(idx, g):
                            e.wait_ge(s.weighed, idx * 2 + g + 1)
                            if isinstance(i, int) and i == 0:
                                e.wait_ge(s.back, l * (2 * NG))
                            else:
                                e.wait_ge(s.back, idx * 2 - 1 + g)
                            e.activation(out_t[:, g, :], out_ps[:], ACT.Copy).then_inc(s.out_copied, 1)

                        def copy_stack(t):
                            e.wait_ge(s.stacked, k * 4 + t + 1)
                            dst = (left, right)[t // 2]
                            e.activation(dst[:, 1 - par, t % 2, :], stack_ps[:], ACT.Copy).then_inc(s.stack_copied, 1)

                        if "p" in what:
                            e.wait_ge(s.xc1, k + 1)
                            e.activation(sq1[:], xc1[:], ACT.Square, scale=1.0 / np.sqrt(D)).then_inc(s.sq1, 1)
                        if "a" in what:
                            exps(0, 2)
                        if "f" in what:
                            e.wait_ge(s.xc2, m + 1)
                            e.activation(sq2[:], xc2[:], ACT.Square, scale=1.0 / np.sqrt(D)).then_inc(s.sq2, 1)
                        if "a" in what:
                            exps(2, 4)
                        if "p" in what:
                            e.wait_ge(s.q, k + 1)
                            e.wait_ge(s.q_turned, l * NG if isinstance(i, int) and i == -1 else k)
                            e.activation(q16[:, :, 0, :].rearrange("p b (h d) -> p b h d", d=HD),
                                         c.v[:, 1 - par, :, 0:HD].rearrange("p (b h) d -> p b h d", h=H),
                                         ACT.Copy).then_inc(s.hi, 1)
                        if "a" in what:
                            copy_out(n, 0)
                            exps(4, 6)
                        if "p" in what:
                            e.wait_ge(s.q_turned, k + 1)
                            e.activation(qt16[:], q_turn_ps, ACT.Copy).then_inc(s.q_copied, 1)
                            copy_stack(0)
                            copy_stack(1)
                        if "a" in what:
                            exps(6, 7)
                        if "p" in what:
                            copy_stack(2)
                        if "a" in what:
                            exps(7, 8)
                        if "p" in what:
                            copy_stack(3)
                        if "f" in what:
                            e.wait_ge(s.z2_turned, m + 1)
                            own_wait(e, c)
                            e.activation(zt[:, ds((i - 1) * NPAIR2 * S, NPAIR2 * S)], turn_ps[:, 0:NPAIR2 * S],
                                         ACT.Identity, scale=c.ln2[:, 0, ds(l, 1)],
                                         bias=c.ln2[:, 1, ds(l, 1)]).then_inc(s.zt_copied, 1)
                        if "a" in what:
                            copy_out(n, 1)

                    over_groups(e, step)

                    def mlp(i, par, what):
                        n = l * NG + i
                        if "a" in what:
                            for half in range(HALVES):
                                e.wait_ge(s.h_made, n * 2 + half + 1)
                                e.wait_ge(s.y_made, l * NG if isinstance(i, int) and i < 2 else n - 1)
                                e.activation(hid[:, par, half, :], h_ps(par, half)[:], ACT.Gelu,
                                             bias=B1(half)).then_inc(s.gelued, 1)
                        if "b" in what:
                            e.wait_ge(s.y_made, n)
                            e.wait_ge(s.y_back, l * NG if isinstance(i, int) and i < 3 else n - 2)
                            e.activation(y_t[:, 1 - par, :], y_ps(1 - par)[:, 0:NPAIR2 * S], ACT.Identity,
                                         bias=B2).then_inc(s.y_copied, 1)

                    over_mlp_groups(e, mlp)

            @block.tensor
            def _(e):
                with e.Fori(0, LAYERS) as l:
                    def step(i, par, what):
                        n, k, m = l * NG + i, l * NG + i + 1, l * NG + i - 1

                        def score(h):
                            g, j = h // 4, h % 4
                            if h == 0:
                                e.wait_ge(s.stack_copied, n * 4 + 4)
                            if isinstance(i, int) and i == 0 and h < SBANKS:
                                e.wait_ge(s.biased, l * (NG * H))
                            else:
                                e.wait_ge(s.biased, n * H + h - SBANKS + 1)
                            for b in range(GB):
                                mm = e.matmul(score_ps[h % SBANKS][:, b * S:(b + 1) * S],
                                              left[QROWS * j:QROWS * (j + 1), par, g, b * S:(b + 1) * S],
                                              right[QROWS * j:QROWS * (j + 1), par, g, b * S:(b + 1) * S],
                                              start=b == 0, stop=False, skip_group_check=True)
                            mm.then_inc(s.scored, 1)

                        def shift(h):
                            e.wait_ge(s.maxed, n * H + h + 1)
                            for b in range(GB):
                                mm = e.matmul(score_ps[h % SBANKS][:, b * S:(b + 1) * S],
                                              mx[:, h % SBANKS, b:b + 1].broadcast_to([P, S]), c.neg_ident[:],
                                              start=False, stop=True, skip_group_check=True)
                            mm.then_inc(s.shifted, 1)

                        def weigh(g):
                            e.wait_ge(s.exped, n * H + 4 * g + 4)
                            e.wait_ge(s.out_copied, n * 2 + g)
                            for b in range(GB):
                                for j in range(4):
                                    h = 4 * g + j
                                    mm = e.matmul(out_ps[QROWS * j:QROWS * (j + 1), b * S:(b + 1) * S],
                                                  c.v[:, par, b * H + h, :], prob[:, h, b * S:(b + 1) * S],
                                                  start=True, stop=True)
                            mm.then_inc(s.weighed, 1)

                        def back(g):
                            e.wait_ge(s.out_copied, m * 2 + g + 1)
                            e.wait_ge(s.divided, m * 2 + g)
                            for b in range(GB):
                                mm = e.transpose(back_ps[:, b * S:(b + 1) * S], out_t[:, g, b * S:(b + 1) * S],
                                                 c.ident[:])
                            mm.then_inc(s.back, 1)

                        def stack(t):
                            if t == 0:
                                e.wait_ge(s.q_copied, k + 1)
                            e.wait_ge(s.stack_copied, k * 4 + t)
                            e.matmul(stack_ps[:], c.sel[:, t, :], qt16[:], start=True, stop=True).then_inc(s.stacked, 1)

                        if "a" in what:
                            score(0)
                            score(1)
                            shift(0)
                            score(2)
                        if "f" in what:
                            back(0)
                        if "a" in what:
                            shift(1)
                            score(3)
                            shift(2)
                        if "f" in what:
                            back(1)
                        if "a" in what:
                            score(4)
                            shift(3)
                            score(5)
                            weigh(0)
                            shift(4)
                        if "p" in what:
                            e.wait_ge(s.lo, k + 1)
                            e.wait_ge(s.zt_copied, l * NG if isinstance(i, int) and i <= 1 else m)
                            for b in range(GB):
                                mm = e.transpose(q_turn_ps[:, b * S:(b + 1) * S],
                                                 q16[:, b].rearrange("p a d -> p (a d)"), c.ident16[:])
                            mm.then_inc(s.q_turned, 1)
                        if "a" in what:
                            score(6)
                            shift(5)
                        if "p" in what:
                            stack(0)
                        if "a" in what:
                            score(7)
                            shift(6)
                        if "p" in what:
                            stack(1)
                        if "a" in what:
                            shift(7)
                        if "p" in what:
                            stack(2)
                        if "f" in what:
                            e.wait_ge(s.z2, m + 1)
                            if "p" in what:
                                e.wait_ge(s.q_copied, k + 1)
                            for q in range(NPAIR2):
                                mm = e.transpose(turn_ps[:, q * S:(q + 1) * S], z2[:, q * 2 * D:(q + 1) * 2 * D],
                                                 c.ident[:])
                            mm.then_inc(s.z2_turned, 1)
                        if "p" in what:
                            stack(3)
                        if "a" in what:
                            weigh(1)

                    over_groups(e, step)

                    def mlp(i, par, what):
                        n = l * NG + i
                        if "a" in what:
                            if isinstance(i, int) and i == 0:
                                e.wait_ge(s.w_loaded, l * 16 + 16)
                                e.wait_ge(s.zt_copied, (l + 1) * NG)
                                e.wait_ge(s.biased, (l + 1) * (NG * H))
                            for half in range(HALVES):
                                e.wait_ge(s.gelued, l * (2 * NG) if isinstance(i, int) and i < 2 else n * 2 - 3 + half)
                                for q in range(2):
                                    mm = e.matmul(h_ps(par, half)[:, q * 2 * S:(q + 1) * 2 * S], W1(q, half),
                                                  zt[:, ds(i * NPAIR2 * S, NPAIR2 * S)], start=True, stop=True)
                                mm.then_inc(s.h_made, 1)
                        if "b" in what:
                            e.wait_ge(s.gelued, n * 2)
                            if isinstance(i, int) and i < 3:
                                e.wait_ge(s.y_copied, l * NG)
                                e.wait_ge(s.out_copied, (l + 1) * (2 * NG))
                            else:
                                e.wait_ge(s.y_copied, n - 2)
                            for half in range(HALVES):
                                for q in range(2):
                                    mm = e.matmul(y_ps(1 - par)[q * D:(q + 1) * D, 0:NPAIR2 * S], W2(half),
                                                  hid[:, 1 - par, half, q * 2 * S:(q + 1) * 2 * S],
                                                  start=half == 0, stop=half == HALVES - 1)
                            mm.then_inc(s.y_made, 1)
                        if "c" in what:
                            e.wait_ge(s.y_copied, n - 1)
                            if isinstance(i, int) and i < 4:
                                e.wait_ge(c.x_ready, (l + 1) * NG)
                                e.wait_ge(s.divided, (l + 1) * (2 * NG))
                            else:
                                e.wait_ge(c.x_ready, n - 3 + NG)
                            for q in range(NPAIR2):
                                mm = e.transpose(yb_ps(par)[:, q * S:(q + 1) * S], y_t[:, par, q * S:(q + 1) * S],
                                                 c.ident[:])
                            mm.then_inc(s.y_back, 1)

                    over_mlp_groups(e, mlp)


NB_CHUNK = 16
CC = NB_CHUNK * D
CHUNKS = B // NB_CHUNK
CP = NB_CHUNK // 2
EXPERTS = 8


def normalise(nc, c, tag, src, affine=None, dst=None, turned=None, logits=None):
    with ExitStack() as ctx:
        sb = lambda n, s, d=F32: ctx.enter_context(nc.sbuf_tensor(tag + n, s, d))
        ps = lambda n, s, d=F32: ctx.enter_context(nc.psum_tensor(tag + n, s, d))
        sem = lambda n: ctx.enter_context(nc.semaphore(tag + n))
        chunk = lambda t, k: t[:, ds(k * CC, CC)].rearrange("p (b d) -> p b d", d=D)
        split = lambda t: t.rearrange("p (b d) -> p b d", d=D)
        total, mean, sqtotal, var, rstd = (sb(n, [P, 2, NB_CHUNK]) for n in ("total", "mean", "sqtotal", "var", "rstd"))
        xc, sq, z = (sb(n, [P, 2, CC]) for n in ("xc", "sq", "z"))
        stage = sb("stage", [P, 2, CC]) if logits else None
        turn_ps = ps("turn", [P, 4, BANK])
        logit_ps = ps("logit", [P, 2, BANK]) if logits else None
        names = ["s_total", "s_mean", "s_xc", "s_sq", "s_sqtotal", "s_var", "s_rstd", "s_z"]
        names += ["s_zw"] if affine else []
        names += ["s_out"] if dst is not None else []
        names += ["s_turned", "s_staged"] if turned is not None or logits else []
        names += ["s_logits", "s_added"] if logits else []
        s = type("Sems", (), {n: sem(n) for n in names})
        done = s.s_out if dst is not None else s.s_z

        def over_chunks(e, step):
            with e.Fori(0, CHUNKS // 2) as j:
                step(j * 2, 0)
                step(j * 2 + 1, 1)

        with nc.Block() as block:
            @block.vector
            def _(e):
                def first(k, par):
                    e.tensor_reduce(total[:, par], chunk(src, k), AX.X, ALU.add).then_inc(s.s_total, 1)
                    e.wait_ge(s.s_total, k + 1)
                    e.tensor_scalar(mean[:, par], total[:, par], -1.0 / D, None, ALU.mult).then_inc(s.s_mean, 1)
                    e.wait_ge(s.s_mean, k + 1)
                    e.tensor_tensor(split(xc[:, par]), chunk(src, k), bcast(mean[:, par], D), ALU.add).then_inc(s.s_xc, 1)

                def second(k, par):
                    e.wait_ge(s.s_sq, k + 1)
                    e.tensor_reduce(sqtotal[:, par], split(sq[:, par]), AX.X, ALU.add).then_inc(s.s_sqtotal, 1)
                    e.wait_ge(s.s_sqtotal, k + 1)
                    e.tensor_scalar(var[:, par], sqtotal[:, par], EPS, None, ALU.add).then_inc(s.s_var, 1)

                def third(k, par):
                    e.wait_ge(s.s_z, k + 1)
                    if affine:
                        e.tensor_tensor(split(z[:, par]), split(z[:, par]), mid(affine[0][:], NB_CHUNK),
                                        ALU.mult).then_inc(s.s_zw, 1)
                        e.wait_ge(s.s_zw, k + 1)
                        e.tensor_tensor(chunk(dst, k), split(z[:, par]), mid(affine[1][:], NB_CHUNK),
                                        ALU.add).then_inc(s.s_out, 1)
                    elif dst is not None:
                        e.tensor_copy(chunk(dst, k), split(z[:, par])).then_inc(s.s_out, 1)

                def both(j):
                    first(j * 2, 0)
                    first(j * 2 + 1, 1)
                    second(j * 2, 0)
                    second(j * 2 + 1, 1)
                    third(j * 2, 0)
                    third(j * 2 + 1, 1)
                    for k, par in ((j * 2, 0), (j * 2 + 1, 1)):
                        if logits:
                            w, bias, out = logits
                            e.wait_ge(s.s_logits, k + 1)
                            e.tensor_tensor(out[:, ds(k * NB_CHUNK * EXPERTS, NB_CHUNK * EXPERTS)].rearrange(
                                "p (b e) -> p b e", e=EXPERTS),
                                logit_ps[:, par, 0:NB_CHUNK * EXPERTS].rearrange("p (b e) -> p b e", e=EXPERTS),
                                mid(bias[:], NB_CHUNK), ALU.add).then_inc(s.s_added, 1)
                    e.wait_ge(done, j * 2 + 2)

                with e.Fori(0, CHUNKS // 2) as j:
                    both(j)

            @block.gpsimd
            def _(e):
                def step(k, par):
                    e.wait_ge(s.s_var, k + 1)
                    e.tensor_tensor(rstd[:, par], var[:, par], c.minus_half[:], ALU.pow).then_inc(s.s_rstd, 1)
                    e.wait_ge(s.s_rstd, k + 1)
                    if turned is not None or logits:
                        e.wait_ge(s.s_turned, k * 1 if isinstance(k, int) else k - par)
                    if affine or dst is not None:
                        e.wait_ge(s.s_out, k - par)
                    e.tensor_tensor(split(z[:, par]), split(xc[:, par]), bcast(rstd[:, par], D),
                                    ALU.mult).then_inc(s.s_z, 1)

                over_chunks(e, step)

            @block.scalar
            def _(e):
                def step(k, par):
                    e.wait_ge(s.s_xc, k + 1)
                    e.activation(sq[:, par], xc[:, par], ACT.Square, scale=1.0 / np.sqrt(D)).then_inc(s.s_sq, 1)

                def copy(k, par):
                    if turned is not None:
                        e.wait_ge(s.s_turned, k + 1)
                        own_wait(e, c)
                        e.activation(turned[:, ds(k * CC, CC)],
                                     turn_ps[:, 2 * par:2 * par + 2, :].rearrange("p a b -> p (a b)"),
                                     ACT.Copy).then_inc(s.s_staged, 1)
                    elif logits:
                        e.wait_ge(s.s_turned, k + 1)
                        e.wait_ge(s.s_logits, k - par)
                        e.activation(stage[:, par], turn_ps[:, 2 * par:2 * par + 2, :].rearrange("p a b -> p (a b)"),
                                     ACT.Copy).then_inc(s.s_staged, 1)

                with e.Fori(0, CHUNKS // 2) as j:
                    step(j * 2, 0)
                    step(j * 2 + 1, 1)
                    copy(j * 2, 0)
                    copy(j * 2 + 1, 1)

            @block.tensor
            def _(e):
                if turned is None and not logits:
                    return

                def step(k, par):
                    e.wait_ge(s.s_z, k + 1)
                    e.wait_ge(s.s_staged, k - par)
                    for q in range(CP):
                        mm = e.transpose(turn_ps[:, 2 * par + q // 4, (q % 4) * P:(q % 4 + 1) * P],
                                         z[:, par, q * P:(q + 1) * P], c.ident[:])
                    mm.then_inc(s.s_turned, 1)

                def product(k, par):
                    e.wait_ge(s.s_staged, k + 1)
                    e.wait_ge(s.s_added, k - par)
                    for q in range(CP):
                        mm = e.matmul(logit_ps[:, par, q * 2 * EXPERTS:(q + 1) * 2 * EXPERTS],
                                      stage[:, par, q * P:(q + 1) * P], logits[0][:], start=True, stop=True)
                    mm.then_inc(s.s_logits, 1)

                with e.Fori(0, CHUNKS // 2) as j:
                    step(j * 2, 0)
                    step(j * 2 + 1, 1)
                    if logits:
                        product(j * 2, 0)
                        product(j * 2 + 1, 1)


AH, AHD = 4, 16
SB = 8
SETS = B // SB
SPAIRS = SB * AH
ITERATIONS = 5


def sinkhorn(nc, c, a):
    with ExitStack() as ctx:
        sb = lambda n, s, d=F32: ctx.enter_context(nc.sbuf_tensor("a_" + n, s, d))
        ps = lambda n, s, d=F32: ctx.enter_context(nc.psum_tensor("a_" + n, s, d))
        sem = lambda n: ctx.enter_context(nc.semaphore("a_" + n))
        w = sb("w", [P, 3 * D])
        head = sb("head", [P, 4, AH])
        cosv, sinv, gate, part, t1, t2, t3 = (sb(n, [P, AH]) for n in ("cos", "sin", "gate", "part", "t1", "t2", "t3"))
        a1, a2, a3 = (sb(n, [P, AH]) for n in ("a1", "a2", "a3"))
        half_pi = sb("half_pi", [P, 1])
        mixk = sb("mixk", [P, D])
        mixq = sb("mixq", [P, D])
        wu, wm = (sb(n, [P, 2, P]) for n in ("wu", "wm"))
        wv = sb("wv", [P, 2, D])
        wproj = sb("wproj", [P, 2, D])
        bproj = sb("bproj", [P, D])
        zset = sb("zset", [P, SB // 2 * S])
        ut, mt = (sb(n, [P, 2, SB // 2 * S]) for n in ("ut", "mt"))
        val = sb("val", [P, SB, AH, AHD])
        valb = sb("valb", [P, SB, AH, QROWS])
        rmax, cmax = (sb(n, [P, 2, 4], BF16) for n in ("rmax", "cmax"))
        k_ij = sb("k_ij", [P, AH, SB, S])
        k_ji = sb("k_ji", [P, AH, SB, S])
        ub, vb = (sb(n, [P, AH, SB, QROWS]) for n in ("ub", "vb"))
        rows = sb("rows", [P, S])
        kv, ku, u, v, prod, inv, alpha, beta = (sb(n, [P, AH, SB]) for n in
                                                ("kv", "ku", "u", "v", "prod", "inv", "alpha", "beta"))
        minus_half = sb("mh", [P, AH, SB])
        out_t = sb("out_t", [P, SB * S])
        att = sb("att", [P, SB, D])
        att_t = sb("att_t", [P, SB // 2 * S])
        res = sb("res", [P, SB, D])
        bank = [ps(f"bank{i}", [P, BANK]) for i in range(8)]
        names = ("loaded", "const", "coef", "mixed", "trig", "sig", "wready", "zset", "ut_ps", "ut", "val_ps", "val",
                 "scored", "rmaxed", "rowed", "cmaxed", "coled", "exped", "summed", "rows", "turned", "factor",
                 "pool", "valb", "out_ps", "out_t", "back", "att", "att_ps", "att_t", "proj", "res", "x",
                 "fin_u", "fin_v")
        s = type("Sems", (), {n: sem("a_" + n) for n in names})
        def diag(t):
            return t[:].rearrange("p h b r -> p h (b r)")[:, :, 0:(SB - 1) * (QROWS + 1) + 1:QROWS + 1]
        heads3 = lambda t: t[:].rearrange("p (h d) -> p h d", d=AHD)

        with nc.Block() as block:
            @block.sync
            def _(e):
                loads = [(w[0:D, :], a["L0_attn_W_qkv"]), (w[D:P, :], a["L0_attn_W_qkv"]),
                         (wproj[0:D, 0, :], a["L0_attn_W_proj"]), (wproj[D:P, 1, :], a["L0_attn_W_proj"]),
                         (bproj[:], a["L0_attn_b_proj"].partition_broadcast(P))]
                for n, name in enumerate(("phase", "ent", "gate")):
                    loads.append((head[:, n, :], a["L0_attn_" + name].partition_broadcast(P)))
                for h in range(AH):
                    loads.append((head[:, 3, h:h + 1], a["L0_attn_tau"].partition_broadcast(P)))
                e.wait_ge(s.const, 3)
                for dst, src in loads:
                    e.dma_start(dst, src).then_inc(s.loaded, 16)

            @block.gpsimd
            def _(e):
                e.memset(wproj[:], 0.0).then_inc(s.const, 1)
                e.memset(half_pi[:], float(np.pi / 2)).then_inc(s.const, 1)
                e.memset(minus_half[:], -0.5).then_inc(s.const, 1)
                for t in (wu, wm, wv):
                    e.memset(t[:], 0.0)
                e.memset(valb[:], 0.0)
                for t in (ub, vb):
                    ins = e.memset(t[:], 0.0)
                ins.then_inc(s.const, 1)
                with e.Fori(0, SETS) as k:
                    for n, (f, other) in enumerate(((u, kv), (v, ku))):
                        e.wait_ge(s.fin_u, k + 1)
                        e.tensor_tensor(prod[:], f[:], other[:], ALU.mult).then_inc(s.pool, 1)
                        e.wait_ge(s.pool, k * 6 + n * 3 + 1)
                        e.tensor_tensor(inv[:], prod[:], minus_half[:], ALU.pow).then_inc(s.pool, 1)
                        e.wait_ge(s.pool, k * 6 + n * 3 + 2)
                        e.tensor_tensor((alpha, beta)[n][:], f[:], inv[:], ALU.mult).then_inc(s.pool, 1)
                        e.wait_ge(s.pool, k * 6 + n * 3 + 3)
                    e.wait_ge(s.out_ps, k)
                    e.wait_ge(s.val, k * 2 + 2)
                    for h in range(AH):
                        ins = e.tensor_tensor(valb[:, :, h, 0:AHD], val[:, :, h, :], bcast(beta[:, h, :], AHD),
                                              ALU.mult)
                    ins.then_inc(s.valb, 1)
                    e.wait_ge(s.res, k + 1)
                    own_wait(e, c)
                    xs = c.x[:, ds(k * (SB * D), SB * D)].rearrange("p (b d) -> p b d", d=D)
                    e.tensor_tensor(xs, xs, res[:], ALU.add).then_inc(s.x, 1)

            @block.scalar
            def _(e):
                e.wait_ge(s.loaded, 16 * 12)
                e.wait_ge(s.coef, 1)
                e.activation(cosv[:], t2[:], ACT.Sin).then_inc(s.trig, 1)
                e.activation(sinv[:], t1[:], ACT.Sin).then_inc(s.trig, 1)
                e.activation(gate[:], head[:, 2, :], ACT.Sigmoid).then_inc(s.sig, 1)
                with e.Fori(0, SETS) as k:
                    e.wait_ge(s.val_ps, k)
                    own_wait(e, c)
                    e.activation(zset[:], c.zt[:, ds(k * (SB // 2 * S), SB // 2 * S)], ACT.Copy).then_inc(s.zset, 1)
                    for n, t in enumerate((ut, mt)):
                        for par in range(2):
                            e.wait_ge(s.ut_ps, k * 4 + 2 * n + par + 1)
                            e.activation(t[:, par], bank[2 * n + par][:], ACT.Copy).then_inc(s.ut, 1)
                    e.wait_ge(s.val_ps, k + 1)
                    e.wait_ge(s.valb, k)
                    for n in range(2):
                        e.activation(val[:].rearrange("p b h d -> p (b h d)")[:, n * 2 * P:(n + 1) * 2 * P],
                                     bank[4][:, n * 2 * P:(n + 1) * 2 * P], ACT.Copy).then_inc(s.val, 1)
                    for n in range(2 * AH):
                        h, half = n // 2, n % 2
                        e.wait_ge(s.coled, k * (2 * AH) + n + 1)
                        dst = lambda t: t[:, h, 4 * half:4 * half + 4, :].rearrange("p b t -> p (b t)")
                        e.activation(dst(k_ij), bank[n % 3][:], ACT.Exp).then_inc(s.exped, 1)
                        e.activation(dst(k_ji), bank[3 + n % 3][:], ACT.Exp).then_inc(s.exped, 1)
                    for n in range(2 * ITERATIONS + 1):
                        e.wait_ge(s.summed, k * (2 * ITERATIONS + 1) + n + 1)
                        e.activation(rows[:], bank[6][:, 0:S], ACT.Copy).then_inc(s.rows, 1)
                    e.wait_ge(s.out_ps, k + 1)
                    for n in range(2):
                        e.activation(out_t[:, n * BANK:(n + 1) * BANK], bank[n][:], ACT.Copy).then_inc(s.out_t, 1)
                    e.wait_ge(s.att_ps, k + 1)
                    e.activation(att_t[:], bank[4][:], ACT.Copy).then_inc(s.att_t, 1)

            @block.vector
            def _(e):
                n = [0]

                def chain(ins):
                    n[0] += 1
                    ins.then_inc(s.mixed, 1)
                    e.wait_ge(s.mixed, n[0])

                e.wait_ge(s.loaded, 16 * 12)
                two_pi = float(2 * np.pi)
                chain(e.tensor_scalar(t3[:], head[:, 0, :], 1.0 / two_pi, 12582912.0, ALU.mult, ALU.add))
                chain(e.tensor_scalar(t3[:], t3[:], -12582912.0, None, ALU.add))
                chain(e.tensor_scalar(t1[:], t3[:], -6.28125, None, ALU.mult))
                chain(e.tensor_tensor(t1[:], t1[:], head[:, 0, :], ALU.add))
                chain(e.tensor_scalar(t3[:], t3[:], -(two_pi - 6.28125), None, ALU.mult))
                chain(e.tensor_tensor(t1[:], t1[:], t3[:], ALU.add))
                chain(e.tensor_scalar(t1[:], t1[:], float(np.float32(3.1415925)), float(-np.float32(3.1415925)),
                                      ALU.min, ALU.max))
                chain(e.tensor_scalar(t2[:], t1[:], -1.0, None, ALU.mult))
                chain(e.tensor_tensor(t2[:], t2[:], t1[:], ALU.max))
                e.tensor_scalar(t2[:], t2[:], -1.0, float(np.pi / 2), ALU.mult, ALU.add).then_inc(s.coef, 1)
                e.wait_ge(s.trig, 2)
                e.wait_ge(s.sig, 1)
                scale = float(AHD) ** -0.5
                chain(e.tensor_tensor(t1[:], cosv[:], sinv[:], ALU.add))
                chain(e.tensor_scalar(t1[:], t1[:], 0.5, None, ALU.mult))
                chain(e.tensor_tensor(t1[:], t1[:], gate[:], ALU.mult))
                chain(e.tensor_scalar(t2[:], gate[:], -1.0, 1.0, ALU.mult, ALU.add))
                chain(e.tensor_tensor(t1[:], t1[:], t2[:], ALU.add))
                chain(e.reciprocal(t3[:], head[:, 3, :]))
                chain(e.tensor_scalar(t1[:], t1[:], scale, None, ALU.mult))
                chain(e.tensor_tensor(a1[:], t1[:], t3[:], ALU.mult))
                chain(e.tensor_tensor(t1[:], cosv[:], sinv[:], ALU.subtract))
                chain(e.tensor_tensor(t1[:], t1[:], gate[:], ALU.mult))
                chain(e.tensor_scalar(t1[:], t1[:], 0.5 * scale, None, ALU.mult))
                chain(e.tensor_tensor(a2[:], t1[:], t3[:], ALU.mult))
                chain(e.tensor_tensor(t1[:], gate[:], head[:, 1, :], ALU.mult))
                chain(e.tensor_scalar(t1[:], t1[:], 0.1, None, ALU.mult))
                chain(e.tensor_tensor(a3[:], t1[:], t3[:], ALU.mult))
                wq, wk = w[:, 0:D].rearrange("p (h d) -> p h d", d=AHD), w[:, D:2 * D].rearrange("p (h d) -> p h d", d=AHD)
                chain(e.tensor_tensor(heads3(mixk), wk, bcast(a1[:], AHD), ALU.mult))
                chain(e.tensor_tensor(heads3(mixq), wq, bcast(a3[:], AHD), ALU.mult))
                chain(e.tensor_tensor(mixk[:], mixk[:], mixq[:], ALU.add))
                chain(e.tensor_tensor(heads3(mixq), wq, bcast(a2[:], AHD), ALU.mult))
                e.wait_ge(s.const, 4)
                for par in range(2):
                    rws = slice(par * D, (par + 1) * D)
                    for t, lo, hi in ((wu, wq[rws], wk[rws]), (wm, heads3(mixk)[rws], heads3(mixq)[rws])):
                        o = t[rws, par, :].rearrange("p (h two d) -> p h two d", two=2, d=AHD)
                        e.tensor_copy(o[:, :, 0, :], lo)
                        e.tensor_copy(o[:, :, 1, :], hi)
                    ins = e.tensor_copy(wv[rws, par, :], w[rws, 2 * D:3 * D])
                ins.then_inc(s.wready, 1)

                with e.Fori(0, SETS) as k:
                    def row_max(n):
                        e.wait_ge(s.scored, k * (2 * AH) + n + 1)
                        e.tensor_reduce(rmax[:, n % 2], bank[n % 3][:].rearrange("p (b t) -> p b t", t=S), AX.X,
                                        ALU.max).then_inc(s.rmaxed, 1)

                    def col_max(n):
                        e.wait_ge(s.rowed, k * (2 * AH) + n + 1)
                        if n >= 2:
                            e.wait_ge(s.coled, k * (2 * AH) + n - 1)
                        e.tensor_reduce(cmax[:, n % 2], bank[3 + n % 3][:].rearrange("p (b t) -> p b t", t=S), AX.X,
                                        ALU.max).then_inc(s.cmaxed, 1)

                    for n in range(2 * AH + 1):
                        if n < 2 * AH:
                            row_max(n)
                        if n >= 1:
                            col_max(n - 1)
                    for n in range(2 * ITERATIONS + 1):
                        f = k * (2 * ITERATIONS + 1) + n
                        e.wait_ge(s.turned, f + 1)
                        sums = bank[7][:, 0:P].rearrange("p (h r) -> p h r", h=AH)[:, :, 0:SB]
                        if n == 0:
                            e.wait_ge(s.pool, k * 6)
                        if n == 2 * ITERATIONS - 2:
                            e.reciprocal(u[:], sums)
                        elif n == 2 * ITERATIONS - 1:
                            e.reciprocal(v[:], sums)
                            e.tensor_copy(ku[:], sums)
                        elif n == 2 * ITERATIONS:
                            e.tensor_copy(kv[:], sums).then_inc(s.fin_u, 1)
                        if n < 2 * ITERATIONS:
                            e.reciprocal(diag((ub, vb)[n % 2]), sums).then_inc(s.factor, 1)
                    for n in range(2):
                        e.wait_ge(s.back, k * 2 + n + 1)
                        e.tensor_tensor(att[:, 4 * n:4 * n + 4, :].rearrange("p b (h d) -> p b h d", d=AHD),
                                        bank[2 + n][:].rearrange("p (b h r) -> p b h r", h=AH, r=QROWS)[:, :, :, 0:AHD],
                                        alpha[:, :, 4 * n:4 * n + 4].rearrange("p h b -> p b h").unsqueeze(3)
                                        .broadcast_to([P, 4, AH, AHD]), ALU.mult).then_inc(s.att, 1)
                    e.wait_ge(s.proj, k + 1)
                    e.wait_ge(s.x, k)
                    e.tensor_tensor(res[:], bank[5][:].rearrange("p (b d) -> p b d", d=D), mid(bproj[:], SB),
                                    ALU.add).then_inc(s.res, 1)

            @block.tensor
            def _(e):
                e.wait_ge(s.wready, 1)
                with e.Fori(0, SETS) as k:
                    e.wait_ge(s.zset, k + 1)
                    e.wait_ge(s.res, k)
                    for n, t in enumerate((wu, wm)):
                        for par in range(2):
                            e.matmul(bank[2 * n + par][:], t[:, par, :], zset[:], start=True,
                                     stop=True).then_inc(s.ut_ps, 1)
                    for q in range(SB // 2):
                        mm = e.matmul(bank[4][:, q * P:(q + 1) * P], zset[:, q * S:(q + 1) * S],
                                      wv[:].rearrange("p a d -> p (a d)"), start=True, stop=True)
                    mm.then_inc(s.val_ps, 1)
                    e.wait_ge(s.ut, k * 4 + 4)

                    def unit(n):
                        return n // 2, n % 2, [4 * (n % 2) + b for b in range(4)]

                    def score(n):
                        h, half, batches = unit(n)
                        if n >= 3:
                            e.wait_ge(s.exped, k * (4 * AH) + 2 * (n - 3) + 2)
                        if n == 1:
                            e.wait_ge(s.val, k * 2 + 2)
                        hr = slice(QROWS * h, QROWS * (h + 1))
                        for i, b in enumerate(batches):
                            at = slice((b // 2) * S, (b // 2 + 1) * S)
                            e.matmul(bank[n % 3][:, i * S:(i + 1) * S], ut[hr, b % 2, at], mt[hr, b % 2, at],
                                     start=i == 0, stop=False, skip_group_check=True)
                            mm = e.matmul(bank[3 + n % 3][:, i * S:(i + 1) * S], mt[hr, b % 2, at], ut[hr, b % 2, at],
                                          start=i == 0, stop=False, skip_group_check=True)
                        mm.then_inc(s.scored, 1)

                    def shift(n, m, along, across, done):
                        e.matmul(along[:], c.neg_ident[:], bcast(m[:, n % 2], S), start=False, stop=False,
                                 skip_group_check=True)
                        for i in range(4):
                            mm = e.matmul(across[:, i * S:(i + 1) * S], m[:, n % 2, i:i + 1].broadcast_to([P, S]),
                                          c.neg_ident[:], start=False, stop=True, skip_group_check=True)
                        mm.then_inc(done, 1)

                    for n in range(2 * AH + 2):
                        if n < 2 * AH:
                            score(n)
                        if 1 <= n <= 2 * AH:
                            e.wait_ge(s.rmaxed, k * (2 * AH) + n)
                            shift(n - 1, rmax, bank[(n - 1) % 3], bank[3 + (n - 1) % 3], s.rowed)
                        if n >= 2:
                            e.wait_ge(s.cmaxed, k * (2 * AH) + n - 1)
                            shift(n - 2, cmax, bank[3 + (n - 2) % 3], bank[(n - 2) % 3], s.coled)
                    e.wait_ge(s.exped, (k + 1) * (4 * AH))
                    for n in range(2 * ITERATIONS + 1):
                        f = k * (2 * ITERATIONS + 1) + n
                        if n > 0:
                            e.wait_ge(s.factor, k * (2 * ITERATIONS) + n)
                        e.wait_ge(s.rows, f)
                        kern = (k_ji, k_ij)[n % 2]
                        for b in range(SB):
                            for h in range(AH):
                                lhs = c.diag_ones[:, b, :] if n == 0 else (vb, ub)[n % 2][:, h, b, :]
                                mm = e.matmul(bank[6][QROWS * h:QROWS * (h + 1), 0:S], lhs, kern[:, h, b, :],
                                              start=b == 0, stop=b == SB - 1, skip_group_check=True)
                        mm.then_inc(s.summed, 1)
                        e.wait_ge(s.rows, f + 1)
                        if n > 0:
                            e.wait_ge(s.factor, k * (2 * ITERATIONS) + n)
                        else:
                            e.wait_ge(s.fin_u, k)
                        e.transpose(bank[7][:, 0:P], rows[:], c.ident[:]).then_inc(s.turned, 1)
                    e.wait_ge(s.valb, k + 1)
                    for b in range(SB):
                        for h in range(AH):
                            mm = e.matmul(bank[b // 4][QROWS * h:QROWS * (h + 1), (b % 4) * S:(b % 4 + 1) * S],
                                          valb[:, b, h, :], k_ji[:, h, b, :], start=True, stop=True)
                    mm.then_inc(s.out_ps, 1)
                    for n in range(2):
                        e.wait_ge(s.out_t, k * 2 + n + 1)
                        for b in range(4):
                            mm = e.transpose(bank[2 + n][:, b * S:(b + 1) * S],
                                             out_t[:, (4 * n + b) * S:(4 * n + b + 1) * S], c.ident[:])
                        mm.then_inc(s.back, 1)
                    e.wait_ge(s.att, k * 2 + 2)
                    for q in range(SB // 2):
                        mm = e.transpose(bank[4][:, q * S:(q + 1) * S],
                                         att[:, 2 * q:2 * q + 2, :].rearrange("p b d -> p (b d)"), c.ident[:])
                    mm.then_inc(s.att_ps, 1)
                    e.wait_ge(s.att_t, k + 1)
                    for q in range(SB // 2):
                        mm = e.matmul(bank[5][:, q * P:(q + 1) * P], att_t[:, q * S:(q + 1) * S],
                                      wproj[:].rearrange("p a d -> p (a d)"), start=True, stop=True)
                    mm.then_inc(s.proj, 1)


def route(nc, c):
    with ExitStack() as ctx:
        sb = lambda n, s, d=F32: ctx.enter_context(nc.sbuf_tensor("r_" + n, s, d))
        sem = lambda n: ctx.enter_context(nc.semaphore("r_" + n))
        wide = [P, B * EXPERTS]
        shifted, probs, rest, equal, picked, both = (sb(n, wide) for n in
                                                     ("shifted", "probs", "rest", "equal", "picked", "both"))
        peak, total, first, second, rank = (sb(n, [P, B]) for n in ("peak", "total", "first", "second", "rank"))
        s_step, s_exp = sem("step"), sem("exp")
        w3 = lambda t: t[:].rearrange("p (b e) -> p b e", e=EXPERTS)
        over = lambda t: bcast(t[:], EXPERTS)

        with nc.Block() as block:
            @block.scalar
            def _(e):
                e.wait_ge(s_step, 2)
                e.activation(shifted[:], shifted[:], ACT.Exp).then_inc(s_exp, 1)

            @block.vector
            def _(e):
                n = [0]

                def then(ins):
                    n[0] += 1
                    ins.then_inc(s_step, 1)
                    e.wait_ge(s_step, n[0])

                def pick(values, largest, out):
                    then(e.tensor_reduce(largest[:], w3(values), AX.X, ALU.max))
                    then(e.tensor_tensor(w3(equal), w3(values), over(largest), ALU.is_equal))
                    then(e.tensor_tensor(w3(equal), w3(equal), mid(c.priority[:], B), ALU.mult))
                    then(e.tensor_reduce(rank[:], w3(equal), AX.X, ALU.max))
                    then(e.tensor_tensor(w3(out), w3(equal), over(rank), ALU.is_equal))

                then(e.tensor_reduce(peak[:], w3(c.gates), AX.X, ALU.max))
                then(e.tensor_tensor(w3(shifted), w3(c.gates), over(peak), ALU.subtract))
                e.wait_ge(s_exp, 1)
                then(e.tensor_reduce(total[:], w3(shifted), AX.X, ALU.add))
                then(e.reciprocal(total[:], total[:]))
                then(e.tensor_tensor(w3(probs), w3(shifted), over(total), ALU.mult))
                pick(probs, first, picked)
                then(e.tensor_scalar(rest[:], picked[:], -2.0, None, ALU.mult))
                then(e.tensor_tensor(rest[:], rest[:], probs[:], ALU.add))
                pick(rest, second, both)
                then(e.tensor_tensor(both[:], both[:], picked[:], ALU.add))
                then(e.tensor_tensor(both[:], both[:], probs[:], ALU.mult))
                then(e.tensor_tensor(total[:], first[:], second[:], ALU.add))
                then(e.reciprocal(total[:], total[:]))
                then(e.tensor_tensor(w3(c.gates), w3(both), over(total), ALU.mult))


def experts(nc, c, a):
    with ExitStack() as ctx:
        sb = lambda n, s, d=F32: ctx.enter_context(nc.sbuf_tensor("m_" + n, s, d))
        ps = lambda n, s, d=F32: ctx.enter_context(nc.psum_tensor("m_" + n, s, d))
        sem = lambda n: ctx.enter_context(nc.semaphore("m_" + n))
        w1 = sb("w1", [P, EXPERTS, 2, HID])
        w2 = sb("w2", [P, EXPERTS, HALVES, D])
        bias = sb("bias", [P, EXPERTS, HALVES + 3])
        b1 = sb("b1", [P, EXPERTS, HALVES])
        hid = sb("hid", [P, 2, HALVES, BANK])
        y_t = sb("y_t", [P, 2, NPAIR2 * S])
        gated = sb("gated", [P, 2, GC])
        bank = [ps(f"bank{i}", [P, BANK]) for i in range(8)]
        names = ("loaded", "offsets", "b1_ready", "w1_ready", "h_made", "gelued", "y_made", "y_copied", "y_back",
                 "gated", "summed")
        s = type("Sems", (), {n: sem("m_" + n) for n in names})

        def over_experts(e, step):
            def steps(g, first=False):
                for x in range(EXPERTS):
                    before = (g, x - 1) if x >= 1 else (None if first else (g - 1, EXPERTS - 1))
                    before2 = (g, x - 2) if x >= 2 else (None if first else (g - 1, EXPERTS + x - 2))
                    step((g, x), before, before2)
            steps(0, first=True)
            with e.Fori(1, NG) as g:
                steps(g)
            step(None, (NG - 1, EXPERTS - 1), (NG - 1, EXPERTS - 2))
            step(None, None, (NG - 1, EXPERTS - 1))

        at = lambda gx: gx[0] * EXPERTS + gx[1]

        with nc.Block() as block:
            @block.sync
            def _(e):
                e.dma_start(w1[:].rearrange("p x a n -> p (x a n)"), a["moe_w1"]).then_inc(s.loaded, 16)
                e.dma_start(w2[:].rearrange("p x a n -> p (x a n)"), a["moe_w2"]).then_inc(s.loaded, 16)
                e.dma_start(bias[:].rearrange("p x n -> p (x n)"), a["moe_bias"]).then_inc(s.loaded, 16)

            @block.tensor
            def _(e):
                e.wait_ge(s.loaded, 48)
                for x in range(EXPERTS):
                    for half in range(HALVES):
                        mm = e.matmul(bank[0][:, x * HALVES + half:x * HALVES + half + 1],
                                      w1[:, x, 0, half * P:(half + 1) * P], bias[:, x, HALVES + 2:],
                                      start=True, stop=True)
                mm.then_inc(s.offsets, 1)
                e.wait_ge(s.w1_ready, EXPERTS)

                def step(now, before, before2):
                    if now:
                        g, x = now
                        n, par = at(now), x % 2
                        for half in range(HALVES):
                            if not isinstance(g, int) or x >= 2:
                                e.wait_ge(s.gelued, n * 2 - 3 + half)
                            for q in range(2):
                                mm = e.matmul(bank[2 * par + half][:, q * 2 * S:(q + 1) * 2 * S],
                                              w1[:, x, q, half * P:(half + 1) * P],
                                              c.zt[:, ds(g * NPAIR2 * S, NPAIR2 * S)], start=True, stop=True)
                            mm.then_inc(s.h_made, 1)
                    if before:
                        n, x = at(before), before[1]
                        par = x % 2
                        e.wait_ge(s.gelued, n * 2 + 2)
                        if not isinstance(n, int) or n >= 2:
                            e.wait_ge(s.y_copied, n - 1)
                        for half in range(HALVES):
                            for q in range(2):
                                mm = e.matmul(bank[4 + par][q * D:(q + 1) * D, 0:NPAIR2 * S], w2[:, x, half, :],
                                              hid[:, par, half, q * 2 * S:(q + 1) * 2 * S],
                                              start=half == 0, stop=half == HALVES - 1)
                        mm.then_inc(s.y_made, 1)
                    if before2:
                        n, par = at(before2), before2[1] % 2
                        e.wait_ge(s.y_copied, n + 1)
                        if not isinstance(n, int) or n >= 2:
                            e.wait_ge(s.gated, n - 1)
                        for q in range(NPAIR2):
                            mm = e.transpose(bank[6 + par][:, q * S:(q + 1) * S], y_t[:, par, q * S:(q + 1) * S],
                                             c.ident[:])
                        mm.then_inc(s.y_back, 1)

                over_experts(e, step)

            @block.scalar
            def _(e):
                def step(now, before, before2):
                    if now:
                        n, x = at(now), now[1]
                        par = x % 2
                        for half in range(HALVES):
                            e.wait_ge(s.h_made, n * 2 + half + 1)
                            if not isinstance(n, int) or n >= 2:
                                e.wait_ge(s.y_made, n - 1)
                            e.activation(hid[:, par, half, :], bank[2 * par + half][:], ACT.Gelu,
                                         bias=b1[:, x, half:half + 1]).then_inc(s.gelued, 1)
                    if before:
                        n, x = at(before), before[1]
                        par = x % 2
                        e.wait_ge(s.y_made, n + 1)
                        if not isinstance(n, int) or n >= 2:
                            e.wait_ge(s.y_back, n - 1)
                        e.activation(y_t[:, par, :], bank[4 + par][:, 0:NPAIR2 * S], ACT.Identity,
                                     bias=bias[:, x, HALVES:HALVES + 1]).then_inc(s.y_copied, 1)

                over_experts(e, step)

            @block.vector
            def _(e):
                e.wait_ge(s.offsets, 1)
                e.tensor_tensor(b1[:], bank[0][:, 0:EXPERTS * HALVES].rearrange("p (x n) -> p x n", n=HALVES),
                                bias[:, :, 0:HALVES], ALU.add).then_inc(s.b1_ready, 1)
                e.wait_ge(s.b1_ready, 1)
                for x in range(EXPERTS):
                    wx = w1[:, x].rearrange("p a n -> p (a n)")
                    e.tensor_scalar(wx, wx, bias[:, x, HALVES + 1:HALVES + 2], None, ALU.mult).then_inc(s.w1_ready, 1)

                def step(now, before, before2):
                    if before2:
                        g, x = before2
                        n, par = at(before2), x % 2
                        e.wait_ge(s.y_back, n + 1)
                        if not isinstance(n, int) or n >= 2:
                            e.wait_ge(s.summed, n - 1)
                        gate = c.gates[:, ds(g * GB * EXPERTS, GB * EXPERTS)].rearrange(
                            "p (b e) -> p b e", e=EXPERTS)[:, :, x]
                        e.tensor_tensor(gated[:, par, :].rearrange("p (b d) -> p b d", d=D),
                                        bank[6 + par][:, 0:GC].rearrange("p (b d) -> p b d", d=D),
                                        bcast(gate, D), ALU.mult).then_inc(s.gated, 1)

                over_experts(e, step)

            @block.gpsimd
            def _(e):
                def step(now, before, before2):
                    if before2:
                        g, x = before2
                        n, par = at(before2), x % 2
                        e.wait_ge(s.gated, n + 1)
                        if not isinstance(n, int) or n >= 1:
                            e.wait_ge(s.summed, n)
                        own_wait(e, c)
                        e.tensor_tensor(group(c.x, g), group(c.x, g),
                                        gated[:, par, :].rearrange("p (b d) -> p b d", d=D),
                                        ALU.add).then_inc(s.summed, 1)

                over_experts(e, step)


def store(nc, c, a):
    with ExitStack() as ctx:
        stored = ctx.enter_context(nc.semaphore("stored"))
        with nc.Block() as block:
            @block.sync
            def _(e):
                e.dma_start(a["out"].rearrange("b s d -> s b d"),
                            c.x[:].rearrange("p (b d) -> p b d", d=D)).then_inc(stored, 16)
                e.wait_ge(stored, 16)


class Chip:

    def __init__(self, nc, ctx):
        sb = lambda n, s, d=F32: ctx.enter_context(nc.sbuf_tensor(n, s, d))
        self.x = sb("x_sb", [P, B * D])
        self.ident = sb("ident", [P, P])
        self.ident16 = sb("ident16", [P, P], F16)
        self.neg_ident = sb("neg_ident", [P, P], BF16)
        self.sel_f = sb("sel_f", [P, 4, P])
        self.sel = sb("sel", [P, 4, P], F16)
        self.bias = sb("bias", [P, H, S])
        self.ln1_w, self.ln1_b = sb("ln1_w", [P, LAYERS * D]), sb("ln1_b", [P, LAYERS * D])
        self.ln2 = sb("ln2_wb", [P, 2, LAYERS])
        self.v = sb("v", [P, 2, PAIRS, QROWS])
        self.minus_half = sb("minus_half", [P, NB_CHUNK])
        self.zt = sb("zt", [P, NG * NPAIR2 * S])
        self.xt = sb("xt", [P, B * D])
        self.gates = sb("gates", [P, B * EXPERTS])
        self.priority = sb("priority", [P, EXPERTS])
        self.diag_ones = sb("diag_ones", [P, SB, QROWS])
        self.lnf_w, self.lnf_b = sb("lnf_w", [P, D]), sb("lnf_b", [P, D])
        self.wr, self.br = sb("wr_sb", [P, 2 * EXPERTS]), sb("br", [P, EXPERTS])
        self.waited = ctx.enter_context(nc.semaphore("waited"))
        self.x_ready = ctx.enter_context(nc.semaphore("x_ready"))


def build(nc, a):
    with ExitStack() as ctx:
        c = Chip(nc, ctx)
        embed(nc, c, a)
        tower(nc, c, a)
        normalise(nc, c, "nf_", c.x, affine=(c.lnf_w, c.lnf_b), dst=c.x)
        normalise(nc, c, "na_", c.x, turned=c.zt)
        sinkhorn(nc, c, a)
        normalise(nc, c, "nx_", c.x, dst=c.xt, logits=(c.wr, c.br, c.gates))
        normalise(nc, c, "ne_", c.xt, turned=c.zt)
        route(nc, c)
        experts(nc, c, a)
        store(nc, c, a)


def constants():
    f = np.float32
    inv_freq = (1.0 / 10000.0 ** (np.arange(0, D, 2, dtype=f) / D)).astype(f)
    angle = (np.arange(POSITIONS, dtype=f)[:, None] * inv_freq[None]).astype(f)
    pos = np.concatenate([np.sin(angle), np.cos(angle)], axis=-1).astype(f)
    at = np.arange(S)
    dist = np.abs(at[:, None] // GRID_W - at[None] // GRID_W) + np.abs(at[:, None] % GRID_W - at[None] % GRID_W)
    bias = np.zeros((H, S, S))
    for h in range(H):
        bias[h] = (np.triu(-2.0 ** -(0.5 + h) * dist) + np.tril(-2.0 ** -(1.0 + h) * dist)) / SCALE
    sel = np.zeros((P, 4, P), f)
    for side in range(2):
        for g in range(2):
            for j in range(4):
                for part in range(4):
                    which = part // 2 if side == 0 else part % 2
                    for d in range(HD):
                        sel[which * D + (4 * g + j) * HD + d, 2 * side + g, QROWS * j + HD * part + d] = 1
    return {
        "c_ident": np.eye(P, dtype=f), "c_sel": sel, "c_iota_v": np.tile(np.arange(VOCAB, dtype=f), (P, 1)),
        "c_iota_p": np.arange(P, dtype=f)[:, None],
        "c_pos": np.ascontiguousarray(pos.reshape(POS_CHUNKS, P, D).transpose(1, 0, 2)),
        "c_priority": np.tile(np.arange(EXPERTS, 0, -1, dtype=f), (P, 1)),
        "c_diag": np.tile(np.eye(SB, QROWS, dtype=f)[None], (P, 1, 1)),
        "c_bias": np.ascontiguousarray(bias.transpose(2, 0, 1)).astype(f),
    }


def laid_out(v):
    v = {k: np.asarray(x) for k, x in v.items()}
    w1, w2, b1, b2 = (v[f"L0_tok_{n}"] for n in ("w1", "w2", "b1", "b2"))
    zero = np.zeros_like(w1)
    arrays = {
        "mlp": np.concatenate([
            np.concatenate([w1, zero], 1), np.concatenate([zero, w1], 1),
            w2.reshape(LAYERS, HALVES, P, D).transpose(0, 2, 1, 3).reshape(LAYERS, P, HALVES * D),
            b1.reshape(LAYERS, HALVES, P).transpose(0, 2, 1),
            np.concatenate([b2, b2], 1)[:, :, None]], 2),
        "ln2": np.concatenate([np.stack([v["L0_tok_ln2_w"].T, v["L0_tok_ln2_b"].T], 1)] * 2, 0),
    }
    w1, w2, b1, b2, g, b = (v[f"L0_ffn_{n}"] for n in ("W1", "W2", "b1", "b2", "ln_g", "ln_b"))
    zero = np.zeros_like(w1)
    arrays["moe_w1"] = np.stack([np.concatenate([w1, zero], 1), np.concatenate([zero, w1], 1)], 2) \
        .transpose(1, 0, 2, 3).reshape(P, EXPERTS * 2 * HID)
    arrays["moe_w2"] = w2.reshape(EXPERTS, HALVES, P, D).transpose(2, 0, 1, 3).reshape(P, EXPERTS * HALVES * D)
    twice = lambda t: np.concatenate([t.T, t.T], 0)[:, :, None]
    arrays["moe_bias"] = np.concatenate([b1.reshape(EXPERTS, HALVES, P).transpose(2, 0, 1), twice(b2), twice(g),
                                       twice(b)], 2).reshape(P, EXPERTS * (HALVES + 3))
    wr = v["L0_ffn_Wr"]
    arrays["wr"] = np.concatenate([np.concatenate([wr, np.zeros_like(wr)], 1),
                                   np.concatenate([np.zeros_like(wr), wr], 1)], 0)
    for n in ("x", "pos_S", "L0_tok_lnf_w", "L0_tok_lnf_b", "L0_ffn_br", "L0_attn_W_qkv", "L0_attn_W_proj",
              "L0_attn_b_proj", "L0_attn_phase", "L0_attn_ent", "L0_attn_gate", "L0_attn_tau", "L0_tok_emb_table", "L0_tok_input_weight", "L0_tok_position_weight",
              "L0_tok_ln1_w", "L0_tok_ln1_b"):
        arrays[n] = v[n]
    arrays["L0_attn_tau"] = arrays["L0_attn_tau"].reshape(1)
    return {k: np.ascontiguousarray(x) for k, x in arrays.items()} | constants()


def kernel(**inputs):
    import concourse.bacc as bacc
    from concourse.bass_utils import run_bass_kernel_spmd

    nc = bacc.Bacc("TRN2", target_bir_lowering=False, num_devices=1)
    arrays = laid_out(inputs)
    aps = {n: nc.dram_tensor(n, v.shape, mybir.dt.from_np(v.dtype), kind="ExternalInput").ap()
           for n, v in arrays.items()}
    aps["out"] = nc.dram_tensor("out", (B, S, D), F32, kind="ExternalOutput").ap()
    build(nc, aps)
    return run_bass_kernel_spmd(nc, [arrays], core_ids=[0]).results[0]["out"]
```

```python
from contextlib import ExitStack

import numpy as np

import concourse.bass as bass
from concourse import mybir
from concourse.alu_op_type import AluOpType as ALU

ACT = mybir.ActivationFunctionType
AX = mybir.AxisListType
F32 = mybir.dt.float32
F16 = mybir.dt.float16
BF16 = mybir.dt.bfloat16
I32 = mybir.dt.int32
ds = bass.ds

P = 128
B, S, D = 128, 128, 64
LAYERS, H = 6, 8
HD = D // H
HID = 256
HALVES = HID // P
VOCAB = 16
POSITIONS = 1024
POS_CHUNKS = POSITIONS // P
GRID_W = 32
GB = 4
NG = B // GB
GC = GB * D
PAIRS = GB * H
NPAIR2 = GB // 2
EB = 8
BANK = 512
SBANKS = 4
QROWS = 32
AHEAD, BEHIND = 3, 2
ROUNDS = (NG - AHEAD - BEHIND) // 2
W1_UP = 64.0
LEAD = 4
EPS = 1e-5
SCALE = 1.0 / float(np.sqrt(HD))


def group(t, g):
    return t[:, ds(g * GC, GC)].rearrange("p (b d) -> p b d", d=D)


def bcast(t, n):
    return t.unsqueeze(2).broadcast_to([t.shape[0], t.shape[1], n])


def mid(t, n):
    return t.unsqueeze(1).broadcast_to([t.shape[0], n, t.shape[1]])


def of_parity(t, q):
    return t.rearrange("p (a q t) -> p a q t", q=2, t=S)[:, :, q, :]


def own_wait(e, c):
    e.sem_inc(c.waited, 1)


def embed(nc, c, a):
    with ExitStack() as ctx:
        sb = lambda n, s, d=F32: ctx.enter_context(nc.sbuf_tensor(n, s, d))
        ps = lambda n, s, d=F32: ctx.enter_context(nc.psum_tensor(n, s, d))
        sem = lambda n: ctx.enter_context(nc.semaphore(n))
        steps = B // EB
        tok_i, tok_f = sb("tok_i", [P, S], I32), sb("tok_f", [P, S])
        tok_t = sb("tok_t", [P, B])
        pos_i, pos_f = sb("pos_i", [P, S], I32), sb("pos_f", [P, S])
        iota_v = sb("iota_v", [P, VOCAB])
        iota_p = sb("iota_p", [P, 1])
        onehot = sb("onehot", [P, B * VOCAB])
        pos_hot = sb("pos_hot", [P, POS_CHUNKS, S])
        pos_tab = sb("pos_tab", [P, POS_CHUNKS, D])
        emb = sb("emb", [P, EB * D])
        weights = sb("weights", [P, 2])
        pos_emb = sb("pos_emb", [P, D])
        hot_t = sb("hot_t", [P, 2, S])
        tokt_ps, hot_ps = ps("tokt_ps", [P, B]), ps("hot_ps", [P, 2, BANK])
        pos_ps, x_ps = ps("pos_ps", [P, D]), ps("x_ps", [P, 2, BANK])
        loaded, emb_zero, emb_loaded = sem("e_loaded"), sem("e_emb_zero"), sem("e_emb_loaded")
        cast, tok_turned, tok_copied = sem("e_cast"), sem("e_tok_turned"), sem("e_tok_copied")
        hot, pos_made, pos_done, x_made = sem("e_hot"), sem("e_pos_made"), sem("e_pos_done"), sem("e_x_made")
        turned, copied = sem("e_turned"), sem("e_copied")

        with nc.Block() as block:
            @block.sync
            def _(e):
                for dst, src in (
                    (c.ident, a["c_ident"]), (c.sel_f, a["c_sel"]), (tok_i, a["x"]),
                    (iota_v, a["c_iota_v"]), (iota_p, a["c_iota_p"]), (pos_tab, a["c_pos"]),
                    (c.bias, a["c_bias"]), (c.bias16, a["c_bias16"]),
                    (pos_i, a["pos_S"].partition_broadcast(P)),
                    (weights[:, 0:1], a["L0_tok_input_weight"].partition_broadcast(P)),
                    (weights[:, 1:2], a["L0_tok_position_weight"].partition_broadcast(P)),
                    (c.ln1_w, a["L0_tok_ln1_w"].rearrange("l d -> (l d)").partition_broadcast(P)),
                    (c.ln1_b, a["L0_tok_ln1_b"].rearrange("l d -> (l d)").partition_broadcast(P)),
                    (c.priority, a["c_priority"]), (c.diag_ones, a["c_diag"]),
                    (c.wr, a["wr"]), (c.br, a["L0_ffn_br"].partition_broadcast(P)),
                    (c.lnf_w, a["L0_tok_lnf_w"].partition_broadcast(P)),
                    (c.lnf_b, a["L0_tok_lnf_b"].partition_broadcast(P)),
                ):
                    e.dma_start(dst[:] if not isinstance(dst, bass.AP) else dst, src).then_inc(loaded, 16)
                e.wait_ge(emb_zero, 1)
                for b in range(EB):
                    e.dma_start(emb[b * VOCAB:(b + 1) * VOCAB, b * D:(b + 1) * D],
                                a["L0_tok_emb_table"]).then_inc(emb_loaded, 16)

            @block.gpsimd
            def _(e):
                e.memset(emb[:], 0.0).then_inc(emb_zero, 1)
                e.memset(c.minus_half[:], -0.5)
                for par in range(2):
                    e.memset(c.v[:, par, :, HD:HD + 1], 1.0)
                    e.memset(c.v[:, par, :, HD + 1:QROWS], 0.0)

            @block.vector
            def _(e):
                e.wait_ge(loaded, 16 * 19)
                e.tensor_copy(tok_f[:], tok_i[:]).then_inc(cast, 1)
                e.tensor_copy(pos_f[:], pos_i[:]).then_inc(cast, 1)
                e.tensor_copy(c.ident16[:], c.ident[:])
                e.tensor_copy(c.sel[:], c.sel_f[:])
                e.tensor_scalar(c.neg_ident[:], c.ident[:], -1.0, None, ALU.mult)
                e.wait_ge(cast, 2)
                for k in range(POS_CHUNKS):
                    e.tensor_scalar(pos_hot[:, k, :], pos_f[:], float(-k * P), iota_p[:, 0:1],
                                    ALU.add, ALU.is_equal).then_inc(hot, 1)
                e.wait_ge(tok_turned, 1)
                e.tensor_copy(tok_t[:], tokt_ps[:]).then_inc(tok_copied, 1)
                e.wait_ge(tok_copied, 1)
                e.tensor_tensor(onehot[:].rearrange("p (b v) -> p b v", v=VOCAB), bcast(tok_t[:], VOCAB),
                                mid(iota_v[:], B), ALU.is_equal).then_inc(hot, 1)
                e.wait_ge(emb_loaded, 16 * EB)
                e.tensor_scalar(emb[:], emb[:], weights[:, 0:1], None, ALU.mult).then_inc(cast, 1)
                e.wait_ge(pos_made, 1)
                e.tensor_scalar(pos_emb[:], pos_ps[:], weights[:, 1:2], None, ALU.mult).then_inc(pos_done, 1)
                e.wait_ge(pos_done, 1)
                for i in range(steps):
                    e.wait_ge(x_made, i + 1)
                    for k in range(EB // GB):
                        e.tensor_tensor(group(c.x, i * EB // GB + k),
                                        x_ps[:, i % 2, k * GC:(k + 1) * GC].rearrange("p (b d) -> p b d", d=D),
                                        mid(pos_emb[:], GB), ALU.add).then_inc(c.x_ready, 1)

            @block.tensor
            def _(e):
                e.wait_ge(loaded, 16 * 19)
                e.wait_ge(cast, 1)
                e.transpose(tokt_ps[:], tok_f[:], c.ident[:]).then_inc(tok_turned, 1)
                e.wait_ge(hot, POS_CHUNKS)
                for k in range(POS_CHUNKS):
                    mm = e.matmul(pos_ps[:], pos_hot[:, k, :], pos_tab[:, k, :],
                                  start=k == 0, stop=k == POS_CHUNKS - 1)
                mm.then_inc(pos_made, 1)
                e.wait_ge(hot, POS_CHUNKS + 1)
                e.wait_ge(cast, 3)
                for i in range(steps + 1):
                    if i < steps:
                        if i >= 2:
                            e.wait_ge(copied, i - 1)
                        e.transpose(hot_ps[:, i % 2, 0:S], onehot[:, i * EB * VOCAB:(i + 1) * EB * VOCAB],
                                    c.ident[:]).then_inc(turned, 1)
                    if i >= 1:
                        e.wait_ge(copied, i)
                        if i >= 3:
                            e.wait_ge(c.x_ready, (i - 2) * EB // GB)
                        e.matmul(x_ps[:, (i - 1) % 2, :], hot_t[:, (i - 1) % 2, :], emb[:],
                                 start=True, stop=True).then_inc(x_made, 1)

            @block.scalar
            def _(e):
                for i in range(steps):
                    e.wait_ge(turned, i + 1)
                    if i >= 2:
                        e.wait_ge(x_made, i - 1)
                    e.activation(hot_t[:, i % 2, :], hot_ps[:, i % 2, 0:S], ACT.Copy).then_inc(copied, 1)


def tower(nc, c, a):
    with ExitStack() as ctx:
        sb = lambda n, s, d=F32: ctx.enter_context(nc.sbuf_tensor(n, s, d))
        ps = lambda n, s, d=F32: ctx.enter_context(nc.psum_tensor(n, s, d))
        sem = lambda n: ctx.enter_context(nc.semaphore(n))

        sum1, mean1, sqsum1, var1, rstd1 = (sb(n, [P, GB]) for n in ("sum1", "mean1", "sqsum1", "var1", "rstd1"))
        xc1, sq1, z1, zw1 = (sb(n, [P, GC]) for n in ("xc1", "sq1", "z1", "zw1"))
        qf = sb("qf", [P, 2, GC])
        q16 = sb("q16", [P, GB, 2, D], F16)
        qt16 = sb("qt16", [P, GB * S], F16)
        left = sb("left", [P, 2, 2, GB * S], F16)
        right = sb("right", [P, 2, 2, GB * S], F16)
        mx = sb("mx", [P, SBANKS, GB], BF16)
        biased = sb("biased", [P, 2, BANK])
        prob = sb("prob", [P, H, BANK])
        out_t = sb("out_t", [P, 2, BANK])
        rden = sb("rden", [P, 2, GB, 4])
        att = sb("att", [P, GC])
        sum2, mean2, sqsum2, var2, rstd2 = (sb(n, [P, GB]) for n in ("sum2", "mean2", "sqsum2", "var2", "rstd2"))
        xc2, sq2, z2 = (sb(n, [P, GC]) for n in ("xc2", "sq2", "z2"))
        z16 = sb("z16", [P, GB, 2, D], F16)
        zt = c.zt_split
        wcur = sb("wcur", [P, HID + HALVES * D + HALVES + 3])
        W1 = wcur[:, 0:HID]
        W2 = lambda half: wcur[:, HID + half * D:HID + (half + 1) * D]
        B1 = wcur[:, HID + HALVES * D:HID + HALVES * D + HALVES]
        B2, LN2_W, LN2_B = (wcur[:, n:n + 1] for n in range(HID + HALVES * D + HALVES, HID + HALVES * D + HALVES + 3))
        w1g = sb("w1g", [P, HID])
        w1_parts = sb("w1_parts", [P, 2, HID], F16)
        b1g = sb("b1g", [P, HALVES])
        hid = sb("hid", [P, 2, HALVES, BANK])
        y_t = sb("y_t", [P, 2, NPAIR2 * S])

        pool = [ps(f"bank{i}", [P, BANK]) for i in range(8)]
        score_ps = pool[0:SBANKS]
        turn_ps, stack_ps, out_ps, back_ps = pool[SBANKS:]
        q_turn_ps = turn_ps[:, 0:GB * S // 2].bitcast(F16)
        h_ps = lambda par, half: pool[2 * par + half]
        y_ps = lambda par: pool[4 + par]
        yb_ps = lambda par: pool[6 + par]

        names = ("sqsum1", "sqsum2", "v", "sum1", "mean1", "xc1", "sq1", "var1", "rstd1", "z1", "zw1", "q", "hi", "lo", "q_turned",
                 "q_copied", "stacked", "stack_copied", "scored", "maxed", "shifted", "biased", "exped",
                 "weighed", "out_copied", "back", "recip", "divided", "x_att", "sum2", "mean2", "xc2", "sq2",
                 "var2", "rstd2", "z2", "z2_turned", "hi2", "lo2", "offset", "w_gained", "w_split", "zt_copied", "w_loaded", "h_made", "gelued", "y_made",
                 "y_copied", "y_back")
        sems = {n: sem("t_" + n) for n in names}
        s = type("Sems", (), sems)

        def over_groups(e, step):
            for i in range(-AHEAD, BEHIND):
                step(i, i % 2)
            with e.Fori(0, ROUNDS) as j:
                step(j * 2 + BEHIND, BEHIND % 2)
                step(j * 2 + BEHIND + 1, (BEHIND + 1) % 2)
            for i in range(BEHIND + 2 * ROUNDS, NG + BEHIND):
                step(i, i % 2)

        def live(g):
            return not isinstance(g, int) or 0 <= g < NG

        def over_mlp_groups(e, step):
            step(0, 0, "a")
            step(1, 1, "ab")
            with e.Fori(0, (NG - 2) // 2) as j:
                step(j * 2 + 2, 0, "abc")
                step(j * 2 + 3, 1, "abc")
            step(NG, 0, "bc")
            step(NG + 1, 1, "c")

        per_group = {"scored": H, "maxed": H, "shifted": H, "biased": H // 2, "exped": H, "weighed": 4, "out_copied": 2,
                     "back": 2, "recip": 2, "divided": 2, "stacked": 4, "stack_copied": 4, "h_made": 2, "gelued": 2}
        with nc.Block() as block:
            @block.gpsimd
            def _(e):
                for n in names:
                    if n not in ("w_loaded", "offset", "w_gained", "w_split"):
                        e.sem_inc(sems[n], LEAD * per_group.get(n, 1))

        with nc.Block() as block:
            @block.sync
            def _(e):
                with e.Fori(0, LAYERS) as l:
                    e.wait_ge(s.y_copied, l * NG + LEAD)
                    e.dma_start(wcur[:], a["mlp"][ds(l, 1)].rearrange("l p n -> (l p) n")).then_inc(s.w_loaded, 16)

            @block.vector
            def _(e):
                with e.Fori(0, LAYERS) as l:
                    G = lambda g: l * NG + g + LEAD

                    def peak(g, h):
                        if live(g):
                            e.wait_ge(s.scored, G(g) * H + h + 1)
                            e.tensor_reduce(mx[:, h % SBANKS, :],
                                            score_ps[h % SBANKS][:].rearrange("p (b t) -> p b t", t=S),
                                            AX.X, ALU.max).then_inc(s.maxed, 1)

                    def add_bias(g, h):
                        if live(g) and h % 2 == 0:
                            e.wait_ge(s.shifted, G(g) * H + h + 1)
                            e.wait_ge(s.exped, G(g) * H + h - 3)
                            e.tensor_tensor(biased[:, h // 2 % 2, :].rearrange("p (b t) -> p b t", t=S),
                                            score_ps[h % SBANKS][:].rearrange("p (b t) -> p b t", t=S),
                                            mid(c.bias[:, h // 2, :], GB), ALU.add).then_inc(s.biased, 1)

                    def mean(g, total, negated, totalled, ready):
                        if live(g):
                            e.tensor_reduce(total[:], group(c.x, g), AX.X, ALU.add).then_inc(totalled, 1)
                            e.wait_ge(totalled, G(g) + 1)
                            e.tensor_scalar(negated[:], total[:], -1.0 / D, None, ALU.mult).then_inc(ready, 1)

                    def variance(g, squares, squared, total, var, totalled, ready):
                        if live(g):
                            e.wait_ge(squared, G(g) + 1)
                            e.tensor_reduce(total[:], squares[:].rearrange("p (b d) -> p b d", d=D), AX.X,
                                            ALU.add).then_inc(totalled, 1)
                            e.wait_ge(totalled, G(g) + 1)
                            e.tensor_scalar(var[:], total[:], EPS, None, ALU.add).then_inc(ready, 1)

                    def divide(g, half):
                        if live(g):
                            e.wait_ge(s.back, G(g) * 2 + half + 1)
                            back = back_ps[:].rearrange("p (b j r) -> p b j r", b=GB, j=4)
                            e.reciprocal(rden[:, half], back[:, :, :, HD]).then_inc(s.recip, 1)
                            e.wait_ge(s.recip, G(g) * 2 + half + 1)
                            if half == 0:
                                e.wait_ge(s.x_att, G(g))
                            e.tensor_tensor(
                                att[:].rearrange("p (b g j d) -> p b g j d", b=GB, g=2, j=4)[:, :, half],
                                back[:, :, :, 0:HD],
                                rden[:, half].unsqueeze(3).broadcast_to([P, GB, 4, HD]),
                                ALU.mult).then_inc(s.divided, 1)

                    def step(i, par):
                        for h in range(H):
                            peak(i + (h + 2) // H, (h + 2) % H)
                            add_bias(i, h)
                            if h == 0:
                                variance(i + 2, sq1, s.sq1, sqsum1, var1, s.sqsum1, s.var1)
                            if h == 1:
                                divide(i - 1, 0)
                            if h == 2:
                                variance(i - 2, sq2, s.sq2, sqsum2, var2, s.sqsum2, s.var2)
                            if h == 4 and live(i + 3):
                                e.wait_ge(c.x_ready, l * NG + (i + 4))
                                mean(i + 3, sum1, mean1, s.sum1, s.mean1)
                            if h == 5:
                                divide(i - 1, 1)
                            if h == 2 and isinstance(i, int) and i == 0:
                                e.wait_ge(s.offset, l + 1)
                                e.tensor_tensor(b1g[:], back_ps[:, 0:HALVES], B1, ALU.add).then_inc(s.w_gained, 1)
                                e.tensor_scalar(w1g[:], W1, LN2_W, W1_UP, ALU.mult, ALU.mult).then_inc(s.w_gained, 1)
                                e.wait_ge(s.w_gained, l * 3 + 2)
                                e.tensor_copy(w1_parts[:, 0, :], w1g[:]).then_inc(s.w_gained, 1)
                                e.wait_ge(s.w_gained, l * 3 + 3)
                                e.tensor_tensor(w1_parts[:, 1, :], w1g[:], w1_parts[:, 0, :],
                                                ALU.subtract).then_inc(s.w_split, 1)
                            if h == 7 and live(i - 1):
                                e.wait_ge(s.x_att, G(i))
                                mean(i - 1, sum2, mean2, s.sum2, s.mean2)

                    over_groups(e, step)

                    def mlp(i, par, what):
                        if "c" in what:
                            e.wait_ge(s.y_back, G(i - 2) + 1)
                            e.tensor_tensor(group(c.x, i - 2), group(c.x, i - 2),
                                            yb_ps(par)[:, 0:GC].rearrange("p (b d) -> p b d", d=D),
                                            ALU.add).then_inc(c.x_ready, 1)

                    over_mlp_groups(e, mlp)

            @block.gpsimd
            def _(e):
                with e.Fori(0, LAYERS) as l:
                    G = lambda g: l * NG + g + LEAD
                    split = lambda t: t.rearrange("p (b d) -> p b d", d=D)

                    def centre(g, negated, ready, out, done):
                        if live(g):
                            e.wait_ge(ready, G(g) + 1)
                            own_wait(e, c)
                            e.tensor_tensor(split(out[:]), group(c.x, g), bcast(negated[:], D), ALU.add).then_inc(done, 1)

                    def scaled(g, var, ready, rstd, rooted, xc, z, done):
                        if live(g):
                            e.wait_ge(ready, G(g) + 1)
                            e.tensor_tensor(rstd[:], var[:], c.minus_half[:, 0:GB], ALU.pow).then_inc(rooted, 1)
                            e.wait_ge(rooted, G(g) + 1)
                            e.tensor_tensor(split(z[:]), split(xc[:]), bcast(rstd[:], D), ALU.mult).then_inc(done, 1)

                    def step(i, par):
                        for h in range(H):
                            if h == 0:
                                centre(i - 2, mean2, s.mean2, xc2, s.xc2)
                            if h == 1:
                                scaled(i + 2, var1, s.var1, rstd1, s.rstd1, xc1, z1, s.z1)
                            if h == 2 and live(i + 2):
                                e.wait_ge(s.z1, G(i + 3))
                                own_wait(e, c)
                                e.tensor_tensor(split(zw1[:]), split(z1[:]), mid(c.ln1_w[:, ds(l * D, D)], GB),
                                                ALU.mult).then_inc(s.zw1, 1)
                            if h == 3 and live(i + 2):
                                e.wait_ge(s.zw1, G(i + 3))
                                e.wait_ge(s.v, G(i + 1))
                                own_wait(e, c)
                                e.tensor_tensor(split(qf[:, par, :]), split(zw1[:]), mid(c.ln1_b[:, ds(l * D, D)], GB),
                                                ALU.add).then_inc(s.q, 1)
                            if h == 3 and live(i - 2):
                                e.wait_ge(s.z2_turned, G(i - 2))
                                scaled(i - 2, var2, s.var2, rstd2, s.rstd2, xc2, z2, s.z2)
                            if h == 5 and live(i - 2):
                                e.wait_ge(s.hi2, G(i - 1))
                                e.tensor_tensor(z16[:, :, 1, :], split(z2[:]), z16[:, :, 0, :],
                                                ALU.subtract).then_inc(s.lo2, 1)
                            if h == 5:
                                centre(i + 3, mean1, s.mean1, xc1, s.xc1)
                            if h == 5 and live(i + 2):
                                e.wait_ge(s.hi, G(i + 3))
                                e.tensor_tensor(q16[:, :, 1, :], split(qf[:, par, :]), q16[:, :, 0, :],
                                                ALU.subtract).then_inc(s.lo, 1)
                            if h == 6 and live(i - 1):
                                e.wait_ge(s.divided, G(i) * 2)
                                own_wait(e, c)
                                e.tensor_tensor(group(c.x, i - 1), group(c.x, i - 1), split(att[:]),
                                                ALU.add).then_inc(s.x_att, 1)

                    over_groups(e, step)

            @block.scalar
            def _(e):
                with e.Fori(0, LAYERS) as l:
                    G = lambda g: l * NG + g + LEAD

                    def exp(g, h):
                        if live(g):
                            if h % 2 == 0:
                                e.wait_ge(s.biased, G(g) * (H // 2) + h // 2 + 1)
                            else:
                                e.wait_ge(s.shifted, G(g) * H + h + 1)
                            e.wait_ge(s.weighed, G(g) * 4 - 2 + 2 * (h // 4))
                            e.activation(prob[:, h, :], score_ps[h % SBANKS][:] if h % 2 else biased[:, h // 2 % 2, :],
                                         ACT.Exp, scale=SCALE).then_inc(s.exped, 1)

                    def square(g, xc, ready, sq, done):
                        if live(g):
                            e.wait_ge(ready, G(g) + 1)
                            e.activation(sq[:], xc[:], ACT.Square, scale=1.0 / np.sqrt(D)).then_inc(done, 1)

                    def copy_out(g, half):
                        if live(g):
                            e.wait_ge(s.weighed, G(g) * 4 + 2 * half + 2)
                            e.wait_ge(s.back, G(g) * 2 - 1 + half)
                            e.activation(out_t[:, half, :], out_ps[:], ACT.Copy).then_inc(s.out_copied, 1)

                    def copy_stack(g, parity, n):
                        if live(g):
                            e.wait_ge(s.stacked, G(g) * 4 + n + 1)
                            e.activation((left, right)[n % 2][:, parity, n // 2, :], stack_ps[:],
                                         ACT.Copy).then_inc(s.stack_copied, 1)

                    def step(i, par):
                        for h in range(H):
                            if h % 2:
                                exp(i, h - 1)
                                exp(i, h)
                            if h == 0 and live(i + 1):
                                e.wait_ge(s.q_turned, G(i + 2))
                                e.activation(qt16[:], q_turn_ps, ACT.Copy).then_inc(s.q_copied, 1)
                            if h == 1:
                                square(i - 2, xc2, s.xc2, sq2, s.sq2)
                            if h == 2:
                                copy_stack(i + 1, 1 - par, 0)
                            if h == 3:
                                copy_stack(i + 1, 1 - par, 1)
                                copy_out(i - 1, 1)
                            if h == 4:
                                copy_stack(i + 1, 1 - par, 2)
                            if h == 4 and live(i + 2):
                                e.wait_ge(s.q, G(i + 3))
                                e.wait_ge(s.q_turned, G(i + 2))
                                e.activation(q16[:, :, 0, :], qf[:, par, :].rearrange("p (b d) -> p b d", d=D),
                                             ACT.Copy).then_inc(s.hi, 1)
                            if h == 4 and live(i - 2):
                                e.wait_ge(s.z2, G(i - 1))
                                e.wait_ge(s.z2_turned, G(i - 2))
                                e.activation(z16[:, :, 0, :], z2[:].rearrange("p (b d) -> p b d", d=D),
                                             ACT.Copy).then_inc(s.hi2, 1)
                            if h == 5:
                                copy_stack(i + 1, 1 - par, 3)
                            if h == 6 and live(i + 1):
                                e.wait_ge(s.weighed, G(i) * 4)
                                e.activation(c.v[:, 1 - par, :, 0:HD],
                                             qf[:, 1 - par, :].rearrange("p (n d) -> p n d", d=HD),
                                             ACT.Copy).then_inc(s.v, 1)
                            if h == 7 and live(i - 2):
                                e.wait_ge(s.z2_turned, G(i - 1))
                                own_wait(e, c)
                                e.activation(zt[:, ds((i - 2) * (GB * S), GB * S)], q_turn_ps,
                                             ACT.Copy).then_inc(s.zt_copied, 1)
                            if h == 7:
                                copy_out(i, 0)
                                square(i + 3, xc1, s.xc1, sq1, s.sq1)

                    over_groups(e, step)

                    def mlp(i, par, what):
                        if "a" in what:
                            for half in range(HALVES):
                                e.wait_ge(s.h_made, G(i) * 2 + half + 1)
                                e.wait_ge(s.y_made, G(i - 1))
                                e.activation(hid[:, par, half, :], h_ps(par, half)[:], ACT.Gelu,
                                             bias=b1g[:, half:half + 1], scale=1.0 / W1_UP).then_inc(s.gelued, 1)
                        if "b" in what:
                            e.wait_ge(s.y_made, G(i))
                            e.wait_ge(s.y_back, G(i - 2))
                            e.activation(y_t[:, 1 - par, :], y_ps(1 - par)[:, 0:NPAIR2 * S], ACT.Identity,
                                         bias=B2).then_inc(s.y_copied, 1)

                    over_mlp_groups(e, mlp)

            @block.tensor
            def _(e):
                with e.Fori(0, LAYERS) as l:
                    G = lambda g: l * NG + g + LEAD

                    def score(g, parity, h):
                        if not live(g):
                            return
                        if h % 4 == 0:
                            e.wait_ge(s.stack_copied, G(g) * 4 + 2 + h // 2)
                        if isinstance(g, int) and g == 0 and h == 0:
                            e.wait_ge(s.gelued, G(0) * 2)
                        if h % 2:
                            e.wait_ge(s.exped, G(g) * H + h - SBANKS + 1)
                        else:
                            e.wait_ge(s.biased, G(g) * (H // 2) + h // 2 - 1)
                        j = h % 4
                        for b in range(GB):
                            mm = e.matmul(score_ps[h % SBANKS][:, b * S:(b + 1) * S],
                                          left[QROWS * j:QROWS * (j + 1), parity, h // 4, b * S:(b + 1) * S],
                                          right[QROWS * j:QROWS * (j + 1), parity, h // 4, b * S:(b + 1) * S],
                                          start=b == 0, stop=False, skip_group_check=True)
                        mm.then_inc(s.scored, 1)

                    def shift(g, h):
                        if live(g):
                            e.wait_ge(s.maxed, G(g) * H + h + 1)
                            for b in range(GB):
                                mm = e.matmul(score_ps[h % SBANKS][:, b * S:(b + 1) * S],
                                              mx[:, h % SBANKS, b:b + 1].broadcast_to([P, S]), c.neg_ident[:],
                                              start=False, stop=h % 2 == 0, skip_group_check=True)
                            if h % 2:
                                for part in range(2):
                                    mm = e.matmul(score_ps[h % SBANKS][:].rearrange("p (b t) -> p b t", t=S),
                                                  c.ident16[:], mid(c.bias16[:, part, h // 2, :], GB),
                                                  start=False, stop=part == 1, skip_group_check=True)
                            mm.then_inc(s.shifted, 1)

                    def weigh(g, parity, half, batches):
                        if not live(g):
                            return
                        if batches[0] == 0:
                            e.wait_ge(s.exped, G(g) * H + 4 * half + 4)
                            e.wait_ge(s.out_copied, G(g) * 2 + half)
                            if half == 0:
                                e.wait_ge(s.v, G(g) + 1)
                            if isinstance(g, int) and g == 0 and half == 0:
                                e.wait_ge(c.x_ready, l * NG + NG)
                        for b in batches:
                            for j in range(4):
                                h = 4 * half + j
                                mm = e.matmul(out_ps[QROWS * j:QROWS * (j + 1), b * S:(b + 1) * S],
                                              c.v[:, parity, b * H + h, :], prob[:, h, b * S:(b + 1) * S],
                                              start=True, stop=True)
                        mm.then_inc(s.weighed, 1)

                    def back(g, half):
                        if live(g):
                            e.wait_ge(s.out_copied, G(g) * 2 + half + 1)
                            e.wait_ge(s.divided, G(g) * 2 + half)
                            if isinstance(g, int) and g == 0 and half == 0:
                                e.wait_ge(s.w_gained, l * 3 + 1)
                            for b in range(GB):
                                mm = e.transpose(back_ps[:, b * S:(b + 1) * S], out_t[:, half, b * S:(b + 1) * S],
                                                 c.ident[:])
                            mm.then_inc(s.back, 1)

                    def stack(g, n):
                        if live(g):
                            if n == 0:
                                e.wait_ge(s.q_copied, G(g) + 1)
                            e.wait_ge(s.stack_copied, G(g) * 4 + n)
                            e.matmul(stack_ps[:], c.sel[:, 2 * (n % 2) + n // 2, :], qt16[:],
                                     start=True, stop=True).then_inc(s.stacked, 1)

                    def step(i, par):
                        for h in range(H):
                            shift(i + (h + 1) // H, (h + 1) % H)
                            score(i + (h + 3) // H, par if h + 3 < H else 1 - par, (h + 3) % H)
                            if h == 0:
                                back(i - 1, 0)
                            if h in (1, 2):
                                weigh(i - 1, 1 - par, 1, (0, 1) if h == 1 else (2, 3))
                            if 1 <= h <= 4:
                                stack(i + 1, h - 1)
                            if h == 4:
                                back(i - 1, 1)
                            if h == 0 and isinstance(i, int) and i == 0:
                                e.wait_ge(s.w_loaded, l * 16 + 16)
                                e.wait_ge(c.x_ready, l * NG + NG)
                                for half in range(HALVES):
                                    mm = e.matmul(back_ps[:, half:half + 1], W1[:, half * P:(half + 1) * P], LN2_B,
                                                  start=True, stop=True)
                                mm.then_inc(s.offset, 1)
                            if h == 6 and live(i - 2):
                                e.wait_ge(s.lo2, G(i - 1))
                                e.wait_ge(s.q_copied, G(i + 1) if live(i + 1) else G(NG))
                                for b in range(GB):
                                    mm = e.transpose(q_turn_ps[:, b * S:(b + 1) * S],
                                                     z16[:, b].rearrange("p a d -> p (a d)"), c.ident16[:])
                                mm.then_inc(s.z2_turned, 1)
                            if h in (5, 6):
                                weigh(i, par, 0, (0, 1) if h == 5 else (2, 3))
                            if h == 7 and live(i + 2):
                                e.wait_ge(s.lo, G(i + 3))
                                e.wait_ge(s.q_copied, G(i + 2))
                                e.wait_ge(s.zt_copied, G(i - 1) if live(i - 2) else G(0))
                                if isinstance(i, int) and i == -2:
                                    e.wait_ge(s.y_copied, G(0))
                                for b in range(GB):
                                    mm = e.transpose(q_turn_ps[:, b * S:(b + 1) * S],
                                                     q16[:, b].rearrange("p a d -> p (a d)"), c.ident16[:])
                                mm.then_inc(s.q_turned, 1)

                    over_groups(e, step)

                    def mlp(i, par, what):
                        if "a" in what:
                            if isinstance(i, int) and i == 0:
                                e.wait_ge(s.w_split, l + 1)
                                e.wait_ge(s.zt_copied, G(NG))
                                e.wait_ge(s.exped, G(NG) * H)
                            for half in range(HALVES):
                                e.wait_ge(s.gelued, G(i) * 2 - 3 + half)
                                for part in range(2):
                                    mm = e.matmul(h_ps(par, half)[:], w1_parts[:, part, half * P:(half + 1) * P],
                                                  zt[:, ds(i * (GB * S), GB * S)], start=part == 0, stop=part == 1)
                                mm.then_inc(s.h_made, 1)
                        if "b" in what:
                            e.wait_ge(s.gelued, G(i) * 2)
                            e.wait_ge(s.y_copied, G(i - 2))
                            if isinstance(i, int) and i < 3:
                                e.wait_ge(s.out_copied, G(NG) * 2)
                            for half in range(HALVES):
                                for q in range(2):
                                    mm = e.matmul(
                                        y_ps(1 - par)[q * D:(q + 1) * D, 0:NPAIR2 * S].rearrange("p (a t) -> p a t", t=S),
                                        W2(half), of_parity(hid[:, 1 - par, half, :], q),
                                                  start=half == 0, stop=half == HALVES - 1)
                            mm.then_inc(s.y_made, 1)
                        if "c" in what:
                            e.wait_ge(s.y_copied, G(i - 1))
                            e.wait_ge(c.x_ready, l * NG + (i - 3 + NG))
                            if isinstance(i, int) and i < 4:
                                e.wait_ge(s.divided, G(NG) * 2)
                            for q in range(NPAIR2):
                                mm = e.transpose(yb_ps(par)[:, q * S:(q + 1) * S], y_t[:, par, q * S:(q + 1) * S],
                                                 c.ident[:])
                            mm.then_inc(s.y_back, 1)

                    over_mlp_groups(e, mlp)


NB_CHUNK = 16
CC = NB_CHUNK * D
CHUNKS = B // NB_CHUNK
CP = NB_CHUNK // 2
EXPERTS = 8


def normalise(nc, c, tag, src, affine=None, dst=None, turned=None, logits=None, split_parts=False):
    with ExitStack() as ctx:
        sb = lambda n, s, d=F32: ctx.enter_context(nc.sbuf_tensor(tag + n, s, d))
        ps = lambda n, s, d=F32: ctx.enter_context(nc.psum_tensor(tag + n, s, d))
        sem = lambda n: ctx.enter_context(nc.semaphore(tag + n))
        chunk = lambda t, k: t[:, ds(k * CC, CC)].rearrange("p (b d) -> p b d", d=D)
        split = lambda t: t.rearrange("p (b d) -> p b d", d=D)
        total, mean, sqtotal, var, rstd = (sb(n, [P, 2, NB_CHUNK]) for n in ("total", "mean", "sqtotal", "var", "rstd"))
        xc, sq, z = (sb(n, [P, 2, CC]) for n in ("xc", "sq", "z"))
        z16 = sb("z16", [P, 2, NB_CHUNK, 2, D], F16) if split_parts else None
        stage = sb("stage", [P, 2, CC]) if logits else None
        turn_ps = ps("turn", [P, 4, BANK])
        logit_ps = ps("logit", [P, 2, BANK]) if logits else None
        names = ["s_total", "s_mean", "s_xc", "s_sq", "s_sqtotal", "s_var", "s_rstd", "s_z"]
        names += ["s_zw"] if affine else []
        names += ["s_out"] if dst is not None else []
        names += ["s_turned", "s_staged"] if turned is not None or logits else []
        names += ["s_hi", "s_lo"] if split_parts else []
        names += ["s_logits", "s_added"] if logits else []
        sems = {n: sem(n) for n in names}
        s = type("Sems", (), sems)
        done = s.s_out if dst is not None else s.s_z

        def over_chunks(e, step):
            with e.Fori(0, CHUNKS // 2) as j:
                step(j * 2, 0)
                step(j * 2 + 1, 1)

        with nc.Block() as block:
            @block.vector
            def _(e):
                def first(k, par):
                    e.tensor_reduce(total[:, par], chunk(src, k), AX.X, ALU.add).then_inc(s.s_total, 1)
                    e.wait_ge(s.s_total, k + 1)
                    e.tensor_scalar(mean[:, par], total[:, par], -1.0 / D, None, ALU.mult).then_inc(s.s_mean, 1)
                    e.wait_ge(s.s_mean, k + 1)
                    e.tensor_tensor(split(xc[:, par]), chunk(src, k), bcast(mean[:, par], D), ALU.add).then_inc(s.s_xc, 1)

                def second(k, par):
                    e.wait_ge(s.s_sq, k + 1)
                    e.tensor_reduce(sqtotal[:, par], split(sq[:, par]), AX.X, ALU.add).then_inc(s.s_sqtotal, 1)
                    e.wait_ge(s.s_sqtotal, k + 1)
                    e.tensor_scalar(var[:, par], sqtotal[:, par], EPS, None, ALU.add).then_inc(s.s_var, 1)

                def third(k, par):
                    e.wait_ge(s.s_z, k + 1)
                    if affine:
                        e.tensor_tensor(split(z[:, par]), split(z[:, par]), mid(affine[0][:], NB_CHUNK),
                                        ALU.mult).then_inc(s.s_zw, 1)
                        e.wait_ge(s.s_zw, k + 1)
                        e.tensor_tensor(chunk(dst, k), split(z[:, par]), mid(affine[1][:], NB_CHUNK),
                                        ALU.add).then_inc(s.s_out, 1)
                    elif dst is not None:
                        e.tensor_copy(chunk(dst, k), split(z[:, par])).then_inc(s.s_out, 1)

                def both(j):
                    first(j * 2, 0)
                    first(j * 2 + 1, 1)
                    second(j * 2, 0)
                    second(j * 2 + 1, 1)
                    third(j * 2, 0)
                    third(j * 2 + 1, 1)
                    for k, par in ((j * 2, 0), (j * 2 + 1, 1)):
                        if logits:
                            w, bias, out = logits
                            e.wait_ge(s.s_logits, k + 1)
                            e.tensor_tensor(out[:, ds(k * NB_CHUNK * EXPERTS, NB_CHUNK * EXPERTS)].rearrange(
                                "p (b e) -> p b e", e=EXPERTS),
                                logit_ps[:, par, 0:NB_CHUNK * EXPERTS].rearrange("p (b e) -> p b e", e=EXPERTS),
                                mid(bias[:], NB_CHUNK), ALU.add).then_inc(s.s_added, 1)
                    e.wait_ge(done, j * 2 + 2)

                with e.Fori(0, CHUNKS // 2) as j:
                    both(j)

            @block.gpsimd
            def _(e):
                def step(k, par):
                    e.wait_ge(s.s_var, k + 1)
                    e.tensor_tensor(rstd[:, par], var[:, par], c.minus_half[:], ALU.pow).then_inc(s.s_rstd, 1)
                    e.wait_ge(s.s_rstd, k + 1)
                    if turned is not None or logits:
                        e.wait_ge(s.s_turned, k * 1 if isinstance(k, int) else k - par)
                    if affine or dst is not None:
                        e.wait_ge(s.s_out, k - par)
                    e.tensor_tensor(split(z[:, par]), split(xc[:, par]), bcast(rstd[:, par], D),
                                    ALU.mult).then_inc(s.s_z, 1)
                    if split_parts:
                        e.wait_ge(s.s_hi, k + 1)
                        e.tensor_tensor(z16[:, par, :, 1, :], split(z[:, par]), z16[:, par, :, 0, :],
                                        ALU.subtract).then_inc(s.s_lo, 1)

                over_chunks(e, step)

            @block.scalar
            def _(e):
                def step(k, par):
                    e.wait_ge(s.s_xc, k + 1)
                    e.activation(sq[:, par], xc[:, par], ACT.Square, scale=1.0 / np.sqrt(D)).then_inc(s.s_sq, 1)

                def copy(k, par):
                    if split_parts:
                        e.wait_ge(s.s_turned, k + 1)
                        own_wait(e, c)
                        e.activation(turned[:, ds(k * (2 * CC), 2 * CC)],
                                     turn_ps[:, 2 * par:2 * par + 2, :].rearrange("p a b -> p (a b)").bitcast(F16),
                                     ACT.Copy).then_inc(s.s_staged, 1)
                    elif turned is not None:
                        e.wait_ge(s.s_turned, k + 1)
                        own_wait(e, c)
                        e.activation(turned[:, ds(k * CC, CC)],
                                     turn_ps[:, 2 * par:2 * par + 2, :].rearrange("p a b -> p (a b)"),
                                     ACT.Copy).then_inc(s.s_staged, 1)
                    elif logits:
                        e.wait_ge(s.s_turned, k + 1)
                        e.wait_ge(s.s_logits, k - par)
                        e.activation(stage[:, par], turn_ps[:, 2 * par:2 * par + 2, :].rearrange("p a b -> p (a b)"),
                                     ACT.Copy).then_inc(s.s_staged, 1)

                def rounded(k, par):
                    if split_parts:
                        e.wait_ge(s.s_z, k + 1)
                        e.wait_ge(s.s_turned, k - par)
                        e.activation(z16[:, par, :, 0, :], split(z[:, par]), ACT.Copy).then_inc(s.s_hi, 1)

                with e.Fori(0, CHUNKS // 2) as j:
                    step(j * 2, 0)
                    step(j * 2 + 1, 1)
                    rounded(j * 2, 0)
                    rounded(j * 2 + 1, 1)
                    copy(j * 2, 0)
                    copy(j * 2 + 1, 1)

            @block.tensor
            def _(e):
                if turned is None and not logits:
                    return

                def step(k, par):
                    e.wait_ge(s.s_lo if split_parts else s.s_z, k + 1)
                    e.wait_ge(s.s_staged, k - par)
                    for b in range(NB_CHUNK if split_parts else 0):
                        mm = e.transpose(turn_ps[:, 2 * par + b // 8, (b % 8) * D:(b % 8 + 1) * D].bitcast(F16),
                                         z16[:, par, b].rearrange("p a d -> p (a d)"), c.ident16[:])
                    for q in range(0 if split_parts else CP):
                        mm = e.transpose(turn_ps[:, 2 * par + q // 4, (q % 4) * P:(q % 4 + 1) * P],
                                         z[:, par, q * P:(q + 1) * P], c.ident[:])
                    mm.then_inc(s.s_turned, 1)

                def product(k, par):
                    e.wait_ge(s.s_staged, k + 1)
                    e.wait_ge(s.s_added, k - par)
                    for q in range(CP):
                        mm = e.matmul(logit_ps[:, par, q * 2 * EXPERTS:(q + 1) * 2 * EXPERTS],
                                      stage[:, par, q * P:(q + 1) * P], logits[0][:], start=True, stop=True)
                    mm.then_inc(s.s_logits, 1)

                with e.Fori(0, CHUNKS // 2) as j:
                    step(j * 2, 0)
                    step(j * 2 + 1, 1)
                    if logits:
                        product(j * 2, 0)
                        product(j * 2 + 1, 1)


AH, AHD = 4, 16
SB = 8
SETS = B // SB
SPAIRS = SB * AH
ITERATIONS = 5
SLOTS = 2 * ITERATIONS + 1


def sinkhorn(nc, c, a):
    with ExitStack() as ctx:
        sb = lambda n, s, d=F32: ctx.enter_context(nc.sbuf_tensor("a_" + n, s, d))
        ps = lambda n, s, d=F32: ctx.enter_context(nc.psum_tensor("a_" + n, s, d))
        sem = lambda n: ctx.enter_context(nc.semaphore("a_" + n))
        w = sb("w", [P, 3 * D])
        head = sb("head", [P, 4, AH])
        cosv, sinv, gate, t1, t2, t3 = (sb(n, [P, AH]) for n in ("cos", "sin", "gate", "t1", "t2", "t3"))
        a1, a2, a3 = (sb(n, [P, AH]) for n in ("a1", "a2", "a3"))
        mixk = sb("mixk", [P, D])
        mixq = sb("mixq", [P, D])
        wu, wm = (sb(n, [P, 2, P]) for n in ("wu", "wm"))
        wv = sb("wv", [P, 2, D])
        wproj = sb("wproj", [P, 2, D])
        bproj = sb("bproj", [P, D])
        zset = sb("zset", [P, SB // 2 * S])
        ut, mt = (sb(n, [P, 2, SB // 2 * S]) for n in ("ut", "mt"))
        val = sb("val", [P, 2, SB, AH, AHD])
        valb = sb("valb", [P, SB, AH, QROWS])
        rmax, cmax = (sb(n, [P, 2, 4], BF16) for n in ("rmax", "cmax"))
        half_xt = lambda n: c.xt[:, n * (SPAIRS * S):(n + 1) * (SPAIRS * S)].rearrange(
            "p (h b t) -> p h b t", h=AH, b=SB)
        k_ij = (sb("k_ij", [P, AH, SB, S])[:], half_xt(0))
        k_ji = (sb("k_ji", [P, AH, SB, S])[:], half_xt(1))
        ub, vb = (sb(n, [P, AH, SB, QROWS]) for n in ("ub", "vb"))
        rows = sb("rows", [P, S])
        kv, ku, u, v, prod, inv, alpha, beta = (sb(n, [P, AH, SB]) for n in
                                                ("kv", "ku", "u", "v", "prod", "inv", "alpha", "beta"))
        minus_half = sb("mh", [P, AH, SB])
        out_t = sb("out_t", [P, SB * S])
        att = sb("att", [P, SB, D])
        att_t = sb("att_t", [P, SB // 2 * S])
        res = sb("res", [P, SB, D])
        bank = [ps(f"bank{i}", [P, BANK]) for i in range(8)]
        names = ("loaded", "const", "coef", "mixed", "trig", "sig", "wready", "zset", "ut_ps", "ut", "val_ps", "val",
                 "scored", "rmaxed", "rowed", "cmaxed", "coled", "exped", "summed", "rows", "turned", "factor",
                 "pool", "valb", "out_ps", "out_t", "back", "att", "att_ps", "att_t", "proj", "res", "x", "fin")
        sems = {n: sem("a_" + n) for n in names}
        s = type("Sems", (), sems)
        UNITS = 2 * AH
        per_set = {"zset": 1, "ut_ps": 4, "ut": 4, "val_ps": 1, "val": 1, "scored": UNITS, "rmaxed": UNITS,
                   "rowed": UNITS, "cmaxed": UNITS, "coled": UNITS, "exped": UNITS, "summed": SLOTS, "rows": SLOTS,
                   "turned": SLOTS, "factor": SLOTS - 1, "pool": 6, "valb": 1, "out_ps": 1, "out_t": 2, "back": 2,
                   "att": 2, "att_ps": 1, "att_t": 1, "proj": 1, "res": 1, "x": 1, "fin": 1}
        G = lambda k: k + LEAD
        live = lambda k: not isinstance(k, int) or 0 <= k < SETS

        def diag(t):
            return t[:].rearrange("p h b r -> p h (b r)")[:, :, 0:(SB - 1) * (QROWS + 1) + 1:QROWS + 1]
        heads3 = lambda t: t[:].rearrange("p (h d) -> p h d", d=AHD)

        def over_rounds(e, step):
            step(-1, 1)
            step(0, 0)
            with e.Fori(0, (SETS - 4) // 2) as j:
                step(j * 2 + 1, 1)
                step(j * 2 + 2, 0)
            for k in range(SETS - 3, SETS + 1):
                step(k, k % 2)

        with nc.Block() as block:
            @block.sync
            def _(e):
                loads = [(w[0:D, :], a["L0_attn_W_qkv"]), (w[D:P, :], a["L0_attn_W_qkv"]),
                         (wproj[0:D, 0, :], a["L0_attn_W_proj"]), (wproj[D:P, 1, :], a["L0_attn_W_proj"]),
                         (bproj[:], a["L0_attn_b_proj"].partition_broadcast(P))]
                for n, name in enumerate(("phase", "ent", "gate")):
                    loads.append((head[:, n, :], a["L0_attn_" + name].partition_broadcast(P)))
                for h in range(AH):
                    loads.append((head[:, 3, h:h + 1], a["L0_attn_tau"].partition_broadcast(P)))
                e.wait_ge(s.const, 1)
                for dst, src in loads:
                    e.dma_start(dst, src).then_inc(s.loaded, 16)

            @block.gpsimd
            def _(e):
                e.memset(wproj[:], 0.0).then_inc(s.const, 1)
                e.memset(minus_half[:], -0.5)
                for t in (wu, wm, wv, valb, ub, vb):
                    ins = e.memset(t[:], 0.0)
                ins.then_inc(s.const, 1)
                for n, count in per_set.items():
                    e.sem_inc(sems[n], LEAD * count)

            @block.scalar
            def _(e):
                e.wait_ge(s.loaded, 16 * 12)
                e.wait_ge(s.coef, 1)
                e.activation(cosv[:], t2[:], ACT.Sin).then_inc(s.trig, 1)
                e.activation(sinv[:], t1[:], ACT.Sin).then_inc(s.trig, 1)
                e.activation(gate[:], head[:, 2, :], ACT.Sigmoid).then_inc(s.sig, 1)

            @block.vector
            def _(e):
                n = [0]

                def chain(ins):
                    n[0] += 1
                    ins.then_inc(s.mixed, 1)
                    e.wait_ge(s.mixed, n[0])

                e.wait_ge(s.loaded, 16 * 12)
                two_pi = float(2 * np.pi)
                chain(e.tensor_scalar(t3[:], head[:, 0, :], 1.0 / two_pi, 12582912.0, ALU.mult, ALU.add))
                chain(e.tensor_scalar(t3[:], t3[:], -12582912.0, None, ALU.add))
                chain(e.tensor_scalar(t1[:], t3[:], -6.28125, None, ALU.mult))
                chain(e.tensor_tensor(t1[:], t1[:], head[:, 0, :], ALU.add))
                chain(e.tensor_scalar(t3[:], t3[:], -(two_pi - 6.28125), None, ALU.mult))
                chain(e.tensor_tensor(t1[:], t1[:], t3[:], ALU.add))
                chain(e.tensor_scalar(t1[:], t1[:], float(np.float32(3.1415925)), float(-np.float32(3.1415925)),
                                      ALU.min, ALU.max))
                chain(e.tensor_scalar(t2[:], t1[:], -1.0, None, ALU.mult))
                chain(e.tensor_tensor(t2[:], t2[:], t1[:], ALU.max))
                e.tensor_scalar(t2[:], t2[:], -1.0, float(np.pi / 2), ALU.mult, ALU.add).then_inc(s.coef, 1)
                e.wait_ge(s.trig, 2)
                e.wait_ge(s.sig, 1)
                scale = float(AHD) ** -0.5
                chain(e.tensor_tensor(t1[:], cosv[:], sinv[:], ALU.add))
                chain(e.tensor_scalar(t1[:], t1[:], 0.5, None, ALU.mult))
                chain(e.tensor_tensor(t1[:], t1[:], gate[:], ALU.mult))
                chain(e.tensor_scalar(t2[:], gate[:], -1.0, 1.0, ALU.mult, ALU.add))
                chain(e.tensor_tensor(t1[:], t1[:], t2[:], ALU.add))
                chain(e.reciprocal(t3[:], head[:, 3, :]))
                chain(e.tensor_scalar(t1[:], t1[:], scale, None, ALU.mult))
                chain(e.tensor_tensor(a1[:], t1[:], t3[:], ALU.mult))
                chain(e.tensor_tensor(t1[:], cosv[:], sinv[:], ALU.subtract))
                chain(e.tensor_tensor(t1[:], t1[:], gate[:], ALU.mult))
                chain(e.tensor_scalar(t1[:], t1[:], 0.5 * scale, None, ALU.mult))
                chain(e.tensor_tensor(a2[:], t1[:], t3[:], ALU.mult))
                chain(e.tensor_tensor(t1[:], gate[:], head[:, 1, :], ALU.mult))
                chain(e.tensor_scalar(t1[:], t1[:], 0.1, None, ALU.mult))
                chain(e.tensor_tensor(a3[:], t1[:], t3[:], ALU.mult))
                wq, wk = w[:, 0:D].rearrange("p (h d) -> p h d", d=AHD), w[:, D:2 * D].rearrange("p (h d) -> p h d", d=AHD)
                chain(e.tensor_tensor(heads3(mixk), wk, bcast(a1[:], AHD), ALU.mult))
                chain(e.tensor_tensor(heads3(mixq), wq, bcast(a3[:], AHD), ALU.mult))
                chain(e.tensor_tensor(mixk[:], mixk[:], mixq[:], ALU.add))
                chain(e.tensor_tensor(heads3(mixq), wq, bcast(a2[:], AHD), ALU.mult))
                e.wait_ge(s.const, 2)
                for par in range(2):
                    rws = slice(par * D, (par + 1) * D)
                    for t, lo, hi in ((wu, wq[rws], wk[rws]), (wm, heads3(mixk)[rws], heads3(mixq)[rws])):
                        o = t[rws, par, :].rearrange("p (h two d) -> p h two d", two=2, d=AHD)
                        e.tensor_copy(o[:, :, 0, :], lo)
                        e.tensor_copy(o[:, :, 1, :], hi)
                    ins = e.tensor_copy(wv[rws, par, :], w[rws, 2 * D:3 * D])
                ins.then_inc(s.wready, 1)

        with nc.Block() as block:
            @block.gpsimd
            def _(e):
                def step(k, par):
                    if live(k - 1):
                        e.wait_ge(s.fin, G(k))
                        for n, (f, other) in enumerate(((u, kv), (v, ku))):
                            e.tensor_tensor(prod[:], f[:], other[:], ALU.mult).then_inc(s.pool, 1)
                            e.wait_ge(s.pool, G(k - 1) * 6 + n * 3 + 1)
                            e.tensor_tensor(inv[:], prod[:], minus_half[:], ALU.pow).then_inc(s.pool, 1)
                            e.wait_ge(s.pool, G(k - 1) * 6 + n * 3 + 2)
                            e.tensor_tensor((alpha, beta)[n][:], f[:], inv[:], ALU.mult).then_inc(s.pool, 1)
                            e.wait_ge(s.pool, G(k - 1) * 6 + n * 3 + 3)
                        e.wait_ge(s.out_ps, G(k - 1))
                        e.wait_ge(s.val, G(k))
                        for h in range(AH):
                            ins = e.tensor_tensor(valb[:, :, h, 0:AHD], val[:, 1 - par, :, h, :],
                                                  bcast(beta[:, h, :], AHD), ALU.mult)
                        ins.then_inc(s.valb, 1)
                        e.wait_ge(s.res, G(k))
                        own_wait(e, c)
                        xs = c.x[:, ds((k - 1) * (SB * D), SB * D)].rearrange("p (b d) -> p b d", d=D)
                        e.tensor_tensor(xs, xs, res[:], ALU.add).then_inc(s.x, 1)

                over_rounds(e, step)

            @block.scalar
            def _(e):
                def load_set(k):
                    if live(k):
                        e.wait_ge(s.val_ps, G(k))
                        own_wait(e, c)
                        e.activation(zset[:], c.zt[:, ds(k * (SB // 2 * S), SB // 2 * S)], ACT.Copy).then_inc(s.zset, 1)

                def exp(k, parity, n):
                    if live(k) and 0 <= n < UNITS:
                        h, half = n // 2, n % 2
                        e.wait_ge(s.coled, G(k) * UNITS + n + 1)
                        if n == 0:
                            e.wait_ge(s.out_ps, G(k - 1))
                        for m, t in enumerate((k_ij, k_ji)):
                            ins = e.activation(t[parity][:, h, 4 * half:4 * half + 4, :].rearrange("p b t -> p (b t)"),
                                               bank[2 * (n % 2) + m][:], ACT.Exp)
                        ins.then_inc(s.exped, 1)

                load_set(0)

                def step(k, par):
                    for t in range(SLOTS):
                        exp(k + 1, 1 - par, t - 3)
                        if live(k):
                            e.wait_ge(s.summed, G(k) * SLOTS + t + 1)
                            e.activation(rows[:], bank[6][:, 0:S], ACT.Copy).then_inc(s.rows, 1)
                        if t == 0 and live(k + 1):
                            for n, (dst, m) in enumerate(((ut, 0), (ut, 1), (mt, 0), (mt, 1))):
                                e.wait_ge(s.ut_ps, G(k + 1) * 4 + n + 1)
                                e.activation(dst[:, m], bank[n][:], ACT.Copy).then_inc(s.ut, 1)
                        if t == 2 and live(k - 1):
                            e.wait_ge(s.out_ps, G(k))
                            for n in range(2):
                                e.activation(out_t[:, n * BANK:(n + 1) * BANK], bank[4 + n][:],
                                             ACT.Copy).then_inc(s.out_t, 1)
                        if t == 4 and live(k - 1):
                            e.wait_ge(s.att_ps, G(k))
                            e.activation(att_t[:], bank[4][:], ACT.Copy).then_inc(s.att_t, 1)
                        if t == 6 and live(k + 1):
                            e.wait_ge(s.val_ps, G(k + 2))
                            e.wait_ge(s.valb, G(k))
                            e.activation(val[:, 1 - par].rearrange("p b h d -> p (b h d)"), bank[4][:],
                                         ACT.Copy).then_inc(s.val, 1)
                        if t == 8:
                            load_set(k + 2)

                over_rounds(e, step)

            @block.vector
            def _(e):
                def largest(k, n, ready, b, out, done):
                    if live(k) and 0 <= n < UNITS:
                        e.wait_ge(ready, G(k) * UNITS + n + 1)
                        e.tensor_reduce(out[:, n % 2], bank[b + 2 * (n % 2)][:].rearrange("p (b t) -> p b t", t=S),
                                        AX.X, ALU.max).then_inc(done, 1)

                def step(k, par):
                    sums = bank[7][:, 0:P].rearrange("p (h r) -> p h r", h=AH)[:, :, 0:SB]
                    for t in range(SLOTS):
                        largest(k + 1, t - 2, s.scored, 0, rmax, s.rmaxed)
                        if live(k):
                            e.wait_ge(s.turned, G(k) * SLOTS + t + 1)
                            if t == SLOTS - 3:
                                e.wait_ge(s.pool, G(k) * 6)
                            if t == SLOTS - 3:
                                e.reciprocal(u[:], sums)
                            elif t == SLOTS - 2:
                                e.reciprocal(v[:], sums)
                                e.tensor_copy(ku[:], sums)
                            elif t == SLOTS - 1:
                                e.tensor_copy(kv[:], sums).then_inc(s.fin, 1)
                            if t < SLOTS - 1:
                                e.reciprocal(diag((ub, vb)[t % 2]), sums).then_inc(s.factor, 1)
                        largest(k + 1, t - 2, s.rowed, 1, cmax, s.cmaxed)
                        if t == 3 and live(k - 1):
                            for n in range(2):
                                e.wait_ge(s.back, G(k - 1) * 2 + n + 1)
                                e.tensor_tensor(
                                    att[:, 4 * n:4 * n + 4, :].rearrange("p b (h d) -> p b h d", d=AHD),
                                    bank[4 + n][:].rearrange("p (b h r) -> p b h r", h=AH, r=QROWS)[:, :, :, 0:AHD],
                                    alpha[:, :, 4 * n:4 * n + 4].rearrange("p h b -> p b h").unsqueeze(3)
                                    .broadcast_to([P, 4, AH, AHD]), ALU.mult).then_inc(s.att, 1)
                        if t == 5 and live(k - 1):
                            e.wait_ge(s.proj, G(k))
                            e.wait_ge(s.x, G(k - 1))
                            e.tensor_tensor(res[:], bank[5][:].rearrange("p (b d) -> p b d", d=D), mid(bproj[:], SB),
                                            ALU.add).then_inc(s.res, 1)

                over_rounds(e, step)

            @block.tensor
            def _(e):
                def score(k, n):
                    if live(k) and 0 <= n < UNITS:
                        if n == 0:
                            e.wait_ge(s.ut, G(k) * 4 + 4)
                        e.wait_ge(s.exped, G(k) * UNITS + n - 1)
                        rws = slice(QROWS * (n // 2), QROWS * (n // 2 + 1))
                        ij, ji = bank[2 * (n % 2)], bank[2 * (n % 2) + 1]
                        for i in range(4):
                            b = 4 * (n % 2) + i
                            at = slice((b // 2) * S, (b // 2 + 1) * S)
                            e.matmul(ij[:, i * S:(i + 1) * S], ut[rws, b % 2, at], mt[rws, b % 2, at],
                                     start=i == 0, stop=False, skip_group_check=True)
                            mm = e.matmul(ji[:, i * S:(i + 1) * S], mt[rws, b % 2, at], ut[rws, b % 2, at],
                                          start=i == 0, stop=False, skip_group_check=True)
                        mm.then_inc(s.scored, 1)

                def shift(k, n, m, ready, swap, done):
                    if live(k) and 0 <= n < UNITS:
                        e.wait_ge(ready, G(k) * UNITS + n + 1)
                        along, across = bank[2 * (n % 2) + swap], bank[2 * (n % 2) + 1 - swap]
                        e.matmul(along[:], c.neg_ident[:], bcast(m[:, n % 2], S), start=False, stop=False,
                                 skip_group_check=True)
                        for i in range(4):
                            mm = e.matmul(across[:, i * S:(i + 1) * S], m[:, n % 2, i:i + 1].broadcast_to([P, S]),
                                          c.neg_ident[:], start=False, stop=True, skip_group_check=True)
                        mm.then_inc(done, 1)

                def step(k, par):
                    for t in range(SLOTS):
                        shift(k + 1, t - 3, cmax, s.cmaxed, 1, s.coled)
                        if live(k):
                            if t > 0:
                                e.wait_ge(s.factor, G(k) * (SLOTS - 1) + t)
                            else:
                                e.wait_ge(s.exped, G(k + 1) * UNITS)
                            e.wait_ge(s.rows, G(k) * SLOTS + t)
                            kern = (k_ji, k_ij)[t % 2][par]
                            for b in range(SB):
                                for h in range(AH):
                                    lhs = c.diag_ones[:, b, :] if t == 0 else (vb, ub)[t % 2][:, h, b, :]
                                    mm = e.matmul(bank[6][QROWS * h:QROWS * (h + 1), 0:S], lhs, kern[:, h, b, :],
                                                  start=b == 0, stop=b == SB - 1, skip_group_check=True)
                            mm.then_inc(s.summed, 1)
                        shift(k + 1, t - 2, rmax, s.rmaxed, 0, s.rowed)
                        if t == 0 and live(k + 1):
                            e.wait_ge(s.zset, G(k + 2))
                            e.wait_ge(s.exped, G(k + 1) * UNITS)
                            for n, (wt, m) in enumerate(((wu, 0), (wu, 1), (wm, 0), (wm, 1))):
                                e.matmul(bank[n][:], wt[:, m, :], zset[:], start=True, stop=True).then_inc(s.ut_ps, 1)
                        if t == 2 and live(k - 1):
                            e.wait_ge(s.valb, G(k))
                            e.wait_ge(s.val, G(k + 1) if live(k + 1) or live(k) else G(k))
                            for b in range(SB):
                                for h in range(AH):
                                    mm = e.matmul(
                                        bank[4 + b // 4][QROWS * h:QROWS * (h + 1), (b % 4) * S:(b % 4 + 1) * S],
                                        valb[:, b, h, :], k_ji[1 - par][:, h, b, :], start=True, stop=True)
                            mm.then_inc(s.out_ps, 1)
                        if t == 3 and live(k - 1):
                            for n in range(2):
                                e.wait_ge(s.out_t, G(k - 1) * 2 + n + 1)
                                for b in range(4):
                                    mm = e.transpose(bank[4 + n][:, b * S:(b + 1) * S],
                                                     out_t[:, (4 * n + b) * S:(4 * n + b + 1) * S], c.ident[:])
                                mm.then_inc(s.back, 1)
                        if t == 4 and live(k - 1):
                            e.wait_ge(s.att, G(k) * 2)
                            for q in range(SB // 2):
                                mm = e.transpose(bank[4][:, q * S:(q + 1) * S],
                                                 att[:, 2 * q:2 * q + 2, :].rearrange("p b d -> p (b d)"), c.ident[:])
                            mm.then_inc(s.att_ps, 1)
                        if t == 5 and live(k - 1):
                            e.wait_ge(s.att_t, G(k))
                            for q in range(SB // 2):
                                mm = e.matmul(bank[5][:, q * P:(q + 1) * P], att_t[:, q * S:(q + 1) * S],
                                              wproj[:].rearrange("p a d -> p (a d)"), start=True, stop=True)
                            mm.then_inc(s.proj, 1)
                        if t == 6 and live(k + 1):
                            e.wait_ge(s.att_t, G(k) if live(k - 1) else G(0))
                            for q in range(SB // 2):
                                mm = e.matmul(bank[4][:, q * P:(q + 1) * P], zset[:, q * S:(q + 1) * S],
                                              wv[:].rearrange("p a d -> p (a d)"), start=True, stop=True)
                            mm.then_inc(s.val_ps, 1)
                        if live(k):
                            e.wait_ge(s.rows, G(k) * SLOTS + t + 1)
                            if t > 0:
                                e.wait_ge(s.factor, G(k) * (SLOTS - 1) + t)
                            else:
                                e.wait_ge(s.fin, G(k))
                            e.transpose(bank[7][:, 0:P], rows[:], c.ident[:]).then_inc(s.turned, 1)
                        score(k + 1, t - 1)

                over_rounds(e, step)


def route(nc, c):
    with ExitStack() as ctx:
        sb = lambda n, s, d=F32: ctx.enter_context(nc.sbuf_tensor("r_" + n, s, d))
        sem = lambda n: ctx.enter_context(nc.semaphore("r_" + n))
        wide = [P, B * EXPERTS]
        shifted, probs, rest, equal, picked, both = (sb(n, wide) for n in
                                                     ("shifted", "probs", "rest", "equal", "picked", "both"))
        peak, total, first, second, rank = (sb(n, [P, B]) for n in ("peak", "total", "first", "second", "rank"))
        s_step, s_exp = sem("step"), sem("exp")
        w3 = lambda t: t[:].rearrange("p (b e) -> p b e", e=EXPERTS)
        over = lambda t: bcast(t[:], EXPERTS)

        with nc.Block() as block:
            @block.scalar
            def _(e):
                e.wait_ge(s_step, 2)
                e.activation(shifted[:], shifted[:], ACT.Exp).then_inc(s_exp, 1)

            @block.vector
            def _(e):
                n = [0]

                def then(ins):
                    n[0] += 1
                    ins.then_inc(s_step, 1)
                    e.wait_ge(s_step, n[0])

                def pick(values, largest, out):
                    then(e.tensor_reduce(largest[:], w3(values), AX.X, ALU.max))
                    then(e.tensor_tensor(w3(equal), w3(values), over(largest), ALU.is_equal))
                    then(e.tensor_tensor(w3(equal), w3(equal), mid(c.priority[:], B), ALU.mult))
                    then(e.tensor_reduce(rank[:], w3(equal), AX.X, ALU.max))
                    then(e.tensor_tensor(w3(out), w3(equal), over(rank), ALU.is_equal))

                then(e.tensor_reduce(peak[:], w3(c.gates), AX.X, ALU.max))
                then(e.tensor_tensor(w3(shifted), w3(c.gates), over(peak), ALU.subtract))
                e.wait_ge(s_exp, 1)
                then(e.tensor_reduce(total[:], w3(shifted), AX.X, ALU.add))
                then(e.reciprocal(total[:], total[:]))
                then(e.tensor_tensor(w3(probs), w3(shifted), over(total), ALU.mult))
                pick(probs, first, picked)
                then(e.tensor_scalar(rest[:], picked[:], -2.0, None, ALU.mult))
                then(e.tensor_tensor(rest[:], rest[:], probs[:], ALU.add))
                pick(rest, second, both)
                then(e.tensor_tensor(both[:], both[:], picked[:], ALU.add))
                then(e.tensor_tensor(both[:], both[:], probs[:], ALU.mult))
                then(e.tensor_tensor(total[:], first[:], second[:], ALU.add))
                then(e.reciprocal(total[:], total[:]))
                then(e.tensor_tensor(w3(c.gates), w3(both), over(total), ALU.mult))


def experts(nc, c, a):
    with ExitStack() as ctx:
        sb = lambda n, s, d=F32: ctx.enter_context(nc.sbuf_tensor("m_" + n, s, d))
        ps = lambda n, s, d=F32: ctx.enter_context(nc.psum_tensor("m_" + n, s, d))
        sem = lambda n: ctx.enter_context(nc.semaphore("m_" + n))
        w1 = sb("w1", [P, EXPERTS, HID])
        w1_parts = sb("w1_parts", [P, EXPERTS, 2, HID], F16)
        w2 = sb("w2", [P, EXPERTS, HALVES, D])
        bias = sb("bias", [P, EXPERTS, HALVES + 3])
        b1 = sb("b1", [P, EXPERTS, HALVES])
        hid = sb("hid", [P, 2, HALVES, BANK])
        y_t = sb("y_t", [P, 2, NPAIR2 * S])
        gated = sb("gated", [P, 2, GC])
        bank = [ps(f"bank{i}", [P, BANK]) for i in range(8)]
        names = ("loaded", "offsets", "b1_ready", "w1_ready", "h_made", "gelued", "y_made", "y_copied", "y_back",
                 "gated", "summed")
        s = type("Sems", (), {n: sem("m_" + n) for n in names})

        def over_experts(e, step):
            def steps(g, first=False):
                for x in range(EXPERTS):
                    before = (g, x - 1) if x >= 1 else (None if first else (g - 1, EXPERTS - 1))
                    before2 = (g, x - 2) if x >= 2 else (None if first else (g - 1, EXPERTS + x - 2))
                    step((g, x), before, before2)
            steps(0, first=True)
            with e.Fori(1, NG) as g:
                steps(g)
            step(None, (NG - 1, EXPERTS - 1), (NG - 1, EXPERTS - 2))
            step(None, None, (NG - 1, EXPERTS - 1))

        at = lambda gx: gx[0] * EXPERTS + gx[1]

        with nc.Block() as block:
            @block.sync
            def _(e):
                e.dma_start(w1[:].rearrange("p x n -> p (x n)"), a["moe_w1"]).then_inc(s.loaded, 16)
                e.dma_start(w2[:].rearrange("p x a n -> p (x a n)"), a["moe_w2"]).then_inc(s.loaded, 16)
                e.dma_start(bias[:].rearrange("p x n -> p (x n)"), a["moe_bias"]).then_inc(s.loaded, 16)

            @block.tensor
            def _(e):
                e.wait_ge(s.loaded, 48)
                for x in range(EXPERTS):
                    for half in range(HALVES):
                        mm = e.matmul(bank[0][:, x * HALVES + half:x * HALVES + half + 1],
                                      w1[:, x, half * P:(half + 1) * P], bias[:, x, HALVES + 2:],
                                      start=True, stop=True)
                mm.then_inc(s.offsets, 1)
                e.wait_ge(s.w1_ready, 3 * EXPERTS)

                def step(now, before, before2):
                    if now:
                        g, x = now
                        n, par = at(now), x % 2
                        for half in range(HALVES):
                            if not isinstance(g, int) or x >= 2:
                                e.wait_ge(s.gelued, n * 2 - 3 + half)
                            for part in range(2):
                                mm = e.matmul(bank[2 * par + half][:], w1_parts[:, x, part, half * P:(half + 1) * P],
                                              c.zt_split[:, ds(g * (GB * S), GB * S)],
                                              start=part == 0, stop=part == 1)
                            mm.then_inc(s.h_made, 1)
                    if before:
                        n, x = at(before), before[1]
                        par = x % 2
                        e.wait_ge(s.gelued, n * 2 + 2)
                        if not isinstance(n, int) or n >= 2:
                            e.wait_ge(s.y_copied, n - 1)
                        for half in range(HALVES):
                            for q in range(2):
                                mm = e.matmul(
                                    bank[4 + par][q * D:(q + 1) * D, 0:NPAIR2 * S].rearrange("p (a t) -> p a t", t=S),
                                    w2[:, x, half, :], of_parity(hid[:, par, half, :], q),
                                              start=half == 0, stop=half == HALVES - 1)
                        mm.then_inc(s.y_made, 1)
                    if before2:
                        n, par = at(before2), before2[1] % 2
                        e.wait_ge(s.y_copied, n + 1)
                        if not isinstance(n, int) or n >= 2:
                            e.wait_ge(s.gated, n - 1)
                        for q in range(NPAIR2):
                            mm = e.transpose(bank[6 + par][:, q * S:(q + 1) * S], y_t[:, par, q * S:(q + 1) * S],
                                             c.ident[:])
                        mm.then_inc(s.y_back, 1)

                over_experts(e, step)

            @block.scalar
            def _(e):
                def step(now, before, before2):
                    if now:
                        n, x = at(now), now[1]
                        par = x % 2
                        for half in range(HALVES):
                            e.wait_ge(s.h_made, n * 2 + half + 1)
                            if not isinstance(n, int) or n >= 2:
                                e.wait_ge(s.y_made, n - 1)
                            e.activation(hid[:, par, half, :], bank[2 * par + half][:], ACT.Gelu,
                                         bias=b1[:, x, half:half + 1], scale=1.0 / W1_UP).then_inc(s.gelued, 1)
                    if before:
                        n, x = at(before), before[1]
                        par = x % 2
                        e.wait_ge(s.y_made, n + 1)
                        if not isinstance(n, int) or n >= 2:
                            e.wait_ge(s.y_back, n - 1)
                        e.activation(y_t[:, par, :], bank[4 + par][:, 0:NPAIR2 * S], ACT.Identity,
                                     bias=bias[:, x, HALVES:HALVES + 1]).then_inc(s.y_copied, 1)

                over_experts(e, step)

            @block.vector
            def _(e):
                e.wait_ge(s.offsets, 1)
                e.tensor_tensor(b1[:], bank[0][:, 0:EXPERTS * HALVES].rearrange("p (x n) -> p x n", n=HALVES),
                                bias[:, :, 0:HALVES], ALU.add).then_inc(s.b1_ready, 1)
                e.wait_ge(s.b1_ready, 1)
                for x in range(EXPERTS):
                    e.tensor_scalar(w1[:, x], w1[:, x], bias[:, x, HALVES + 1:HALVES + 2], W1_UP,
                                    ALU.mult, ALU.mult).then_inc(s.w1_ready, 1)
                for x in range(EXPERTS):
                    e.wait_ge(s.w1_ready, x + 1)
                    e.tensor_copy(w1_parts[:, x, 0], w1[:, x]).then_inc(s.w1_ready, 1)
                for x in range(EXPERTS):
                    e.wait_ge(s.w1_ready, EXPERTS + x + 1)
                    e.tensor_tensor(w1_parts[:, x, 1], w1[:, x], w1_parts[:, x, 0], ALU.subtract).then_inc(s.w1_ready, 1)

                def step(now, before, before2):
                    if before2:
                        g, x = before2
                        n, par = at(before2), x % 2
                        e.wait_ge(s.y_back, n + 1)
                        if not isinstance(n, int) or n >= 2:
                            e.wait_ge(s.summed, n - 1)
                        gate = c.gates[:, ds(g * GB * EXPERTS, GB * EXPERTS)].rearrange(
                            "p (b e) -> p b e", e=EXPERTS)[:, :, x]
                        e.tensor_tensor(gated[:, par, :].rearrange("p (b d) -> p b d", d=D),
                                        bank[6 + par][:, 0:GC].rearrange("p (b d) -> p b d", d=D),
                                        bcast(gate, D), ALU.mult).then_inc(s.gated, 1)

                over_experts(e, step)

            @block.gpsimd
            def _(e):
                def step(now, before, before2):
                    if before2:
                        g, x = before2
                        n, par = at(before2), x % 2
                        e.wait_ge(s.gated, n + 1)
                        if not isinstance(n, int) or n >= 1:
                            e.wait_ge(s.summed, n)
                        own_wait(e, c)
                        e.tensor_tensor(group(c.x, g), group(c.x, g),
                                        gated[:, par, :].rearrange("p (b d) -> p b d", d=D),
                                        ALU.add).then_inc(s.summed, 1)

                over_experts(e, step)


def store(nc, c, a):
    with ExitStack() as ctx:
        stored = ctx.enter_context(nc.semaphore("stored"))
        with nc.Block() as block:
            @block.sync
            def _(e):
                e.dma_start(a["out"].rearrange("b s d -> s b d"),
                            c.x[:].rearrange("p (b d) -> p b d", d=D)).then_inc(stored, 16)
                e.wait_ge(stored, 16)


class Chip:

    def __init__(self, nc, ctx):
        sb = lambda n, s, d=F32: ctx.enter_context(nc.sbuf_tensor(n, s, d))
        self.x = sb("x_sb", [P, B * D])
        self.ident = sb("ident", [P, P])
        self.ident16 = sb("ident16", [P, P], F16)
        self.neg_ident = sb("neg_ident", [P, P], BF16)
        self.sel_f = sb("sel_f", [P, 4, P])
        self.sel = sb("sel", [P, 4, P], F16)
        self.bias = sb("bias", [P, H // 2, S])
        self.bias16 = sb("bias16", [P, 2, H // 2, S], F16)
        self.ln1_w, self.ln1_b = sb("ln1_w", [P, LAYERS * D]), sb("ln1_b", [P, LAYERS * D])
        self.v = sb("v", [P, 2, PAIRS, QROWS])
        self.minus_half = sb("minus_half", [P, NB_CHUNK])
        self.zt = sb("zt", [P, NG * NPAIR2 * S])
        self.zt_split = self.zt[:].bitcast(F16)
        self.xt = sb("xt", [P, B * D])
        self.gates = sb("gates", [P, B * EXPERTS])
        self.priority = sb("priority", [P, EXPERTS])
        self.diag_ones = sb("diag_ones", [P, SB, QROWS])
        self.lnf_w, self.lnf_b = sb("lnf_w", [P, D]), sb("lnf_b", [P, D])
        self.wr, self.br = sb("wr_sb", [P, 2 * EXPERTS]), sb("br", [P, EXPERTS])
        self.waited = ctx.enter_context(nc.semaphore("waited"))
        self.x_ready = ctx.enter_context(nc.semaphore("x_ready"))


def build(nc, a):
    with ExitStack() as ctx:
        c = Chip(nc, ctx)
        embed(nc, c, a)
        tower(nc, c, a)
        normalise(nc, c, "nf_", c.x, affine=(c.lnf_w, c.lnf_b), dst=c.x)
        normalise(nc, c, "na_", c.x, turned=c.zt)
        sinkhorn(nc, c, a)
        normalise(nc, c, "nx_", c.x, dst=c.xt, logits=(c.wr, c.br, c.gates))
        normalise(nc, c, "ne_", c.xt, turned=c.zt_split, split_parts=True)
        route(nc, c)
        experts(nc, c, a)
        store(nc, c, a)


def constants():
    f = np.float32
    inv_freq = (1.0 / 10000.0 ** (np.arange(0, D, 2, dtype=f) / D)).astype(f)
    angle = (np.arange(POSITIONS, dtype=f)[:, None] * inv_freq[None]).astype(f)
    pos = np.concatenate([np.sin(angle), np.cos(angle)], axis=-1).astype(f)
    at = np.arange(S)
    dist = np.abs(at[:, None] // GRID_W - at[None] // GRID_W) + np.abs(at[:, None] % GRID_W - at[None] % GRID_W)
    bias = np.zeros((H, S, S))
    for h in range(H):
        bias[h] = (np.triu(-2.0 ** -(0.5 + h) * dist) + np.tril(-2.0 ** -(1.0 + h) * dist)) / SCALE
    bias = bias.transpose(2, 0, 1).astype(f)
    odd = bias[:, 1::2].astype(np.float16)
    odd_rest = (bias[:, 1::2] - odd).astype(np.float16)
    sel = np.zeros((P, 4, P), f)
    for side in range(2):
        for g in range(2):
            for j in range(4):
                for part in range(4):
                    which = part // 2 if side == 0 else part % 2
                    for d in range(HD):
                        sel[which * D + (4 * g + j) * HD + d, 2 * side + g, QROWS * j + HD * part + d] = 1
    return {
        "c_ident": np.eye(P, dtype=f), "c_sel": sel, "c_iota_v": np.tile(np.arange(VOCAB, dtype=f), (P, 1)),
        "c_iota_p": np.arange(P, dtype=f)[:, None],
        "c_pos": np.ascontiguousarray(pos.reshape(POS_CHUNKS, P, D).transpose(1, 0, 2)),
        "c_priority": np.tile(np.arange(EXPERTS, 0, -1, dtype=f), (P, 1)),
        "c_diag": np.tile(np.eye(SB, QROWS, dtype=f)[None], (P, 1, 1)),
        "c_bias": np.ascontiguousarray(bias[:, 0::2]), "c_bias16": np.stack([odd, odd_rest], 1),
    }


def laid_out(v):
    v = {k: np.asarray(x) for k, x in v.items()}
    w1, w2, b1, b2 = (v[f"L0_tok_{n}"] for n in ("w1", "w2", "b1", "b2"))
    ln2_w, ln2_b = v["L0_tok_ln2_w"], v["L0_tok_ln2_b"]
    arrays = {
        "mlp": np.concatenate([
            np.concatenate([w1, w1], 1),
            w2.reshape(LAYERS, HALVES, P, D).transpose(0, 2, 1, 3).reshape(LAYERS, P, HALVES * D),
            b1.reshape(LAYERS, HALVES, P).transpose(0, 2, 1),
            np.concatenate([b2, b2], 1)[:, :, None], np.concatenate([ln2_w, ln2_w], 1)[:, :, None],
            np.concatenate([ln2_b, np.zeros_like(ln2_b)], 1)[:, :, None]], 2),
    }
    w1, w2, b1, b2, g, b = (v[f"L0_ffn_{n}"] for n in ("W1", "W2", "b1", "b2", "ln_g", "ln_b"))
    arrays["moe_w1"] = np.concatenate([w1, w1], 1).transpose(1, 0, 2).reshape(P, EXPERTS * HID)
    arrays["moe_w2"] = w2.reshape(EXPERTS, HALVES, P, D).transpose(2, 0, 1, 3).reshape(P, EXPERTS * HALVES * D)
    twice = lambda t: np.concatenate([t.T, t.T], 0)[:, :, None]
    arrays["moe_bias"] = np.concatenate([b1.reshape(EXPERTS, HALVES, P).transpose(2, 0, 1), twice(b2), twice(g),
                                       np.concatenate([b.T, np.zeros_like(b.T)], 0)[:, :, None]], 2).reshape(P, EXPERTS * (HALVES + 3))
    wr = v["L0_ffn_Wr"]
    arrays["wr"] = np.concatenate([np.concatenate([wr, np.zeros_like(wr)], 1),
                                   np.concatenate([np.zeros_like(wr), wr], 1)], 0)
    for n in ("x", "pos_S", "L0_tok_lnf_w", "L0_tok_lnf_b", "L0_ffn_br", "L0_attn_W_qkv", "L0_attn_W_proj",
              "L0_attn_b_proj", "L0_attn_phase", "L0_attn_ent", "L0_attn_gate", "L0_attn_tau", "L0_tok_emb_table", "L0_tok_input_weight", "L0_tok_position_weight",
              "L0_tok_ln1_w", "L0_tok_ln1_b"):
        arrays[n] = v[n]
    arrays["L0_attn_tau"] = arrays["L0_attn_tau"].reshape(1)
    return {k: np.ascontiguousarray(x) for k, x in arrays.items()} | constants()


def kernel(**inputs):
    import concourse.bacc as bacc
    from concourse.bass_utils import run_bass_kernel_spmd

    nc = bacc.Bacc("TRN2", target_bir_lowering=False, num_devices=1)
    arrays = laid_out(inputs)
    aps = {n: nc.dram_tensor(n, v.shape, mybir.dt.from_np(v.dtype), kind="ExternalInput").ap()
           for n, v in arrays.items()}
    aps["out"] = nc.dram_tensor("out", (B, S, D), F32, kind="ExternalOutput").ap()
    build(nc, aps)
    return run_bass_kernel_spmd(nc, [arrays], core_ids=[0]).results[0]["out"]
```

```python
from contextlib import ExitStack

import numpy as np

import concourse.bass as bass
from concourse import mybir
from concourse.alu_op_type import AluOpType as ALU

ACT = mybir.ActivationFunctionType
AX = mybir.AxisListType
F32 = mybir.dt.float32
F16 = mybir.dt.float16
BF16 = mybir.dt.bfloat16
I32 = mybir.dt.int32
ds = bass.ds

P = 128
B, S, D = 128, 128, 64
LAYERS, H = 6, 8
HD = D // H
HID = 256
HALVES = HID // P
VOCAB = 16
POSITIONS = 1024
POS_CHUNKS = POSITIONS // P
GRID_W = 32
GB = 4
NG = B // GB
GC = GB * D
PAIRS = GB * H
NPAIR2 = GB // 2
EB = 8
AH, AHD = 4, 16
EXPERTS = 8
LATE_LOADS = 11 + AH
STORE = 16
BANK = 512
SBANKS = 4
QROWS = 32
AHEAD, BEHIND = 3, 3
ROUNDS = (NG - AHEAD - BEHIND) // 2
W1_UP = 64.0
LEAD = 4
EPS = 1e-5
SCALE = 1.0 / float(np.sqrt(HD))


def group(t, g):
    return t[:, ds(g * GC, GC)].rearrange("p (b d) -> p b d", d=D)


def bcast(t, n):
    return t.unsqueeze(2).broadcast_to([t.shape[0], t.shape[1], n])


def mid(t, n):
    return t.unsqueeze(1).broadcast_to([t.shape[0], n, t.shape[1]])


def of_parity(t, q):
    return t.rearrange("p (a q t) -> p a q t", q=2, t=S)[:, :, q, :]


def own_wait(e, c):
    e.sem_inc(c.waited, 1)


def embed(nc, c, a):
    with ExitStack() as ctx:
        sb = lambda n, s, d=F32: ctx.enter_context(nc.sbuf_tensor(n, s, d))
        ps = lambda n, s, d=F32: ctx.enter_context(nc.psum_tensor(n, s, d))
        sem = lambda n: ctx.enter_context(nc.semaphore(n))
        steps = B // EB
        tok_i, tok_f = sb("tok_i", [P, S], I32), sb("tok_f", [P, S])
        tok_t = sb("tok_t", [P, B])
        pos_i, pos_f = sb("pos_i", [P, S], I32), sb("pos_f", [P, S])
        iota_v = sb("iota_v", [P, VOCAB])
        iota_p = sb("iota_p", [P, 1])
        onehot = sb("onehot", [P, B * VOCAB])
        pos_hot = sb("pos_hot", [P, POS_CHUNKS, S])
        pos_tab = sb("pos_tab", [P, POS_CHUNKS, D])
        emb = sb("emb", [P, EB * D])
        weights = sb("weights", [P, 2])
        pos_emb = sb("pos_emb", [P, D])
        hot_t = sb("hot_t", [P, 2, S])
        tokt_ps, hot_ps = ps("tokt_ps", [P, B]), ps("hot_ps", [P, 2, BANK])
        pos_ps, x_ps = ps("pos_ps", [P, D]), ps("x_ps", [P, 2, BANK])
        loaded, emb_zero, emb_loaded = sem("e_loaded"), sem("e_emb_zero"), sem("e_emb_loaded")
        cast, tok_turned, tok_copied = sem("e_cast"), sem("e_tok_turned"), sem("e_tok_copied")
        hot, pos_made, pos_done, x_made = sem("e_hot"), sem("e_pos_made"), sem("e_pos_done"), sem("e_x_made")
        turned, copied = sem("e_turned"), sem("e_copied")

        with nc.Block() as block:
            @block.sync
            def _(e):
                for dst, src in (
                    (c.ident, a["c_ident"]), (c.sel_f, a["c_sel"]), (tok_i, a["x"]),
                    (iota_v, a["c_iota_v"]), (iota_p, a["c_iota_p"]), (pos_tab, a["c_pos"]),
                    (c.bias, a["c_bias"]), (c.bias16, a["c_bias16"]),
                    (pos_i, a["pos_S"].partition_broadcast(P)),
                    (weights[:, 0:1], a["L0_tok_input_weight"].partition_broadcast(P)),
                    (weights[:, 1:2], a["L0_tok_position_weight"].partition_broadcast(P)),
                    (c.ln1_w, a["L0_tok_ln1_w"].rearrange("l d -> (l d)").partition_broadcast(P)),
                    (c.ln1_b, a["L0_tok_ln1_b"].rearrange("l d -> (l d)").partition_broadcast(P)),
                    (c.priority, a["c_priority"]), (c.diag_ones, a["c_diag"]),
                    (c.wr, a["wr"]), (c.br, a["L0_ffn_br"].partition_broadcast(P)),
                    (c.lnf_w, a["L0_tok_lnf_w"].partition_broadcast(P)),
                    (c.lnf_b, a["L0_tok_lnf_b"].partition_broadcast(P)),
                ):
                    e.dma_start(dst[:] if not isinstance(dst, bass.AP) else dst, src).then_inc(loaded, 16)
                e.wait_ge(emb_zero, 1)
                for b in range(EB):
                    e.dma_start(emb[b * VOCAB:(b + 1) * VOCAB, b * D:(b + 1) * D],
                                a["L0_tok_emb_table"]).then_inc(emb_loaded, 16)

            @block.gpsimd
            def _(e):
                e.memset(emb[:], 0.0).then_inc(emb_zero, 1)
                e.memset(c.wproj[:], 0.0)
                e.memset(c.minus_half[:], -0.5)
                for par in range(2):
                    e.memset(c.v[:, par, :, HD:HD + 1], 1.0)
                    e.memset(c.v[:, par, :, HD + 1:QROWS], 0.0)

            @block.vector
            def _(e):
                e.wait_ge(loaded, 16 * 19)
                e.tensor_copy(tok_f[:], tok_i[:]).then_inc(cast, 1)
                e.tensor_copy(pos_f[:], pos_i[:]).then_inc(cast, 1)
                e.tensor_copy(c.ident16[:], c.ident[:])
                e.tensor_copy(c.sel[:], c.sel_f[:])
                e.tensor_scalar(c.neg_ident[:], c.ident[:], -1.0, None, ALU.mult)
                e.wait_ge(cast, 2)
                for k in range(POS_CHUNKS):
                    e.tensor_scalar(pos_hot[:, k, :], pos_f[:], float(-k * P), iota_p[:, 0:1],
                                    ALU.add, ALU.is_equal).then_inc(hot, 1)
                e.wait_ge(tok_turned, 1)
                e.tensor_copy(tok_t[:], tokt_ps[:]).then_inc(tok_copied, 1)
                e.wait_ge(tok_copied, 1)
                e.tensor_tensor(onehot[:].rearrange("p (b v) -> p b v", v=VOCAB), bcast(tok_t[:], VOCAB),
                                mid(iota_v[:], B), ALU.is_equal).then_inc(hot, 1)
                e.wait_ge(emb_loaded, 16 * EB)
                e.tensor_scalar(emb[:], emb[:], weights[:, 0:1], None, ALU.mult).then_inc(cast, 1)
                e.wait_ge(pos_made, 1)
                e.tensor_scalar(pos_emb[:], pos_ps[:], weights[:, 1:2], None, ALU.mult).then_inc(pos_done, 1)
                e.wait_ge(pos_done, 1)
                for i in range(steps):
                    e.wait_ge(x_made, i + 1)
                    for k in range(EB // GB):
                        e.tensor_tensor(group(c.x, i * EB // GB + k),
                                        x_ps[:, i % 2, k * GC:(k + 1) * GC].rearrange("p (b d) -> p b d", d=D),
                                        mid(pos_emb[:], GB), ALU.add).then_inc(c.x_ready, 1)

            @block.tensor
            def _(e):
                e.wait_ge(loaded, 16 * 19)
                e.wait_ge(cast, 1)
                e.transpose(tokt_ps[:], tok_f[:], c.ident[:]).then_inc(tok_turned, 1)
                e.wait_ge(hot, POS_CHUNKS)
                for k in range(POS_CHUNKS):
                    mm = e.matmul(pos_ps[:], pos_hot[:, k, :], pos_tab[:, k, :],
                                  start=k == 0, stop=k == POS_CHUNKS - 1)
                mm.then_inc(pos_made, 1)
                e.wait_ge(hot, POS_CHUNKS + 1)
                e.wait_ge(cast, 3)
                for i in range(steps + 1):
                    if i < steps:
                        if i >= 2:
                            e.wait_ge(copied, i - 1)
                        e.transpose(hot_ps[:, i % 2, 0:S], onehot[:, i * EB * VOCAB:(i + 1) * EB * VOCAB],
                                    c.ident[:]).then_inc(turned, 1)
                    if i >= 1:
                        e.wait_ge(copied, i)
                        if i >= 3:
                            e.wait_ge(c.x_ready, (i - 2) * EB // GB)
                        e.matmul(x_ps[:, (i - 1) % 2, :], hot_t[:, (i - 1) % 2, :], emb[:],
                                 start=True, stop=True).then_inc(x_made, 1)

            @block.scalar
            def _(e):
                for i in range(steps):
                    e.wait_ge(turned, i + 1)
                    if i >= 2:
                        e.wait_ge(x_made, i - 1)
                    e.activation(hot_t[:, i % 2, :], hot_ps[:, i % 2, 0:S], ACT.Copy).then_inc(copied, 1)


def load_late(e, c, a):
    late = [(c.w_qkv[0:D, :], a["L0_attn_W_qkv"]), (c.w_qkv[D:P, :], a["L0_attn_W_qkv"]),
            (c.wproj[0:D, 0, :], a["L0_attn_W_proj"]), (c.wproj[D:P, 1, :], a["L0_attn_W_proj"]),
            (c.bproj[:], a["L0_attn_b_proj"].partition_broadcast(P)),
            (c.moe_w1[:].rearrange("p x n -> p (x n)"), a["moe_w1"]),
            (c.moe_w2[:].rearrange("p x a n -> p (x a n)"), a["moe_w2"]),
            (c.moe_bias[:].rearrange("p x n -> p (x n)"), a["moe_bias"])]
    for n, name in enumerate(("phase", "ent", "gate")):
        late.append((c.head[:, n, :], a["L0_attn_" + name].partition_broadcast(P)))
    for h in range(AH):
        late.append((c.head[:, 3, h:h + 1], a["L0_attn_tau"].partition_broadcast(P)))
    for dst, src in late:
        e.dma_start(dst, src).then_inc(c.late_loaded, 16)


def tower(nc, c, a):
    with ExitStack() as ctx:
        sb = lambda n, s, d=F32: ctx.enter_context(nc.sbuf_tensor(n, s, d))
        ps = lambda n, s, d=F32: ctx.enter_context(nc.psum_tensor(n, s, d))
        sem = lambda n: ctx.enter_context(nc.semaphore(n))

        sum1, mean1, sqsum1, var1, rstd1 = (sb(n, [P, GB]) for n in ("sum1", "mean1", "sqsum1", "var1", "rstd1"))
        xc1, sq1, z1, zw1 = (sb(n, [P, GC]) for n in ("xc1", "sq1", "z1", "zw1"))
        qf = sb("qf", [P, 2, GC])
        q16 = sb("q16", [P, GB, 2, D], F16)
        qt16 = sb("qt16", [P, GB * S], F16)
        left = sb("left", [P, 2, 2, GB * S], F16)
        right = sb("right", [P, 2, 2, GB * S], F16)
        mx = sb("mx", [P, SBANKS, GB], BF16)
        biased = sb("biased", [P, 2, BANK])
        prob = sb("prob", [P, H, BANK])
        out_t = sb("out_t", [P, 2, BANK])
        rden = sb("rden", [P, 2, GB, 4])
        att = sb("att", [P, GC])
        sum2, mean2, sqsum2, var2, rstd2 = (sb(n, [P, GB]) for n in ("sum2", "mean2", "sqsum2", "var2", "rstd2"))
        xc2, sq2, z2 = (sb(n, [P, GC]) for n in ("xc2", "sq2", "z2"))
        z16 = sb("z16", [P, GB, 2, D], F16)
        zt = c.zt_split
        wcur = sb("wcur", [P, HID + HALVES * D + HALVES + 3])
        W1 = wcur[:, 0:HID]
        W2 = lambda half: wcur[:, HID + half * D:HID + (half + 1) * D]
        B1 = wcur[:, HID + HALVES * D:HID + HALVES * D + HALVES]
        B2, LN2_W, LN2_B = (wcur[:, n:n + 1] for n in range(HID + HALVES * D + HALVES, HID + HALVES * D + HALVES + 3))
        w1g = sb("w1g", [P, HID])
        w1_parts = sb("w1_parts", [P, 2, HID], F16)
        b1g = sb("b1g", [P, HALVES])
        hid = sb("hid", [P, 2, HALVES, BANK])
        y_t = sb("y_t", [P, 2, NPAIR2 * S])

        pool = [ps(f"bank{i}", [P, BANK]) for i in range(8)]
        score_ps = pool[0:SBANKS]
        turn_ps, stack_ps, out_ps, back_ps = pool[SBANKS:]
        q_turn_ps = turn_ps[:, 0:GB * S // 2].bitcast(F16)
        h_ps = lambda par, half: pool[2 * par + half]
        y_ps = lambda par: pool[4 + par]
        yb_ps = lambda par: pool[6 + par]

        names = ("sqsum1", "sqsum2", "v", "sum1", "mean1", "xc1", "sq1", "var1", "rstd1", "z1", "zw1", "q", "hi",
                 "lo", "q_turned",
                 "q_copied", "stacked", "stack_copied", "scored", "maxed", "shifted", "biased", "exped",
                 "weighed", "out_copied", "back", "recip", "divided", "x_att", "sum2", "mean2", "xc2", "sq2",
                 "var2", "rstd2", "z2", "z2_turned", "hi2", "lo2", "offset", "w_gained", "w_split", "zt_copied",
                 "w_loaded", "h_made", "gelued", "y_made",
                 "y_copied", "y_back")
        sems = {n: sem("t_" + n) for n in names}
        s = type("Sems", (), sems)

        def over_groups(e, step):
            for i in range(-AHEAD, BEHIND):
                step(i, i % 2)
            with e.Fori(0, ROUNDS) as j:
                step(j * 2 + BEHIND, BEHIND % 2)
                step(j * 2 + BEHIND + 1, (BEHIND + 1) % 2)
            for i in range(BEHIND + 2 * ROUNDS, NG + BEHIND):
                step(i, i % 2)

        def live(g):
            return not isinstance(g, int) or 0 <= g < NG

        def over_mlp_groups(e, step):
            step(0, 0, "a")
            step(1, 1, "ab")
            with e.Fori(0, (NG - 2) // 2) as j:
                step(j * 2 + 2, 0, "abc")
                step(j * 2 + 3, 1, "abc")
            step(NG, 0, "bc")
            step(NG + 1, 1, "c")

        per_group = {"scored": H, "maxed": H, "shifted": H, "biased": H // 2, "exped": H, "weighed": 4, "out_copied": 2,
                     "back": 2, "recip": 2, "divided": 2, "stacked": 4, "stack_copied": 4, "h_made": 2, "gelued": 2}
        with nc.Block() as block:
            @block.gpsimd
            def _(e):
                for n in names:
                    if n not in ("w_loaded", "offset", "w_gained", "w_split"):
                        e.sem_inc(sems[n], LEAD * per_group.get(n, 1))

        with nc.Block() as block:
            @block.sync
            def _(e):
                load_late(e, c, a)
                with e.Fori(0, LAYERS) as l:
                    e.wait_ge(s.y_copied, l * NG + LEAD)
                    e.dma_start(wcur[:], a["mlp"][ds(l, 1)].rearrange("l p n -> (l p) n")).then_inc(s.w_loaded, 16)

            @block.vector
            def _(e):
                with e.Fori(0, LAYERS) as l:
                    G = lambda g: l * NG + g + LEAD

                    def peak(g, h):
                        if live(g):
                            e.wait_ge(s.scored, G(g) * H + h + 1)
                            e.tensor_reduce(mx[:, h % SBANKS, :],
                                            score_ps[h % SBANKS][:].rearrange("p (b t) -> p b t", t=S),
                                            AX.X, ALU.max).then_inc(s.maxed, 1)

                    def add_bias(g, h):
                        if live(g) and h % 2 == 0:
                            e.wait_ge(s.shifted, G(g) * H + h + 1)
                            e.wait_ge(s.exped, G(g) * H + h - 3)
                            e.tensor_tensor(biased[:, h // 2 % 2, :].rearrange("p (b t) -> p b t", t=S),
                                            score_ps[h % SBANKS][:].rearrange("p (b t) -> p b t", t=S),
                                            mid(c.bias[:, h // 2, :], GB), ALU.add).then_inc(s.biased, 1)

                    def total_of(g, total, totalled):
                        if live(g):
                            e.tensor_reduce(total[:], group(c.x, g), AX.X, ALU.add).then_inc(totalled, 1)

                    def squares_of(g, squares, squared, total, totalled):
                        if live(g):
                            e.wait_ge(squared, G(g) + 1)
                            e.tensor_reduce(total[:], squares[:].rearrange("p (b d) -> p b d", d=D), AX.X,
                                            ALU.add).then_inc(totalled, 1)

                    def divide(g, half):
                        if live(g):
                            e.wait_ge(s.back, G(g) * 2 + half + 1)
                            back = back_ps[:].rearrange("p (b j r) -> p b j r", b=GB, j=4)
                            e.reciprocal(rden[:, half], back[:, :, :, HD]).then_inc(s.recip, 1)
                            e.wait_ge(s.recip, G(g) * 2 + half + 1)
                            if half == 0:
                                e.wait_ge(s.x_att, G(g))
                            e.tensor_tensor(
                                att[:].rearrange("p (b g j d) -> p b g j d", b=GB, g=2, j=4)[:, :, half],
                                back[:, :, :, 0:HD],
                                rden[:, half].unsqueeze(3).broadcast_to([P, GB, 4, HD]),
                                ALU.mult).then_inc(s.divided, 1)

                    def step(i, par):
                        for h in range(H):
                            peak(i + (h + 2) // H, (h + 2) % H)
                            add_bias(i, h)
                            if h == 0 and live(i - 2):
                                e.wait_ge(s.x_att, G(i - 1))
                                total_of(i - 2, sum2, s.sum2)
                            if h == 1:
                                divide(i - 1, 0)
                            if h == 2:
                                squares_of(i + 2, sq1, s.sq1, sqsum1, s.sqsum1)
                            if h == 2 and isinstance(i, int) and i == 0:
                                e.wait_ge(s.offset, l + 1)
                                e.tensor_tensor(b1g[:], back_ps[:, 0:HALVES], B1, ALU.add).then_inc(s.w_gained, 1)
                                e.tensor_scalar(w1g[:], W1, LN2_W, W1_UP, ALU.mult, ALU.mult).then_inc(s.w_gained, 1)
                                e.wait_ge(s.w_gained, l * 3 + 2)
                                e.tensor_copy(w1_parts[:, 0, :], w1g[:]).then_inc(s.w_gained, 1)
                                e.wait_ge(s.w_gained, l * 3 + 3)
                                e.tensor_tensor(w1_parts[:, 1, :], w1g[:], w1_parts[:, 0, :],
                                                ALU.subtract).then_inc(s.w_split, 1)
                            if h == 4:
                                squares_of(i - 2, sq2, s.sq2, sqsum2, s.sqsum2)
                            if h == 5:
                                divide(i - 1, 1)
                            if h == 6 and live(i + 3):
                                e.wait_ge(c.x_ready, l * NG + (i + 4))
                                total_of(i + 3, sum1, s.sum1)

                    over_groups(e, step)

                    def mlp(i, par, what):
                        if "c" in what:
                            e.wait_ge(s.y_back, G(i - 2) + 1)
                            e.tensor_tensor(group(c.x, i - 2), group(c.x, i - 2),
                                            yb_ps(par)[:, 0:GC].rearrange("p (b d) -> p b d", d=D),
                                            ALU.add).then_inc(c.x_ready, 1)

                    over_mlp_groups(e, mlp)

            @block.gpsimd
            def _(e):
                with e.Fori(0, LAYERS) as l:
                    G = lambda g: l * NG + g + LEAD
                    split = lambda t: t.rearrange("p (b d) -> p b d", d=D)

                    def centre(g, total, totalled, negated, ready, out, done):
                        if live(g):
                            e.wait_ge(totalled, G(g) + 1)
                            own_wait(e, c)
                            e.tensor_scalar(negated[:], total[:], -1.0 / D, None, ALU.mult).then_inc(ready, 1)
                            e.wait_ge(ready, G(g) + 1)
                            own_wait(e, c)
                            e.tensor_tensor(split(out[:]), group(c.x, g), bcast(negated[:], D), ALU.add).then_inc(done, 1)

                    def scaled(g, total, totalled, var, ready, rstd, rooted, xc, z, done):
                        if live(g):
                            e.wait_ge(totalled, G(g) + 1)
                            own_wait(e, c)
                            e.tensor_scalar(var[:], total[:], EPS, None, ALU.add).then_inc(ready, 1)
                            e.wait_ge(ready, G(g) + 1)
                            e.tensor_tensor(rstd[:], var[:], c.minus_half[:, 0:GB], ALU.pow).then_inc(rooted, 1)
                            e.wait_ge(rooted, G(g) + 1)
                            e.tensor_tensor(split(z[:]), split(xc[:]), bcast(rstd[:], D), ALU.mult).then_inc(done, 1)

                    def step(i, par):
                        for h in range(H):
                            if h == 0 and live(i - 3):
                                e.wait_ge(s.hi2, G(i - 2))
                                e.tensor_tensor(z16[:, :, 1, :], split(z2[:]), z16[:, :, 0, :],
                                                ALU.subtract).then_inc(s.lo2, 1)
                            if h == 1:
                                centre(i - 2, sum2, s.sum2, mean2, s.mean2, xc2, s.xc2)
                            if h == 3:
                                scaled(i + 2, sqsum1, s.sqsum1, var1, s.var1, rstd1, s.rstd1, xc1, z1, s.z1)
                            if h == 4 and live(i + 2):
                                e.wait_ge(s.z1, G(i + 3))
                                own_wait(e, c)
                                e.tensor_tensor(split(zw1[:]), split(z1[:]), mid(c.ln1_w[:, ds(l * D, D)], GB),
                                                ALU.mult).then_inc(s.zw1, 1)
                                e.wait_ge(s.zw1, G(i + 3))
                                e.wait_ge(s.v, G(i + 1))
                                own_wait(e, c)
                                e.tensor_tensor(split(qf[:, par, :]), split(zw1[:]), mid(c.ln1_b[:, ds(l * D, D)], GB),
                                                ALU.add).then_inc(s.q, 1)
                            if h == 5:
                                scaled(i - 2, sqsum2, s.sqsum2, var2, s.var2, rstd2, s.rstd2, xc2, z2, s.z2)
                            if h == 6 and live(i + 2):
                                e.wait_ge(s.hi, G(i + 3))
                                e.tensor_tensor(q16[:, :, 1, :], split(qf[:, par, :]), q16[:, :, 0, :],
                                                ALU.subtract).then_inc(s.lo, 1)
                            if h == 6 and live(i - 1):
                                e.wait_ge(s.divided, G(i) * 2)
                                own_wait(e, c)
                                e.tensor_tensor(group(c.x, i - 1), group(c.x, i - 1), split(att[:]),
                                                ALU.add).then_inc(s.x_att, 1)
                            if h == 6:
                                centre(i + 3, sum1, s.sum1, mean1, s.mean1, xc1, s.xc1)
                    over_groups(e, step)

            @block.scalar
            def _(e):
                with e.Fori(0, LAYERS) as l:
                    G = lambda g: l * NG + g + LEAD

                    def exp(g, h):
                        if live(g):
                            if h % 2 == 0:
                                e.wait_ge(s.biased, G(g) * (H // 2) + h // 2 + 1)
                            else:
                                e.wait_ge(s.shifted, G(g) * H + h + 1)
                            e.wait_ge(s.weighed, G(g) * 4 - 2 + 2 * (h // 4))
                            e.activation(prob[:, h, :], score_ps[h % SBANKS][:] if h % 2 else biased[:, h // 2 % 2, :],
                                         ACT.Exp, scale=SCALE).then_inc(s.exped, 1)

                    def square(g, xc, ready, sq, done):
                        if live(g):
                            e.wait_ge(ready, G(g) + 1)
                            e.activation(sq[:], xc[:], ACT.Square, scale=1.0 / np.sqrt(D)).then_inc(done, 1)

                    def copy_out(g, half):
                        if live(g):
                            e.wait_ge(s.weighed, G(g) * 4 + 2 * half + 2)
                            e.wait_ge(s.back, G(g) * 2 - 1 + half)
                            e.activation(out_t[:, half, :], out_ps[:], ACT.Copy).then_inc(s.out_copied, 1)

                    def copy_stack(g, parity, n):
                        if live(g):
                            e.wait_ge(s.stacked, G(g) * 4 + n + 1)
                            e.activation((left, right)[n % 2][:, parity, n // 2, :], stack_ps[:],
                                         ACT.Copy).then_inc(s.stack_copied, 1)

                    def step(i, par):
                        for h in range(H):
                            if h % 2:
                                exp(i, h - 1)
                                exp(i, h)
                            if h == 0:
                                copy_stack(i, par, 3)
                            if h == 0 and live(i + 1):
                                e.wait_ge(s.q_turned, G(i + 2))
                                e.activation(qt16[:], q_turn_ps, ACT.Copy).then_inc(s.q_copied, 1)
                            if h == 0:
                                square(i + 2, xc1, s.xc1, sq1, s.sq1)
                            if h in (2, 4, 6):
                                copy_stack(i + 1, 1 - par, h // 2 - 1)
                            if h == 2:
                                square(i - 2, xc2, s.xc2, sq2, s.sq2)
                            if h == 3:
                                copy_out(i - 1, 1)
                            if h == 4 and live(i - 3):
                                e.wait_ge(s.z2_turned, G(i - 2))
                                own_wait(e, c)
                                e.activation(zt[:, ds((i - 3) * (GB * S), GB * S)], q_turn_ps,
                                             ACT.Copy).then_inc(s.zt_copied, 1)
                            if h == 6 and live(i + 2):
                                e.wait_ge(s.q, G(i + 3))
                                e.wait_ge(s.q_turned, G(i + 2))
                                e.activation(q16[:, :, 0, :], qf[:, par, :].rearrange("p (b d) -> p b d", d=D),
                                             ACT.Copy).then_inc(s.hi, 1)
                            if h == 6 and live(i + 1):
                                e.wait_ge(s.weighed, G(i) * 4)
                                e.activation(c.v[:, 1 - par, :, 0:HD],
                                             qf[:, 1 - par, :].rearrange("p (n d) -> p n d", d=HD),
                                             ACT.Copy).then_inc(s.v, 1)
                            if h == 7:
                                copy_out(i, 0)
                            if h == 7 and live(i - 2):
                                e.wait_ge(s.z2, G(i - 1))
                                e.wait_ge(s.z2_turned, G(i - 2))
                                e.activation(z16[:, :, 0, :], z2[:].rearrange("p (b d) -> p b d", d=D),
                                             ACT.Copy).then_inc(s.hi2, 1)

                    over_groups(e, step)

                    def mlp(i, par, what):
                        if "a" in what:
                            for half in range(HALVES):
                                e.wait_ge(s.h_made, G(i) * 2 + half + 1)
                                e.wait_ge(s.y_made, G(i - 1))
                                e.activation(hid[:, par, half, :], h_ps(par, half)[:], ACT.Gelu,
                                             bias=b1g[:, half:half + 1], scale=1.0 / W1_UP).then_inc(s.gelued, 1)
                        if "b" in what:
                            e.wait_ge(s.y_made, G(i))
                            e.wait_ge(s.y_back, G(i - 2))
                            e.activation(y_t[:, 1 - par, :], y_ps(1 - par)[:, 0:NPAIR2 * S], ACT.Identity,
                                         bias=B2).then_inc(s.y_copied, 1)

                    over_mlp_groups(e, mlp)

            @block.tensor
            def _(e):
                with e.Fori(0, LAYERS) as l:
                    G = lambda g: l * NG + g + LEAD

                    def score(g, parity, h):
                        if not live(g):
                            return
                        if h % 4 == 0:
                            e.wait_ge(s.stack_copied, G(g) * 4 + 2 + h // 2)
                        if isinstance(g, int) and g == 0 and h == 0:
                            e.wait_ge(s.gelued, G(0) * 2)
                        if h % 2:
                            e.wait_ge(s.exped, G(g) * H + h - SBANKS + 1)
                        else:
                            e.wait_ge(s.biased, G(g) * (H // 2) + h // 2 - 1)
                        j = h % 4
                        for b in range(GB):
                            mm = e.matmul(score_ps[h % SBANKS][:, b * S:(b + 1) * S],
                                          left[QROWS * j:QROWS * (j + 1), parity, h // 4, b * S:(b + 1) * S],
                                          right[QROWS * j:QROWS * (j + 1), parity, h // 4, b * S:(b + 1) * S],
                                          start=b == 0, stop=False, skip_group_check=True)
                        mm.then_inc(s.scored, 1)

                    def shift(g, h):
                        if live(g):
                            e.wait_ge(s.maxed, G(g) * H + h + 1)
                            for b in range(GB):
                                mm = e.matmul(score_ps[h % SBANKS][:, b * S:(b + 1) * S],
                                              mx[:, h % SBANKS, b:b + 1].broadcast_to([P, S]), c.neg_ident[:],
                                              start=False, stop=h % 2 == 0, skip_group_check=True)
                            if h % 2:
                                for part in range(2):
                                    mm = e.matmul(score_ps[h % SBANKS][:].rearrange("p (b t) -> p b t", t=S),
                                                  c.ident16[:], mid(c.bias16[:, part, h // 2, :], GB),
                                                  start=False, stop=part == 1, skip_group_check=True)
                            mm.then_inc(s.shifted, 1)

                    def weigh(g, parity, half, batches):
                        if not live(g):
                            return
                        if batches[0] == 0:
                            e.wait_ge(s.exped, G(g) * H + 4 * half + 4)
                            e.wait_ge(s.out_copied, G(g) * 2 + half)
                            if half == 0:
                                e.wait_ge(s.v, G(g) + 1)
                            if isinstance(g, int) and g == 0 and half == 0:
                                e.wait_ge(c.x_ready, l * NG + NG)
                        for b in batches:
                            for j in range(4):
                                h = 4 * half + j
                                mm = e.matmul(out_ps[QROWS * j:QROWS * (j + 1), b * S:(b + 1) * S],
                                              c.v[:, parity, b * H + h, :], prob[:, h, b * S:(b + 1) * S],
                                              start=True, stop=True)
                        mm.then_inc(s.weighed, 1)

                    def back(g, half):
                        if live(g):
                            e.wait_ge(s.out_copied, G(g) * 2 + half + 1)
                            e.wait_ge(s.divided, G(g) * 2 + half)
                            if isinstance(g, int) and g == 0 and half == 0:
                                e.wait_ge(s.w_gained, l * 3 + 1)
                            for b in range(GB):
                                mm = e.transpose(back_ps[:, b * S:(b + 1) * S], out_t[:, half, b * S:(b + 1) * S],
                                                 c.ident[:])
                            mm.then_inc(s.back, 1)

                    def stack(g, n):
                        if live(g):
                            if n == 0:
                                e.wait_ge(s.q_copied, G(g) + 1)
                            e.wait_ge(s.stack_copied, G(g) * 4 + n)
                            e.matmul(stack_ps[:], c.sel[:, 2 * (n % 2) + n // 2, :], qt16[:],
                                     start=True, stop=True).then_inc(s.stacked, 1)

                    def step(i, par):
                        for h in range(H):
                            shift(i + (h + 1) // H, (h + 1) % H)
                            score(i + (h + 3) // H, par if h + 3 < H else 1 - par, (h + 3) % H)
                            if h == 0 and live(i + 1):
                                e.wait_ge(s.lo, G(i + 2))
                                e.wait_ge(s.q_copied, G(i + 1))
                                e.wait_ge(s.zt_copied, G(i - 3) if live(i - 4) else G(0))
                                if isinstance(i, int) and i == -1:
                                    e.wait_ge(s.y_copied, G(0))
                                for b in range(GB):
                                    mm = e.transpose(q_turn_ps[:, b * S:(b + 1) * S],
                                                     q16[:, b].rearrange("p a d -> p (a d)"), c.ident16[:])
                                mm.then_inc(s.q_turned, 1)
                            if h == 0:
                                back(i - 1, 0)
                            if h in (1, 2):
                                weigh(i - 1, 1 - par, 1, (0, 1) if h == 1 else (2, 3))
                            if h % 2:
                                stack(i + 1, h // 2)
                            if h == 3 and live(i - 3):
                                e.wait_ge(s.lo2, G(i - 2))
                                e.wait_ge(s.q_copied, G(i + 2) if live(i + 1) else G(NG))
                                for b in range(GB):
                                    mm = e.transpose(q_turn_ps[:, b * S:(b + 1) * S],
                                                     z16[:, b].rearrange("p a d -> p (a d)"), c.ident16[:])
                                mm.then_inc(s.z2_turned, 1)
                            if h == 4:
                                back(i - 1, 1)
                            if h == 0 and isinstance(i, int) and i == 0:
                                e.wait_ge(s.w_loaded, l * 16 + 16)
                                e.wait_ge(c.x_ready, l * NG + NG)
                                for half in range(HALVES):
                                    mm = e.matmul(back_ps[:, half:half + 1], W1[:, half * P:(half + 1) * P], LN2_B,
                                                  start=True, stop=True)
                                mm.then_inc(s.offset, 1)
                            if h in (5, 6):
                                weigh(i, par, 0, (0, 1) if h == 5 else (2, 3))
                    over_groups(e, step)

                    def mlp(i, par, what):
                        if "a" in what:
                            if isinstance(i, int) and i == 0:
                                e.wait_ge(s.w_split, l + 1)
                                e.wait_ge(s.zt_copied, G(NG))
                                e.wait_ge(s.exped, G(NG) * H)
                            for half in range(HALVES):
                                e.wait_ge(s.gelued, G(i) * 2 - 3 + half)
                                for part in range(2):
                                    mm = e.matmul(h_ps(par, half)[:], w1_parts[:, part, half * P:(half + 1) * P],
                                                  zt[:, ds(i * (GB * S), GB * S)], start=part == 0, stop=part == 1)
                                mm.then_inc(s.h_made, 1)
                        if "b" in what:
                            e.wait_ge(s.gelued, G(i) * 2)
                            e.wait_ge(s.y_copied, G(i - 2))
                            if isinstance(i, int) and i < 3:
                                e.wait_ge(s.out_copied, G(NG) * 2)
                            for half in range(HALVES):
                                for q in range(2):
                                    mm = e.matmul(
                                        y_ps(1 - par)[q * D:(q + 1) * D, 0:NPAIR2 * S].rearrange("p (a t) -> p a t", t=S),
                                        W2(half), of_parity(hid[:, 1 - par, half, :], q),
                                                  start=half == 0, stop=half == HALVES - 1)
                            mm.then_inc(s.y_made, 1)
                        if "c" in what:
                            e.wait_ge(s.y_copied, G(i - 1))
                            e.wait_ge(c.x_ready, l * NG + (i - 3 + NG))
                            if isinstance(i, int) and i < 4:
                                e.wait_ge(s.divided, G(NG) * 2)
                            for q in range(NPAIR2):
                                mm = e.transpose(yb_ps(par)[:, q * S:(q + 1) * S], y_t[:, par, q * S:(q + 1) * S],
                                                 c.ident[:])
                            mm.then_inc(s.y_back, 1)

                    over_mlp_groups(e, mlp)


SB = 8
SETS = B // SB
ROUTE_STEPS = 20
SC = SB * D
SPAIRS = SB * AH
ITERATIONS = 5
SLOTS = 2 * ITERATIONS + 1


def sinkhorn(nc, c, a):
    with ExitStack() as ctx:
        sb = lambda n, s, d=F32: ctx.enter_context(nc.sbuf_tensor("a_" + n, s, d))
        ps = lambda n, s, d=F32: ctx.enter_context(nc.psum_tensor("a_" + n, s, d))
        sem = lambda n: ctx.enter_context(nc.semaphore("a_" + n))
        w, head, wproj, bproj = c.w_qkv, c.head, c.wproj, c.bproj
        cosv, sinv, gate, t1, t2, t3 = (sb(n, [P, AH]) for n in ("cos", "sin", "gate", "t1", "t2", "t3"))
        a1, a2, a3 = (sb(n, [P, AH]) for n in ("a1", "a2", "a3"))
        mixk = sb("mixk", [P, D])
        mixq = sb("mixq", [P, D])
        wu, wm = (sb(n, [P, 2, P]) for n in ("wu", "wm"))
        wv = sb("wv", [P, 2, D])
        zset = sb("zset", [P, SB // 2 * S])
        xc, sq, z = ({where: sb(n + "_" + where, [P, SC]) for where in ("front", "back")} for n in ("xc", "sq", "z"))
        small = {t: {n: sb(n + "_" + t, [P, SB]) for n in ("total", "mean", "sqtotal", "var", "rstd")} for t in "faxe"}
        side = {"f": "front", "a": "front", "x": "back", "e": "back"}
        zw = sb("zw", [P, SC])
        z16 = sb("z16", [P, SB, 2, D], F16)
        ut, mt = (sb(n, [P, 2, SB // 2 * S]) for n in ("ut", "mt"))
        val = sb("val", [P, 2, SB, AH, AHD])
        valb = sb("valb", [P, SB, AH, QROWS])
        rmax, cmax = (sb(n, [P, 2, 4], BF16) for n in ("rmax", "cmax"))
        half_xt = lambda n: c.xt[:, n * (SPAIRS * S):(n + 1) * (SPAIRS * S)].rearrange(
            "p (h b t) -> p h b t", h=AH, b=SB)
        k_ij = (sb("k_ij", [P, AH, SB, S])[:], half_xt(0))
        k_ji = (sb("k_ji", [P, AH, SB, S])[:], half_xt(1))
        ub, vb = (sb(n, [P, AH, SB, QROWS]) for n in ("ub", "vb"))
        rows = sb("rows", [P, S])
        kv, ku, u, v, prod, inv, alpha, beta = (sb(n, [P, AH, SB]) for n in
                                                ("kv", "ku", "u", "v", "prod", "inv", "alpha", "beta"))
        minus_half = sb("mh", [P, AH, SB])
        out_t = sb("out_t", [P, SB * S])
        att = sb("att", [P, SB, D])
        att_t = sb("att_t", [P, SB // 2 * S])
        res = sb("res", [P, SB, D])
        logit, probs, rest, equal, picked, both = (sb(n, [P, SB, EXPERTS]) for n in
                                                   ("logit", "probs", "rest", "equal", "picked", "both"))
        peak, ptotal, first, second, rank = (sb(n, [P, SB]) for n in ("peak", "ptotal", "first", "second", "rank"))
        stage = att_t
        bank = [ps(f"bank{i}", [P, BANK]) for i in range(8)]
        names = ("const", "coef", "mixed", "trig", "sig", "wready", "zset", "ut_ps", "ut", "val_ps", "val",
                 "scored", "rmaxed", "rowed", "cmaxed", "coled", "exped", "summed", "rows", "turned", "factor",
                 "pool", "valb", "out_ps", "out_t", "back", "att", "att_ps", "att_t", "proj", "res", "x", "fin",
                 "routed", "peaked", "shifted", "p_exped", "affine_w", "prepared", "z_turned", "x_turned",
                 "staged", "logits", "added", "hi", "lo", "e_turned",
                 "e_copied")
        names += tuple(n + "_" + t for t in "faxe" for n in ("total", "mean", "xc", "sq", "sqtotal", "var", "rstd", "z"))
        sems = {n: sem("a_" + n) for n in names}
        s = type("Sems", (), sems)
        UNITS = 2 * AH
        per_set = {"zset": 1, "ut_ps": 4, "ut": 4, "val_ps": 1, "val": 1, "scored": UNITS, "rmaxed": UNITS,
                   "rowed": UNITS, "cmaxed": UNITS, "coled": UNITS, "exped": UNITS, "summed": SLOTS, "rows": SLOTS,
                   "turned": SLOTS, "factor": SLOTS - 1, "pool": 6, "valb": 1, "out_ps": 1, "out_t": 2, "back": 2,
                   "att": 2, "att_ps": 1, "att_t": 1, "proj": 1, "res": 1, "x": 1, "fin": 1}
        for n in names[names.index("peaked"):]:
            per_set[n] = 1
        per_set["routed"] = ROUTE_STEPS
        G = lambda k: k + LEAD
        live = lambda k: not isinstance(k, int) or 0 <= k < SETS

        def diag(t):
            return t[:].rearrange("p h b r -> p h (b r)")[:, :, 0:(SB - 1) * (QROWS + 1) + 1:QROWS + 1]
        heads3 = lambda t: t[:].rearrange("p (h d) -> p h d", d=AHD)

        def over_rounds(e, step):
            for k in range(-2, 3):
                step(k, k % 2)
            with e.Fori(0, (SETS - 6) // 2) as j:
                step(j * 2 + 3, 1)
                step(j * 2 + 4, 0)
            for k in range(SETS - 3, SETS + 4):
                step(k, k % 2)

        x_of = lambda k: c.x[:, ds(k * SC, SC)].rearrange("p (b d) -> p b d", d=D)
        split = lambda t: t[:].rearrange("p (b d) -> p b d", d=D)

        with nc.Block() as block:
            @block.gpsimd
            def _(e):
                e.memset(minus_half[:], -0.5)
                for t in (wu, wm, wv, valb, ub, vb):
                    ins = e.memset(t[:], 0.0)
                ins.then_inc(s.const, 1)
                for n, count in per_set.items():
                    e.sem_inc(sems[n], LEAD * count)

            @block.scalar
            def _(e):
                e.wait_ge(c.late_loaded, 16 * LATE_LOADS)
                e.wait_ge(s.coef, 1)
                e.activation(cosv[:], t2[:], ACT.Sin).then_inc(s.trig, 1)
                e.activation(sinv[:], t1[:], ACT.Sin).then_inc(s.trig, 1)
                e.activation(gate[:], head[:, 2, :], ACT.Sigmoid).then_inc(s.sig, 1)

            @block.vector
            def _(e):
                n = [0]

                def chain(ins):
                    n[0] += 1
                    ins.then_inc(s.mixed, 1)
                    e.wait_ge(s.mixed, n[0])

                e.wait_ge(c.late_loaded, 16 * LATE_LOADS)
                two_pi = float(2 * np.pi)
                chain(e.tensor_scalar(t3[:], head[:, 0, :], 1.0 / two_pi, 12582912.0, ALU.mult, ALU.add))
                chain(e.tensor_scalar(t3[:], t3[:], -12582912.0, None, ALU.add))
                chain(e.tensor_scalar(t1[:], t3[:], -6.28125, None, ALU.mult))
                chain(e.tensor_tensor(t1[:], t1[:], head[:, 0, :], ALU.add))
                chain(e.tensor_scalar(t3[:], t3[:], -(two_pi - 6.28125), None, ALU.mult))
                chain(e.tensor_tensor(t1[:], t1[:], t3[:], ALU.add))
                chain(e.tensor_scalar(t1[:], t1[:], float(np.float32(3.1415925)), float(-np.float32(3.1415925)),
                                      ALU.min, ALU.max))
                chain(e.tensor_scalar(t2[:], t1[:], -1.0, None, ALU.mult))
                chain(e.tensor_tensor(t2[:], t2[:], t1[:], ALU.max))
                e.tensor_scalar(t2[:], t2[:], -1.0, float(np.pi / 2), ALU.mult, ALU.add).then_inc(s.coef, 1)
                e.wait_ge(s.trig, 2)
                e.wait_ge(s.sig, 1)
                scale = float(AHD) ** -0.5
                chain(e.tensor_tensor(t1[:], cosv[:], sinv[:], ALU.add))
                chain(e.tensor_scalar(t1[:], t1[:], 0.5, None, ALU.mult))
                chain(e.tensor_tensor(t1[:], t1[:], gate[:], ALU.mult))
                chain(e.tensor_scalar(t2[:], gate[:], -1.0, 1.0, ALU.mult, ALU.add))
                chain(e.tensor_tensor(t1[:], t1[:], t2[:], ALU.add))
                chain(e.reciprocal(t3[:], head[:, 3, :]))
                chain(e.tensor_scalar(t1[:], t1[:], scale, None, ALU.mult))
                chain(e.tensor_tensor(a1[:], t1[:], t3[:], ALU.mult))
                chain(e.tensor_tensor(t1[:], cosv[:], sinv[:], ALU.subtract))
                chain(e.tensor_tensor(t1[:], t1[:], gate[:], ALU.mult))
                chain(e.tensor_scalar(t1[:], t1[:], 0.5 * scale, None, ALU.mult))
                chain(e.tensor_tensor(a2[:], t1[:], t3[:], ALU.mult))
                chain(e.tensor_tensor(t1[:], gate[:], head[:, 1, :], ALU.mult))
                chain(e.tensor_scalar(t1[:], t1[:], 0.1, None, ALU.mult))
                chain(e.tensor_tensor(a3[:], t1[:], t3[:], ALU.mult))
                wq, wk = w[:, 0:D].rearrange("p (h d) -> p h d", d=AHD), w[:, D:2 * D].rearrange("p (h d) -> p h d", d=AHD)
                chain(e.tensor_tensor(heads3(mixk), wk, bcast(a1[:], AHD), ALU.mult))
                chain(e.tensor_tensor(heads3(mixq), wq, bcast(a3[:], AHD), ALU.mult))
                chain(e.tensor_tensor(mixk[:], mixk[:], mixq[:], ALU.add))
                chain(e.tensor_tensor(heads3(mixq), wq, bcast(a2[:], AHD), ALU.mult))
                e.wait_ge(s.const, 1)
                for par in range(2):
                    rws = slice(par * D, (par + 1) * D)
                    for t, lo, hi in ((wu, wq[rws], wk[rws]), (wm, heads3(mixk)[rws], heads3(mixq)[rws])):
                        o = t[rws, par, :].rearrange("p (h two d) -> p h two d", two=2, d=AHD)
                        e.tensor_copy(o[:, :, 0, :], lo)
                        e.tensor_copy(o[:, :, 1, :], hi)
                    ins = e.tensor_copy(wv[rws, par, :], w[rws, 2 * D:3 * D])
                ins.then_inc(s.wready, 1)

        with nc.Block() as block:
            @block.gpsimd
            def _(e):
                def scaled(t, k):
                    if live(k):
                        m = small[t]
                        e.wait_ge(sems["var_" + t], G(k) + 1)
                        e.tensor_tensor(m["rstd"][:], m["var"][:], minus_half[:, 0], ALU.pow).then_inc(sems["rstd_" + t], 1)
                        e.wait_ge(sems["rstd_" + t], G(k) + 1)
                        if t == "f":
                            e.wait_ge(s.z_turned, G(k))
                        elif t == "a":
                            e.wait_ge(s.prepared, G(k) + 1)
                        elif t == "x":
                            e.wait_ge(s.lo, G(k))
                        else:
                            e.wait_ge(s.x_turned, G(k) + 1)
                        e.tensor_tensor(split(z[side[t]]), split(xc[side[t]]), bcast(m["rstd"][:], D),
                                        ALU.mult).then_inc(sems["z_" + t], 1)

                def step(k, par):
                    if live(k - 1):
                        e.wait_ge(s.fin, G(k))
                        for n, (f, other) in enumerate(((u, kv), (v, ku))):
                            e.tensor_tensor(prod[:], f[:], other[:], ALU.mult).then_inc(s.pool, 1)
                            e.wait_ge(s.pool, G(k - 1) * 6 + n * 3 + 1)
                            e.tensor_tensor(inv[:], prod[:], minus_half[:], ALU.pow).then_inc(s.pool, 1)
                            e.wait_ge(s.pool, G(k - 1) * 6 + n * 3 + 2)
                            e.tensor_tensor((alpha, beta)[n][:], f[:], inv[:], ALU.mult).then_inc(s.pool, 1)
                            e.wait_ge(s.pool, G(k - 1) * 6 + n * 3 + 3)
                        e.wait_ge(s.out_ps, G(k - 1))
                        e.wait_ge(s.val, G(k))
                        for h in range(AH):
                            ins = e.tensor_tensor(valb[:, :, h, 0:AHD], val[:, 1 - par, :, h, :],
                                                  bcast(beta[:, h, :], AHD), ALU.mult)
                        ins.then_inc(s.valb, 1)
                    scaled("f", k + 2)
                    if live(k - 1):
                        e.wait_ge(s.res, G(k))
                        own_wait(e, c)
                        xs = c.x[:, ds((k - 1) * (SB * D), SB * D)].rearrange("p (b d) -> p b d", d=D)
                        e.tensor_tensor(xs, xs, res[:], ALU.add).then_inc(s.x, 1)
                    scaled("x", k - 2)
                    scaled("a", k + 2)
                    scaled("e", k - 2)

                over_rounds(e, step)

            @block.scalar
            def _(e):
                def square(t, k):
                    if live(k):
                        e.wait_ge(sems["xc_" + t], G(k) + 1)
                        e.activation(sq[side[t]][:], xc[side[t]][:], ACT.Square,
                                     scale=1.0 / np.sqrt(D)).then_inc(sems["sq_" + t], 1)

                def exp(k, parity, n):
                    if live(k) and 0 <= n < UNITS:
                        h, half = n // 2, n % 2
                        e.wait_ge(s.coled, G(k) * UNITS + n + 1)
                        if n == 0:
                            e.wait_ge(s.out_ps, G(k - 1))
                        for m, t in enumerate((k_ij, k_ji)):
                            ins = e.activation(t[parity][:, h, 4 * half:4 * half + 4, :].rearrange("p b t -> p (b t)"),
                                               bank[2 * (n % 2) + m][:], ACT.Exp)
                        ins.then_inc(s.exped, 1)

                def step(k, par):
                    for t in range(SLOTS):
                        exp(k + 1, 1 - par, t - 3)
                        if live(k):
                            e.wait_ge(s.summed, G(k) * SLOTS + t + 1)
                            e.activation(rows[:], bank[6][:, 0:S], ACT.Copy).then_inc(s.rows, 1)
                        if t == 0 and live(k - 3):
                            e.wait_ge(s.shifted, G(k - 2))
                            e.wait_ge(s.routed, G(k - 3) * ROUTE_STEPS)
                            e.activation(probs[:], logit[:], ACT.Exp).then_inc(s.p_exped, 1)
                        if t == 0 and live(k + 1):
                            for n, (dst, m) in enumerate(((ut, 0), (ut, 1), (mt, 0), (mt, 1))):
                                e.wait_ge(s.ut_ps, G(k + 1) * 4 + n + 1)
                                e.activation(dst[:, m], bank[n][:], ACT.Copy).then_inc(s.ut, 1)
                        if t == 2 and live(k - 1):
                            e.wait_ge(s.out_ps, G(k))
                            for n in range(2):
                                e.activation(out_t[:, n * BANK:(n + 1) * BANK], bank[4 + n][:],
                                             ACT.Copy).then_inc(s.out_t, 1)
                        if t == 4 and live(k - 1):
                            e.wait_ge(s.att_ps, G(k))
                            e.wait_ge(s.logits, G(k - 2) if live(k - 3) else G(0))
                            e.activation(att_t[:], bank[4][:], ACT.Copy).then_inc(s.att_t, 1)
                        if t == 6 and live(k + 1):
                            e.wait_ge(s.val_ps, G(k + 2))
                            e.wait_ge(s.valb, G(k))
                            e.activation(val[:, 1 - par].rearrange("p b h d -> p (b h d)"), bank[4][:],
                                         ACT.Copy).then_inc(s.val, 1)
                        if t == 0 and live(k - 3):
                            e.wait_ge(s.e_turned, G(k - 2))
                            own_wait(e, c)
                            e.activation(c.zt_split[:, ds((k - 3) * (SB * S), SB * S)], bank[5][:].bitcast(F16),
                                         ACT.Copy).then_inc(s.e_copied, 1)
                        if t == 1:
                            square("f", k + 2)
                        if t == 4:
                            square("x", k - 2)
                        if t == 5:
                            square("a", k + 2)
                        if t == 7 and live(k - 2):
                            e.wait_ge(s.x_turned, G(k - 1))
                            e.wait_ge(s.proj, G(k) if live(k - 1) else G(SETS))
                            e.activation(stage[:], bank[5][:], ACT.Copy).then_inc(s.staged, 1)
                        if t == 8:
                            square("e", k - 2)
                        if t == 9 and live(k + 2):
                            e.wait_ge(s.z_turned, G(k + 3))
                            e.wait_ge(s.val_ps, G(k + 2))
                            e.activation(zset[:], bank[5][:], ACT.Copy).then_inc(s.zset, 1)
                        if t == 10 and live(k - 2):
                            e.wait_ge(s.z_e, G(k - 1))
                            e.wait_ge(s.e_turned, G(k - 2))
                            e.activation(z16[:, :, 0, :], split(z["back"]), ACT.Copy).then_inc(s.hi, 1)

                over_rounds(e, step)

            @block.vector
            def _(e):
                def largest(k, n, ready, b, out, done):
                    if live(k) and 0 <= n < UNITS:
                        e.wait_ge(ready, G(k) * UNITS + n + 1)
                        e.tensor_reduce(out[:, n % 2], bank[b + 2 * (n % 2)][:].rearrange("p (b t) -> p b t", t=S),
                                        AX.X, ALU.max).then_inc(done, 1)

                def average(t, k, source):
                    if live(k):
                        m = small[t]
                        e.tensor_reduce(m["total"][:], source, AX.X, ALU.add).then_inc(sems["total_" + t], 1)
                        e.wait_ge(sems["total_" + t], G(k) + 1)
                        e.tensor_scalar(m["mean"][:], m["total"][:], -1.0 / D, None, ALU.mult).then_inc(sems["mean_" + t], 1)
                        e.wait_ge(sems["mean_" + t], G(k) + 1)
                        e.wait_ge(sems["z_" + {"f": "a", "a": "f", "x": "e", "e": "x"}[t]], G(k) + (t in "ae"))
                        e.tensor_tensor(split(xc[side[t]]), source, bcast(m["mean"][:], D),
                                        ALU.add).then_inc(sems["xc_" + t], 1)

                def variance(t, k):
                    if live(k):
                        m = small[t]
                        e.wait_ge(sems["sq_" + t], G(k) + 1)
                        e.tensor_reduce(m["sqtotal"][:], split(sq[side[t]]), AX.X, ALU.add).then_inc(sems["sqtotal_" + t], 1)
                        e.wait_ge(sems["sqtotal_" + t], G(k) + 1)
                        e.tensor_scalar(m["var"][:], m["sqtotal"][:], EPS, None, ALU.add).then_inc(sems["var_" + t], 1)

                def route(k):
                    n = [0]

                    def then(ins):
                        n[0] += 1
                        ins.then_inc(s.routed, 1)
                        e.wait_ge(s.routed, G(k) * ROUTE_STEPS + n[0])

                    def pick(values, largest, out):
                        then(e.tensor_reduce(largest[:], values[:], AX.X, ALU.max))
                        then(e.tensor_tensor(equal[:], values[:], over(largest), ALU.is_equal))
                        then(e.tensor_tensor(equal[:], equal[:], mid(c.priority[:], SB), ALU.mult))
                        then(e.tensor_reduce(rank[:], equal[:], AX.X, ALU.max))
                        then(e.tensor_tensor(out[:], equal[:], over(rank), ALU.is_equal))

                    over = lambda t: bcast(t[:], EXPERTS)
                    e.wait_ge(s.p_exped, G(k) + 1)
                    then(e.tensor_reduce(ptotal[:], probs[:], AX.X, ALU.add))
                    then(e.reciprocal(ptotal[:], ptotal[:]))
                    then(e.tensor_tensor(probs[:], probs[:], over(ptotal), ALU.mult))
                    pick(probs, first, picked)
                    then(e.tensor_scalar(rest[:], picked[:], -2.0, None, ALU.mult))
                    then(e.tensor_tensor(rest[:], rest[:], probs[:], ALU.add))
                    pick(rest, second, both)
                    then(e.tensor_tensor(both[:], both[:], picked[:], ALU.add))
                    then(e.tensor_tensor(both[:], both[:], probs[:], ALU.mult))
                    then(e.tensor_tensor(ptotal[:], first[:], second[:], ALU.add))
                    then(e.reciprocal(ptotal[:], ptotal[:]))
                    e.tensor_tensor(c.gates[:, ds(k * (SB * EXPERTS), SB * EXPERTS)].rearrange(
                        "p (b e) -> p b e", e=EXPERTS), both[:], over(ptotal), ALU.mult).then_inc(s.routed, 1)
                    assert n[0] + 1 == ROUTE_STEPS

                def step(k, par):
                    sums = bank[7][:, 0:P].rearrange("p (h r) -> p h r", h=AH)[:, :, 0:SB]
                    for t in range(SLOTS):
                        largest(k + 1, t - 2, s.scored, 0, rmax, s.rmaxed)
                        if live(k):
                            e.wait_ge(s.turned, G(k) * SLOTS + t + 1)
                            if t == SLOTS - 3:
                                e.wait_ge(s.pool, G(k) * 6)
                            if t == SLOTS - 3:
                                e.reciprocal(u[:], sums)
                            elif t == SLOTS - 2:
                                e.reciprocal(v[:], sums)
                                e.tensor_copy(ku[:], sums)
                            elif t == SLOTS - 1:
                                e.tensor_copy(kv[:], sums).then_inc(s.fin, 1)
                            if t < SLOTS - 1:
                                e.reciprocal(diag((ub, vb)[t % 2]), sums).then_inc(s.factor, 1)
                        largest(k + 1, t - 2, s.rowed, 1, cmax, s.cmaxed)
                        if t == 1 and live(k + 2):
                            average("f", k + 2, x_of(k + 2))
                        if t == 2:
                            variance("f", k + 2)
                        if t == 4 and live(k + 2):
                            e.wait_ge(s.z_f, G(k + 3))
                            e.tensor_tensor(split(zw), split(z["front"]), mid(c.lnf_w[:], SB), ALU.mult).then_inc(s.affine_w, 1)
                            e.wait_ge(s.affine_w, G(k + 3))
                            e.tensor_tensor(x_of(k + 2), split(zw), mid(c.lnf_b[:], SB), ALU.add).then_inc(s.prepared, 1)
                        if t == 3 and live(k - 2):
                            e.wait_ge(s.x, G(k - 1))
                            average("x", k - 2, x_of(k - 2))
                        if t == 5 and live(k + 2):
                            e.wait_ge(s.prepared, G(k + 3))
                            own_wait(e, c)
                            average("a", k + 2, x_of(k + 2))
                        if t == 5:
                            variance("x", k - 2)
                        if t == 6:
                            variance("a", k + 2)
                        if t == 7 and live(k - 2):
                            e.wait_ge(s.z_x, G(k - 1))
                            average("e", k - 2, split(z["back"]))
                        if t == 8:
                            variance("e", k - 2)
                        if t == 9 and live(k - 2):
                            e.wait_ge(s.logits, G(k - 1))
                            e.tensor_tensor(logit[:], bank[4][:, 0:SB * EXPERTS].rearrange("p (b e) -> p b e", e=EXPERTS),
                                            mid(c.br[:], SB), ALU.add).then_inc(s.added, 1)
                            e.wait_ge(s.added, G(k - 1))
                            e.tensor_reduce(peak[:], logit[:], AX.X, ALU.max).then_inc(s.peaked, 1)
                            e.wait_ge(s.peaked, G(k - 1))
                            e.tensor_tensor(logit[:], logit[:], bcast(peak[:], EXPERTS),
                                            ALU.subtract).then_inc(s.shifted, 1)
                        if t == 0 and live(k - 3):
                            route(k - 3)
                        if t == 10 and live(k - 2):
                            e.wait_ge(s.hi, G(k - 1))
                            e.tensor_tensor(z16[:, :, 1, :], split(z["back"]), z16[:, :, 0, :],
                                            ALU.subtract).then_inc(s.lo, 1)
                        if t == 3 and live(k - 1):
                            for n in range(2):
                                e.wait_ge(s.back, G(k - 1) * 2 + n + 1)
                                e.tensor_tensor(
                                    att[:, 4 * n:4 * n + 4, :].rearrange("p b (h d) -> p b h d", d=AHD),
                                    bank[4 + n][:].rearrange("p (b h r) -> p b h r", h=AH, r=QROWS)[:, :, :, 0:AHD],
                                    alpha[:, :, 4 * n:4 * n + 4].rearrange("p h b -> p b h").unsqueeze(3)
                                    .broadcast_to([P, 4, AH, AHD]), ALU.mult).then_inc(s.att, 1)
                        if t == 5 and live(k - 1):
                            e.wait_ge(s.proj, G(k))
                            e.wait_ge(s.x, G(k - 1))
                            e.tensor_tensor(res[:], bank[5][:].rearrange("p (b d) -> p b d", d=D), mid(bproj[:], SB),
                                            ALU.add).then_inc(s.res, 1)

                over_rounds(e, step)

            @block.tensor
            def _(e):
                def score(k, n):
                    if live(k) and 0 <= n < UNITS:
                        if n == 0:
                            e.wait_ge(s.ut, G(k) * 4 + 4)
                        e.wait_ge(s.exped, G(k) * UNITS + n - 1)
                        rws = slice(QROWS * (n // 2), QROWS * (n // 2 + 1))
                        ij, ji = bank[2 * (n % 2)], bank[2 * (n % 2) + 1]
                        for i in range(4):
                            b = 4 * (n % 2) + i
                            at = slice((b // 2) * S, (b // 2 + 1) * S)
                            e.matmul(ij[:, i * S:(i + 1) * S], ut[rws, b % 2, at], mt[rws, b % 2, at],
                                     start=i == 0, stop=False, skip_group_check=True)
                            mm = e.matmul(ji[:, i * S:(i + 1) * S], mt[rws, b % 2, at], ut[rws, b % 2, at],
                                          start=i == 0, stop=False, skip_group_check=True)
                        mm.then_inc(s.scored, 1)

                def shift(k, n, m, ready, swap, done):
                    if live(k) and 0 <= n < UNITS:
                        e.wait_ge(ready, G(k) * UNITS + n + 1)
                        along, across = bank[2 * (n % 2) + swap], bank[2 * (n % 2) + 1 - swap]
                        e.matmul(along[:], c.neg_ident[:], bcast(m[:, n % 2], S), start=False, stop=False,
                                 skip_group_check=True)
                        for i in range(4):
                            mm = e.matmul(across[:, i * S:(i + 1) * S], m[:, n % 2, i:i + 1].broadcast_to([P, S]),
                                          c.neg_ident[:], start=False, stop=True, skip_group_check=True)
                        mm.then_inc(done, 1)

                def step(k, par):
                    for t in range(SLOTS):
                        shift(k + 1, t - 3, cmax, s.cmaxed, 1, s.coled)
                        if live(k):
                            if t > 0:
                                e.wait_ge(s.factor, G(k) * (SLOTS - 1) + t)
                            else:
                                e.wait_ge(s.exped, G(k + 1) * UNITS)
                            e.wait_ge(s.rows, G(k) * SLOTS + t)
                            kern = (k_ji, k_ij)[t % 2][par]
                            for b in range(SB):
                                for h in range(AH):
                                    lhs = c.diag_ones[:, b, :] if t == 0 else (vb, ub)[t % 2][:, h, b, :]
                                    mm = e.matmul(bank[6][QROWS * h:QROWS * (h + 1), 0:S], lhs, kern[:, h, b, :],
                                                  start=b == 0, stop=b == SB - 1, skip_group_check=True)
                            mm.then_inc(s.summed, 1)
                        shift(k + 1, t - 2, rmax, s.rmaxed, 0, s.rowed)
                        if t == 0 and live(k + 1):
                            e.wait_ge(s.zset, G(k + 2))
                            e.wait_ge(s.exped, G(k + 1) * UNITS)
                            for n, (wt, m) in enumerate(((wu, 0), (wu, 1), (wm, 0), (wm, 1))):
                                e.matmul(bank[n][:], wt[:, m, :], zset[:], start=True, stop=True).then_inc(s.ut_ps, 1)
                        if t == 0 and live(k - 3):
                            e.wait_ge(s.lo, G(k - 2))
                            e.wait_ge(s.zset, G(k + 2) if live(k + 1) else G(SETS))
                            for b in range(SB):
                                mm = e.transpose(bank[5][:, b * D:(b + 1) * D].bitcast(F16),
                                                 z16[:, b].rearrange("p a d -> p (a d)"), c.ident16[:])
                            mm.then_inc(s.e_turned, 1)
                        if t == 7 and live(k - 2):
                            e.wait_ge(s.z_x, G(k - 1))
                            e.wait_ge(s.res, G(k) if live(k - 1) else G(SETS))
                            for q in range(SB // 2):
                                mm = e.transpose(bank[5][:, q * P:(q + 1) * P], z["back"][:, q * P:(q + 1) * P], c.ident[:])
                            mm.then_inc(s.x_turned, 1)
                        if t == 8 and live(k - 2):
                            e.wait_ge(s.staged, G(k - 1))
                            e.wait_ge(s.val, G(k + 2) if live(k + 1) else G(SETS))
                            for q in range(SB // 2):
                                mm = e.matmul(bank[4][:, q * 2 * EXPERTS:(q + 1) * 2 * EXPERTS],
                                              stage[:, q * P:(q + 1) * P], c.wr[:], start=True, stop=True)
                            mm.then_inc(s.logits, 1)
                        if t == 9 and live(k + 2):
                            e.wait_ge(s.z_a, G(k + 3))
                            e.wait_ge(s.staged, G(k - 1) if live(k - 2) else G(0))
                            e.wait_ge(s.res, G(k) if live(k - 1) else G(0))
                            for q in range(SB // 2):
                                mm = e.transpose(bank[5][:, q * P:(q + 1) * P], z["front"][:, q * P:(q + 1) * P], c.ident[:])
                            mm.then_inc(s.z_turned, 1)
                        if t == 2 and live(k - 1):
                            e.wait_ge(s.valb, G(k))
                            e.wait_ge(s.e_copied, G(k - 2) if live(k - 3) else G(0))
                            e.wait_ge(s.added, G(k - 2) if live(k - 3) else G(0))
                            e.wait_ge(s.zset, G(k + 2) if live(k + 1) else G(SETS))
                            e.wait_ge(s.val, G(k + 1) if live(k + 1) or live(k) else G(k))
                            for b in range(SB):
                                for h in range(AH):
                                    mm = e.matmul(
                                        bank[4 + b // 4][QROWS * h:QROWS * (h + 1), (b % 4) * S:(b % 4 + 1) * S],
                                        valb[:, b, h, :], k_ji[1 - par][:, h, b, :], start=True, stop=True)
                            mm.then_inc(s.out_ps, 1)
                        if t == 3 and live(k - 1):
                            for n in range(2):
                                e.wait_ge(s.out_t, G(k - 1) * 2 + n + 1)
                                for b in range(4):
                                    mm = e.transpose(bank[4 + n][:, b * S:(b + 1) * S],
                                                     out_t[:, (4 * n + b) * S:(4 * n + b + 1) * S], c.ident[:])
                                mm.then_inc(s.back, 1)
                        if t == 4 and live(k - 1):
                            e.wait_ge(s.att, G(k) * 2)
                            for q in range(SB // 2):
                                mm = e.transpose(bank[4][:, q * S:(q + 1) * S],
                                                 att[:, 2 * q:2 * q + 2, :].rearrange("p b d -> p (b d)"), c.ident[:])
                            mm.then_inc(s.att_ps, 1)
                        if t == 5 and live(k - 1):
                            e.wait_ge(s.att_t, G(k))
                            for q in range(SB // 2):
                                mm = e.matmul(bank[5][:, q * P:(q + 1) * P], att_t[:, q * S:(q + 1) * S],
                                              wproj[:].rearrange("p a d -> p (a d)"), start=True, stop=True)
                            mm.then_inc(s.proj, 1)
                        if t == 6 and live(k + 1):
                            e.wait_ge(s.att_t, G(k) if live(k - 1) else G(0))
                            for q in range(SB // 2):
                                mm = e.matmul(bank[4][:, q * P:(q + 1) * P], zset[:, q * S:(q + 1) * S],
                                              wv[:].rearrange("p a d -> p (a d)"), start=True, stop=True)
                            mm.then_inc(s.val_ps, 1)
                        if live(k):
                            e.wait_ge(s.rows, G(k) * SLOTS + t + 1)
                            if t > 0:
                                e.wait_ge(s.factor, G(k) * (SLOTS - 1) + t)
                            else:
                                e.wait_ge(s.fin, G(k))
                            e.transpose(bank[7][:, 0:P], rows[:], c.ident[:]).then_inc(s.turned, 1)
                        score(k + 1, t - 1)

                over_rounds(e, step)


def experts(nc, c, a):
    with ExitStack() as ctx:
        sb = lambda n, s, d=F32: ctx.enter_context(nc.sbuf_tensor("m_" + n, s, d))
        ps = lambda n, s, d=F32: ctx.enter_context(nc.psum_tensor("m_" + n, s, d))
        sem = lambda n: ctx.enter_context(nc.semaphore("m_" + n))
        w1, w2, bias = c.moe_w1, c.moe_w2, c.moe_bias
        w1_parts = sb("w1_parts", [P, EXPERTS, 2, HID], F16)
        b1 = sb("b1", [P, EXPERTS, HALVES])
        hid = sb("hid", [P, 2, HALVES, BANK])
        y_t = sb("y_t", [P, 2, NPAIR2 * S])
        gated = sb("gated", [P, 2, GC])
        bank = [ps(f"bank{i}", [P, BANK]) for i in range(8)]
        names = ("stored", "offsets", "b1_ready", "w1_ready", "h_made", "gelued", "y_made", "y_copied", "y_back",
                 "gated", "summed")
        s = type("Sems", (), {n: sem("m_" + n) for n in names})

        def over_experts(e, step):
            def steps(g, first=False):
                for x in range(EXPERTS):
                    before = (g, x - 1) if x >= 1 else (None if first else (g - 1, EXPERTS - 1))
                    before2 = (g, x - 2) if x >= 2 else (None if first else (g - 1, EXPERTS + x - 2))
                    step((g, x), before, before2)
            steps(0, first=True)
            with e.Fori(1, NG) as g:
                steps(g)
            step(None, (NG - 1, EXPERTS - 1), (NG - 1, EXPERTS - 2))
            step(None, None, (NG - 1, EXPERTS - 1))

        at = lambda gx: gx[0] * EXPERTS + gx[1]

        with nc.Block() as block:
            @block.sync
            def _(e):
                with e.Fori(0, B // STORE) as j:
                    e.wait_ge(s.summed, j * (STORE // GB * EXPERTS) + STORE // GB * EXPERTS)
                    e.dma_start(a["out"][ds(j * STORE, STORE)].rearrange("b s d -> s b d"),
                                c.x[:, ds(j * (STORE * D), STORE * D)].rearrange("p (b d) -> p b d", d=D)
                                ).then_inc(s.stored, 16)
                e.wait_ge(s.stored, 16 * (B // STORE))

            @block.tensor
            def _(e):
                e.wait_ge(c.late_loaded, 16 * LATE_LOADS)
                for x in range(EXPERTS):
                    for half in range(HALVES):
                        mm = e.matmul(bank[0][:, x * HALVES + half:x * HALVES + half + 1],
                                      w1[:, x, half * P:(half + 1) * P], bias[:, x, HALVES + 2:],
                                      start=True, stop=True)
                mm.then_inc(s.offsets, 1)
                e.wait_ge(s.w1_ready, 3 * EXPERTS)

                def step(now, before, before2):
                    if now:
                        g, x = now
                        n, par = at(now), x % 2
                        for half in range(HALVES):
                            if not isinstance(g, int) or x >= 2:
                                e.wait_ge(s.gelued, n * 2 - 3 + half)
                            for part in range(2):
                                mm = e.matmul(bank[2 * par + half][:], w1_parts[:, x, part, half * P:(half + 1) * P],
                                              c.zt_split[:, ds(g * (GB * S), GB * S)],
                                              start=part == 0, stop=part == 1)
                            mm.then_inc(s.h_made, 1)
                    if before:
                        n, x = at(before), before[1]
                        par = x % 2
                        e.wait_ge(s.gelued, n * 2 + 2)
                        if not isinstance(n, int) or n >= 2:
                            e.wait_ge(s.y_copied, n - 1)
                        for half in range(HALVES):
                            for q in range(2):
                                mm = e.matmul(
                                    bank[4 + par][q * D:(q + 1) * D, 0:NPAIR2 * S].rearrange("p (a t) -> p a t", t=S),
                                    w2[:, x, half, :], of_parity(hid[:, par, half, :], q),
                                              start=half == 0, stop=half == HALVES - 1)
                        mm.then_inc(s.y_made, 1)
                    if before2:
                        n, par = at(before2), before2[1] % 2
                        e.wait_ge(s.y_copied, n + 1)
                        if not isinstance(n, int) or n >= 2:
                            e.wait_ge(s.gated, n - 1)
                        for q in range(NPAIR2):
                            mm = e.transpose(bank[6 + par][:, q * S:(q + 1) * S], y_t[:, par, q * S:(q + 1) * S],
                                             c.ident[:])
                        mm.then_inc(s.y_back, 1)

                over_experts(e, step)

            @block.scalar
            def _(e):
                def step(now, before, before2):
                    if now:
                        n, x = at(now), now[1]
                        par = x % 2
                        for half in range(HALVES):
                            e.wait_ge(s.h_made, n * 2 + half + 1)
                            if not isinstance(n, int) or n >= 2:
                                e.wait_ge(s.y_made, n - 1)
                            e.activation(hid[:, par, half, :], bank[2 * par + half][:], ACT.Gelu,
                                         bias=b1[:, x, half:half + 1], scale=1.0 / W1_UP).then_inc(s.gelued, 1)
                    if before:
                        n, x = at(before), before[1]
                        par = x % 2
                        e.wait_ge(s.y_made, n + 1)
                        if not isinstance(n, int) or n >= 2:
                            e.wait_ge(s.y_back, n - 1)
                        e.activation(y_t[:, par, :], bank[4 + par][:, 0:NPAIR2 * S], ACT.Identity,
                                     bias=bias[:, x, HALVES:HALVES + 1]).then_inc(s.y_copied, 1)

                over_experts(e, step)

            @block.vector
            def _(e):
                e.wait_ge(s.offsets, 1)
                e.tensor_tensor(b1[:], bank[0][:, 0:EXPERTS * HALVES].rearrange("p (x n) -> p x n", n=HALVES),
                                bias[:, :, 0:HALVES], ALU.add).then_inc(s.b1_ready, 1)
                e.wait_ge(s.b1_ready, 1)
                for x in range(EXPERTS):
                    e.tensor_scalar(w1[:, x], w1[:, x], bias[:, x, HALVES + 1:HALVES + 2], W1_UP,
                                    ALU.mult, ALU.mult).then_inc(s.w1_ready, 1)
                for x in range(EXPERTS):
                    e.wait_ge(s.w1_ready, x + 1)
                    e.tensor_copy(w1_parts[:, x, 0], w1[:, x]).then_inc(s.w1_ready, 1)
                for x in range(EXPERTS):
                    e.wait_ge(s.w1_ready, EXPERTS + x + 1)
                    e.tensor_tensor(w1_parts[:, x, 1], w1[:, x], w1_parts[:, x, 0], ALU.subtract).then_inc(s.w1_ready, 1)

                def step(now, before, before2):
                    if before2:
                        g, x = before2
                        n, par = at(before2), x % 2
                        e.wait_ge(s.y_back, n + 1)
                        if not isinstance(n, int) or n >= 2:
                            e.wait_ge(s.summed, n - 1)
                        gate = c.gates[:, ds(g * GB * EXPERTS, GB * EXPERTS)].rearrange(
                            "p (b e) -> p b e", e=EXPERTS)[:, :, x]
                        e.tensor_tensor(gated[:, par, :].rearrange("p (b d) -> p b d", d=D),
                                        bank[6 + par][:, 0:GC].rearrange("p (b d) -> p b d", d=D),
                                        bcast(gate, D), ALU.mult).then_inc(s.gated, 1)

                over_experts(e, step)

            @block.gpsimd
            def _(e):
                def step(now, before, before2):
                    if before2:
                        g, x = before2
                        n, par = at(before2), x % 2
                        e.wait_ge(s.gated, n + 1)
                        if not isinstance(n, int) or n >= 1:
                            e.wait_ge(s.summed, n)
                        own_wait(e, c)
                        e.tensor_tensor(group(c.x, g), group(c.x, g),
                                        gated[:, par, :].rearrange("p (b d) -> p b d", d=D),
                                        ALU.add).then_inc(s.summed, 1)

                over_experts(e, step)


class Chip:

    def __init__(self, nc, ctx, tower_ctx):
        sb = lambda n, s, d=F32: ctx.enter_context(nc.sbuf_tensor(n, s, d))
        self.x = sb("x_sb", [P, B * D])
        self.ident = sb("ident", [P, P])
        self.ident16 = sb("ident16", [P, P], F16)
        self.neg_ident = sb("neg_ident", [P, P], BF16)
        self.minus_half = sb("minus_half", [P, GB])
        self.zt_split = sb("zt_split", [P, B * S], F16)
        self.xt = sb("xt", [P, B * D])
        self.gates = sb("gates", [P, B * EXPERTS])
        self.priority = sb("priority", [P, EXPERTS])
        self.diag_ones = sb("diag_ones", [P, SB, QROWS])
        self.lnf_w, self.lnf_b = sb("lnf_w", [P, D]), sb("lnf_b", [P, D])
        self.wr, self.br = sb("wr_sb", [P, 2 * EXPERTS]), sb("br", [P, EXPERTS])
        self.w_qkv, self.head = sb("w_qkv", [P, 3 * D]), sb("head", [P, 4, AH])
        self.wproj, self.bproj = sb("wproj", [P, 2, D]), sb("bproj", [P, D])
        self.moe_w1, self.moe_w2 = sb("moe_w1_sb", [P, EXPERTS, HID]), sb("moe_w2_sb", [P, EXPERTS, HALVES, D])
        self.moe_bias = sb("moe_bias_sb", [P, EXPERTS, HALVES + 3])
        self.late_loaded = ctx.enter_context(nc.semaphore("late_loaded"))
        self.waited = ctx.enter_context(nc.semaphore("waited"))
        self.x_ready = ctx.enter_context(nc.semaphore("x_ready"))
        sb = lambda n, s, d=F32: tower_ctx.enter_context(nc.sbuf_tensor(n, s, d))
        self.sel_f = sb("sel_f", [P, 4, P])
        self.sel = sb("sel", [P, 4, P], F16)
        self.bias = sb("bias", [P, H // 2, S])
        self.bias16 = sb("bias16", [P, 2, H // 2, S], F16)
        self.ln1_w, self.ln1_b = sb("ln1_w", [P, LAYERS * D]), sb("ln1_b", [P, LAYERS * D])
        self.v = sb("v", [P, 2, PAIRS, QROWS])


def build(nc, a):
    with ExitStack() as ctx:
        with ExitStack() as tower_ctx:
            c = Chip(nc, ctx, tower_ctx)
            embed(nc, c, a)
            tower(nc, c, a)
        sinkhorn(nc, c, a)
        experts(nc, c, a)


def constants():
    f = np.float32
    inv_freq = (1.0 / 10000.0 ** (np.arange(0, D, 2, dtype=f) / D)).astype(f)
    angle = (np.arange(POSITIONS, dtype=f)[:, None] * inv_freq[None]).astype(f)
    pos = np.concatenate([np.sin(angle), np.cos(angle)], axis=-1).astype(f)
    at = np.arange(S)
    dist = np.abs(at[:, None] // GRID_W - at[None] // GRID_W) + np.abs(at[:, None] % GRID_W - at[None] % GRID_W)
    bias = np.zeros((H, S, S))
    for h in range(H):
        bias[h] = (np.triu(-2.0 ** -(0.5 + h) * dist) + np.tril(-2.0 ** -(1.0 + h) * dist)) / SCALE
    bias = bias.transpose(2, 0, 1).astype(f)
    odd = bias[:, 1::2].astype(np.float16)
    odd_rest = (bias[:, 1::2] - odd).astype(np.float16)
    sel = np.zeros((P, 4, P), f)
    for side in range(2):
        for g in range(2):
            for j in range(4):
                for part in range(4):
                    which = part // 2 if side == 0 else part % 2
                    for d in range(HD):
                        sel[which * D + (4 * g + j) * HD + d, 2 * side + g, QROWS * j + HD * part + d] = 1
    return {
        "c_ident": np.eye(P, dtype=f), "c_sel": sel, "c_iota_v": np.tile(np.arange(VOCAB, dtype=f), (P, 1)),
        "c_iota_p": np.arange(P, dtype=f)[:, None],
        "c_pos": np.ascontiguousarray(pos.reshape(POS_CHUNKS, P, D).transpose(1, 0, 2)),
        "c_priority": np.tile(np.arange(EXPERTS, 0, -1, dtype=f), (P, 1)),
        "c_diag": np.tile(np.eye(SB, QROWS, dtype=f)[None], (P, 1, 1)),
        "c_bias": np.ascontiguousarray(bias[:, 0::2]), "c_bias16": np.stack([odd, odd_rest], 1),
    }


def laid_out(v):
    v = {k: np.asarray(x) for k, x in v.items()}
    w1, w2, b1, b2 = (v[f"L0_tok_{n}"] for n in ("w1", "w2", "b1", "b2"))
    ln2_w, ln2_b = v["L0_tok_ln2_w"], v["L0_tok_ln2_b"]
    arrays = {
        "mlp": np.concatenate([
            np.concatenate([w1, w1], 1),
            w2.reshape(LAYERS, HALVES, P, D).transpose(0, 2, 1, 3).reshape(LAYERS, P, HALVES * D),
            b1.reshape(LAYERS, HALVES, P).transpose(0, 2, 1),
            np.concatenate([b2, b2], 1)[:, :, None], np.concatenate([ln2_w, ln2_w], 1)[:, :, None],
            np.concatenate([ln2_b, np.zeros_like(ln2_b)], 1)[:, :, None]], 2),
    }
    w1, w2, b1, b2, g, b = (v[f"L0_ffn_{n}"] for n in ("W1", "W2", "b1", "b2", "ln_g", "ln_b"))
    arrays["moe_w1"] = np.concatenate([w1, w1], 1).transpose(1, 0, 2).reshape(P, EXPERTS * HID)
    arrays["moe_w2"] = w2.reshape(EXPERTS, HALVES, P, D).transpose(2, 0, 1, 3).reshape(P, EXPERTS * HALVES * D)
    twice = lambda t: np.concatenate([t.T, t.T], 0)[:, :, None]
    arrays["moe_bias"] = np.concatenate([b1.reshape(EXPERTS, HALVES, P).transpose(2, 0, 1), twice(b2), twice(g),
                                       np.concatenate([b.T, np.zeros_like(b.T)], 0)[:, :, None]],
                                      2).reshape(P, EXPERTS * (HALVES + 3))
    wr = v["L0_ffn_Wr"]
    arrays["wr"] = np.concatenate([np.concatenate([wr, np.zeros_like(wr)], 1),
                                   np.concatenate([np.zeros_like(wr), wr], 1)], 0)
    for n in ("x", "pos_S", "L0_tok_lnf_w", "L0_tok_lnf_b", "L0_ffn_br", "L0_attn_W_qkv", "L0_attn_W_proj",
              "L0_attn_b_proj", "L0_attn_phase", "L0_attn_ent", "L0_attn_gate", "L0_attn_tau", "L0_tok_emb_table",
              "L0_tok_input_weight", "L0_tok_position_weight",
              "L0_tok_ln1_w", "L0_tok_ln1_b"):
        arrays[n] = v[n]
    arrays["L0_attn_tau"] = arrays["L0_attn_tau"].reshape(1)
    return {k: np.ascontiguousarray(x) for k, x in arrays.items()} | constants()


def kernel(**inputs):
    import concourse.bacc as bacc
    from concourse.bass_utils import run_bass_kernel_spmd

    nc = bacc.Bacc("TRN2", target_bir_lowering=False, num_devices=1)
    arrays = laid_out(inputs)
    aps = {n: nc.dram_tensor(n, v.shape, mybir.dt.from_np(v.dtype), kind="ExternalInput").ap()
           for n, v in arrays.items()}
    aps["out"] = nc.dram_tensor("out", (B, S, D), F32, kind="ExternalOutput").ap()
    build(nc, aps)
    return run_bass_kernel_spmd(nc, [arrays], core_ids=[0]).results[0]["out"]
```
